# Optimizing a Trainium2 kernel written in Bass

```python
import numpy as np
import jax
import jax.numpy as jnp

def _softmax(x, axis=-1):
    return jax.nn.softmax(x, axis=axis)

def _gelu(x):
    return jax.nn.gelu(x, approximate=True)

def _silu(x):
    return jax.nn.silu(x)

def _sigmoid(x):
    return jax.nn.sigmoid(x)

def _layernorm(x, axis=-1, eps=1e-05):
    m = jnp.mean(x, axis=axis, keepdims=True)
    v = jnp.var(x, axis=axis, keepdims=True)
    return (x - m) / jnp.sqrt(v + eps)

def _scatter_add(tgt, idx, src, axis=0):
    return tgt.at[idx].add(src)

def _segment_sum(src, seg, n):
    return jax.ops.segment_sum(src, seg, n)
kernel_name = 'mk_hybrid_d1_jaxref_r8_5a811f'

def setup_inputs(seed: int=0):
    np.random.seed(seed)
    _w = jnp.asarray

    def _L0_attn_a_setup():
        import jax, jax.numpy as jnp
        import numpy as np
        import math
        from jax import lax
        B, L, D = (8, 512, 128)
        FILTER_ORDER = 64
        EMB_DIM = 3
        SHIFT = 0.05
        KSIZE = 3

        def _implicit_filter(f_w1, f_b1, freq1, f_w2, f_b2, freq2, f_w3, f_b3, freq3, f_wout):
            t = jnp.linspace(0.0, 1.0, L)
            t_resc = jnp.linspace(0.0, L - 1.0, L)
            w = 2.0 * jnp.pi * t_resc / L
            bands = (EMB_DIM - 1) // 2
            f = jnp.linspace(0.0001, bands - 1.0, bands)
            fw = f[None, :] * w[:, None]
            z = jnp.concatenate([t[:, None], jnp.cos(fw), -jnp.sin(fw)], axis=-1)
            h = jnp.sin(freq1 * (z @ f_w1 + f_b1))
            h = jnp.sin(freq2 * (h @ f_w2 + f_b2))
            h = jnp.sin(freq3 * (h @ f_w3 + f_b3))
            h = h @ f_wout
            max_decay = math.log(0.01) / 0.3
            min_decay = math.log(0.01) / 1.5
            deltas = jnp.linspace(min_decay, max_decay, D)
            decay = jnp.exp(-t[:, None] * jnp.abs(deltas)[None, :])
            return h * (decay + SHIFT)
        key = jax.random.key(seed)
        ks = jax.random.split(key, 12)
        s = 0.02
        return {'u': jax.random.normal(ks[0], (B, L, D), jnp.float32), 'w_in': jax.random.normal(ks[1], (D, 3 * D), jnp.float32) * s, 'b_in': jnp.zeros((3 * D,), jnp.float32), 'sf_w': jax.random.normal(ks[2], (3 * D, KSIZE), jnp.float32) * 0.3, 'sf_b': jnp.zeros((3 * D,), jnp.float32), 'f_w1': jax.random.normal(ks[3], (EMB_DIM, FILTER_ORDER), jnp.float32) * 0.5, 'f_b1': jnp.zeros((FILTER_ORDER,), jnp.float32), 'freq1': jnp.ones((FILTER_ORDER,), jnp.float32), 'f_w2': jax.random.normal(ks[4], (FILTER_ORDER, FILTER_ORDER), jnp.float32) * 0.12, 'f_b2': jnp.zeros((FILTER_ORDER,), jnp.float32), 'freq2': jnp.ones((FILTER_ORDER,), jnp.float32), 'f_w3': jax.random.normal(ks[5], (FILTER_ORDER, FILTER_ORDER), jnp.float32) * 0.12, 'f_b3': jnp.zeros((FILTER_ORDER,), jnp.float32), 'freq3': jnp.ones((FILTER_ORDER,), jnp.float32), 'f_wout': jax.random.normal(ks[6], (FILTER_ORDER, D), jnp.float32) * s, 'filt_bias': jax.random.normal(ks[7], (D,), jnp.float32), 'w_out': jax.random.normal(ks[8], (D, D), jnp.float32) * s, 'b_out': jnp.zeros((D,), jnp.float32)}
    _L0_attn_a_in = _L0_attn_a_setup()

    def _L0_attn_b_setup():
        import jax, jax.numpy as jnp
        import numpy as np
        N_HEAD = 16
        EPS = 1e-06

        def _linear_attention(q, k, v):
            B, H, D = (q.shape[1], q.shape[2], q.shape[3])

            def step(carry, qkv_t):
                S, z = carry
                qt, kt, vt = qkv_t
                S = S + kt[..., :, None] * vt[..., None, :]
                z = z + kt
                num = jnp.einsum('bhi,bhij->bhj', qt, S)
                den = jnp.sum(qt * z, axis=-1, keepdims=True)
                return ((S, z), num / (den + EPS))
            S0 = jnp.zeros((B, H, D, D), q.dtype)
            z0 = jnp.zeros((B, H, D), q.dtype)
            _, y = jax.lax.scan(step, (S0, z0), (q, k, v))
            return y
        key = jax.random.key(seed)
        k1, k2, k3 = jax.random.split(key, 3)
        B, T, C = (2, 256, 128)
        x = jax.random.normal(k1, (B, T, C), dtype=jnp.float32)
        w_attn = jax.random.normal(k2, (C, 3 * C), dtype=jnp.float32) * 0.02
        w_proj = jax.random.normal(k3, (C, C), dtype=jnp.float32) * 0.02
        return {'x': x, 'w_attn': w_attn, 'w_proj': w_proj}
    _L0_attn_b_in = _L0_attn_b_setup()

    def _L0_ffn_setup():
        import jax, jax.numpy as jnp
        import numpy as np
        H = 128
        I = 256
        E = 8
        B, S = (2, 128)

        def _swiglu(x, wg, wu, wd):
            return jax.nn.silu(x @ wg) * (x @ wu) @ wd
        key = jax.random.key(seed)
        ks = jax.random.split(key, 8)
        sc_h = 1.0 / np.sqrt(H)
        sc_i = 1.0 / np.sqrt(I)
        return {'hidden_states': jax.random.normal(ks[0], (B, S, H), jnp.float32), 'gate_w': jax.random.normal(ks[1], (H, E), jnp.float32) * sc_h, 'sh_gate': jax.random.normal(ks[2], (H, I), jnp.float32) * sc_h, 'sh_up': jax.random.normal(ks[3], (H, I), jnp.float32) * sc_h, 'sh_down': jax.random.normal(ks[4], (I, H), jnp.float32) * sc_i, 'rt_gate': jax.random.normal(ks[5], (E, H, I), jnp.float32) * sc_h, 'rt_up': jax.random.normal(ks[6], (E, H, I), jnp.float32) * sc_h, 'rt_down': jax.random.normal(ks[7], (E, I, H), jnp.float32) * sc_i}
    _L0_ffn_in = _L0_ffn_setup()
    _d = {'L0_attn_a_u': _L0_attn_a_in['u'], 'L0_attn_a_w_in': _L0_attn_a_in['w_in'], 'L0_attn_a_b_in': _L0_attn_a_in['b_in'], 'L0_attn_a_sf_w': _L0_attn_a_in['sf_w'], 'L0_attn_a_sf_b': _L0_attn_a_in['sf_b'], 'L0_attn_a_f_w1': _L0_attn_a_in['f_w1'], 'L0_attn_a_f_b1': _L0_attn_a_in['f_b1'], 'L0_attn_a_freq1': _L0_attn_a_in['freq1'], 'L0_attn_a_f_w2': _L0_attn_a_in['f_w2'], 'L0_attn_a_f_b2': _L0_attn_a_in['f_b2'], 'L0_attn_a_freq2': _L0_attn_a_in['freq2'], 'L0_attn_a_f_w3': _L0_attn_a_in['f_w3'], 'L0_attn_a_f_b3': _L0_attn_a_in['f_b3'], 'L0_attn_a_freq3': _L0_attn_a_in['freq3'], 'L0_attn_a_f_wout': _L0_attn_a_in['f_wout'], 'L0_attn_a_filt_bias': _L0_attn_a_in['filt_bias'], 'L0_attn_a_w_out': _L0_attn_a_in['w_out'], 'L0_attn_a_b_out': _L0_attn_a_in['b_out'], 'L0_attn_b_w_attn': _L0_attn_b_in['w_attn'], 'L0_attn_b_w_proj': _L0_attn_b_in['w_proj'], 'L0_ffn_gate_w': _L0_ffn_in['gate_w'], 'L0_ffn_sh_gate': _L0_ffn_in['sh_gate'], 'L0_ffn_sh_up': _L0_ffn_in['sh_up'], 'L0_ffn_sh_down': _L0_ffn_in['sh_down'], 'L0_ffn_rt_gate': _L0_ffn_in['rt_gate'], 'L0_ffn_rt_up': _L0_ffn_in['rt_up'], 'L0_ffn_rt_down': _L0_ffn_in['rt_down']}
    _x0 = _d['L0_attn_a_u']
    _d['L0_attn_a_u'] = jax.random.normal(jax.random.fold_in(jax.random.key(seed), 1), (16, 256, 128), dtype=_x0.dtype)
    del _x0
    return _d

def reference(L0_attn_a_u, L0_attn_a_w_in, L0_attn_a_b_in, L0_attn_a_sf_w, L0_attn_a_sf_b, L0_attn_a_f_w1, L0_attn_a_f_b1, L0_attn_a_freq1, L0_attn_a_f_w2, L0_attn_a_f_b2, L0_attn_a_freq2, L0_attn_a_f_w3, L0_attn_a_f_b3, L0_attn_a_freq3, L0_attn_a_f_wout, L0_attn_a_filt_bias, L0_attn_a_w_out, L0_attn_a_b_out, L0_attn_b_w_attn, L0_attn_b_w_proj, L0_ffn_gate_w, L0_ffn_sh_gate, L0_ffn_sh_up, L0_ffn_sh_down, L0_ffn_rt_gate, L0_ffn_rt_up, L0_ffn_rt_down):

    def _L0_attn_a_ref(u, w_in, b_in, sf_w, sf_b, f_w1, f_b1, freq1, f_w2, f_b2, freq2, f_w3, f_b3, freq3, f_wout, filt_bias, w_out, b_out):
        import jax, jax.numpy as jnp
        import numpy as np
        import math
        from jax import lax
        B, L, D = (8, 512, 128)
        FILTER_ORDER = 64
        EMB_DIM = 3
        SHIFT = 0.05
        KSIZE = 3

        def _implicit_filter(f_w1, f_b1, freq1, f_w2, f_b2, freq2, f_w3, f_b3, freq3, f_wout):
            t = jnp.linspace(0.0, 1.0, L)
            t_resc = jnp.linspace(0.0, L - 1.0, L)
            w = 2.0 * jnp.pi * t_resc / L
            bands = (EMB_DIM - 1) // 2
            f = jnp.linspace(0.0001, bands - 1.0, bands)
            fw = f[None, :] * w[:, None]
            z = jnp.concatenate([t[:, None], jnp.cos(fw), -jnp.sin(fw)], axis=-1)
            h = jnp.sin(freq1 * (z @ f_w1 + f_b1))
            h = jnp.sin(freq2 * (h @ f_w2 + f_b2))
            h = jnp.sin(freq3 * (h @ f_w3 + f_b3))
            h = h @ f_wout
            max_decay = math.log(0.01) / 0.3
            min_decay = math.log(0.01) / 1.5
            deltas = jnp.linspace(min_decay, max_decay, D)
            decay = jnp.exp(-t[:, None] * jnp.abs(deltas)[None, :])
            return h * (decay + SHIFT)
        b, l, d = u.shape
        up = (u @ w_in + b_in).transpose(0, 2, 1)
        uc = lax.conv_general_dilated(up, sf_w[:, None, :], (1,), [(KSIZE - 1, KSIZE - 1)], feature_group_count=3 * d, dimension_numbers=('NCH', 'OIH', 'NCH'))[..., :l] + sf_b[None, :, None]
        x0, x1, v = jnp.split(uc, 3, axis=1)
        k = _implicit_filter(f_w1, f_b1, freq1, f_w2, f_b2, freq2, f_w3, f_b3, freq3, f_wout).T
        v = v * x1
        n = 2 * l
        y = jnp.fft.irfft(jnp.fft.rfft(v, n=n) * jnp.fft.rfft(k, n=n), n=n)[..., :l]
        v = y + v * filt_bias[None, :, None]
        out = (v * x0).transpose(0, 2, 1)
        return out @ w_out + b_out

    def _L0_attn_b_ref(x, w_attn, w_proj):
        import jax, jax.numpy as jnp
        import numpy as np
        N_HEAD = 16
        EPS = 1e-06

        def _linear_attention(q, k, v):
            B, H, D = (q.shape[1], q.shape[2], q.shape[3])

            def step(carry, qkv_t):
                S, z = carry
                qt, kt, vt = qkv_t
                S = S + kt[..., :, None] * vt[..., None, :]
                z = z + kt
                num = jnp.einsum('bhi,bhij->bhj', qt, S)
                den = jnp.sum(qt * z, axis=-1, keepdims=True)
                return ((S, z), num / (den + EPS))
            S0 = jnp.zeros((B, H, D, D), q.dtype)
            z0 = jnp.zeros((B, H, D), q.dtype)
            _, y = jax.lax.scan(step, (S0, z0), (q, k, v))
            return y
        B, T, C = x.shape
        H = N_HEAD
        D = C // H
        qkv = x @ w_attn
        q, k, v = jnp.split(qkv, 3, axis=-1)

        def to_tbhd(a):
            return a.reshape(B, T, H, D).transpose(1, 0, 2, 3)
        q = jax.nn.elu(to_tbhd(q)) + 1.0
        k = jax.nn.elu(to_tbhd(k)) + 1.0
        v = to_tbhd(v)
        y = _linear_attention(q, k, v)
        y = y.transpose(1, 0, 2, 3).reshape(B, T, C)
        return y @ w_proj

    def _L0_ffn_ref(hidden_states, gate_w, sh_gate, sh_up, sh_down, rt_gate, rt_up, rt_down):
        import jax, jax.numpy as jnp
        import numpy as np
        H = 128
        I = 256
        E = 8
        B, S = (2, 128)

        def _swiglu(x, wg, wu, wd):
            return jax.nn.silu(x @ wg) * (x @ wu) @ wd
        b, s, h = hidden_states.shape
        x = hidden_states.reshape(-1, h)
        logits = x @ gate_w
        top_val = jnp.max(logits, axis=-1, keepdims=True)
        top_id = jnp.argmax(logits, axis=-1)
        score = jax.nn.sigmoid(top_val)
        xs = x * score
        g = jnp.einsum('th,ehi->eti', xs, rt_gate)
        u = jnp.einsum('th,ehi->eti', xs, rt_up)
        act = jax.nn.silu(g) * u
        y = jnp.einsum('eti,eih->eth', act, rt_down)
        onehot = jax.nn.one_hot(top_id, E, dtype=x.dtype)
        routed = jnp.einsum('eth,te->th', y, onehot)
        shared = _swiglu(x, sh_gate, sh_up, sh_down)
        return (shared + routed).reshape(b, s, h)
    x = L0_attn_a_u
    x = x + _L0_attn_a_ref(_layernorm(x, axis=-1), L0_attn_a_w_in, L0_attn_a_b_in, L0_attn_a_sf_w, L0_attn_a_sf_b, L0_attn_a_f_w1, L0_attn_a_f_b1, L0_attn_a_freq1, L0_attn_a_f_w2, L0_attn_a_f_b2, L0_attn_a_freq2, L0_attn_a_f_w3, L0_attn_a_f_b3, L0_attn_a_freq3, L0_attn_a_f_wout, L0_attn_a_filt_bias, L0_attn_a_w_out, L0_attn_a_b_out)
    x = x + _L0_ffn_ref(_layernorm(x, axis=-1), L0_ffn_gate_w, L0_ffn_sh_gate, L0_ffn_sh_up, L0_ffn_sh_down, L0_ffn_rt_gate, L0_ffn_rt_up, L0_ffn_rt_down)
    x = x + _L0_attn_b_ref(_layernorm(x, axis=-1), L0_attn_b_w_attn, L0_attn_b_w_proj)
    x = x + _L0_ffn_ref(_layernorm(x, axis=-1), L0_ffn_gate_w, L0_ffn_sh_gate, L0_ffn_sh_up, L0_ffn_sh_down, L0_ffn_rt_gate, L0_ffn_rt_up, L0_ffn_rt_down)
    return x

_drawn_inputs = setup_inputs


def setup_inputs(seed=0):
    import zlib

    import numpy as np

    out = dict(_drawn_inputs(seed))
    spreads = {'L0_attn_a_b_in': (0.0, 0.288),
     'L0_attn_a_sf_b': (0.0, 0.296),
     'L0_attn_a_f_b1': (0.0, 0.8),
     'L0_attn_a_freq1': (1.0, 0.6),
     'L0_attn_a_f_b2': (0.0, 0.631),
     'L0_attn_a_freq2': (1.0, 0.6),
     'L0_attn_a_f_b3': (0.0, 0.8),
     'L0_attn_a_freq3': (1.0, 0.6),
     'L0_attn_a_b_out': (0.0, 0.1)}
    factors = {'L0_attn_a_w_in': 3.081,
     'L0_attn_a_f_w1': 2.961,
     'L0_attn_a_f_w2': 3.269,
     'L0_attn_a_f_w3': 3.423,
     'L0_attn_a_f_wout': 2.825,
     'L0_attn_a_filt_bias': 4.573,
     'L0_attn_b_w_attn': 3.393,
     'L0_attn_b_w_proj': 2.787}
    for name, (base, spread) in spreads.items():
        noise = np.random.default_rng([zlib.crc32(name.encode()), seed]).standard_normal(out[name].shape)
        drawn = base * np.exp(spread * noise) if base else spread * noise
        out[name] = jnp.asarray(drawn.astype(out[name].dtype))
    for name, factor in factors.items():
        out[name] = (out[name] * factor).astype(out[name].dtype)
    return out
```

```python
from contextlib import ExitStack

import numpy as np

import concourse.bass as bass
from concourse import mybir

F32 = mybir.dt.float32
BF16 = mybir.dt.bfloat16
I32 = mybir.dt.int32
U32 = mybir.dt.uint32
ALU = mybir.AluOpType
ACT = mybir.ActivationFunctionType
AX = mybir.AxisListType

P = 128
B, L, D = 16, 256, 128
TILES = B * L // P
PAIR = 4
PAIRS = TILES // PAIR
PT = PAIR * P
NF = 512
TAU = NF // P
SB = L // P
FB = NF // 2 // P
ORDER = 64
E = 8
I = 256
IB = I // P
WE = 2 * I + IB * D
RING = 4
RT = -(-(TILES + E - 1) // RING) * RING
HEADS, HD = 16, 8
HV = HD + 1
GROUPS = 4
LN_EPS = 1e-5
ATT_EPS = 1e-6
ROUND = 1.5 * 2.0 ** 23
TWO_PI_HI = 6.28125
TWO_PI_LO = 2 * np.pi - TWO_PI_HI
PI_BELOW = 3.1415925


def packed(columns):
    at, where = 0, {}
    for name, n in columns:
        where[name] = (at, at + n)
        at += n
    return where, at


TABLES, TABLES_N = packed([
    ("identity", P), ("decay", TAU * D), ("dft", TAU * NF), ("inverse_dft", 2 * FB * L),
    ("causal", P), ("own_head", HEADS * HV), ("head_of_group", GROUPS), ("tie_rank", E),
    ("tile_starts", TILES), ("tile_numbers", RT)])
WEIGHTS, WEIGHTS_N = packed([
    ("w_in", 3 * D), ("taps", 9), ("b_in", 3), ("sf_b", 3), ("w_out", D), ("gate_w", E),
    ("sh_gate", I), ("sh_up", I), ("sh_down", IB * D), ("w_attn", 3 * D), ("w_proj", D)])
FILTER, FILTER_N = packed([("f_w2", ORDER), ("f_w3", ORDER), ("f_wout", D), ("f_vectors", 6)])


def shape_constants():
    c = {}
    t = np.linspace(0.0, 1.0, NF)
    w = 2 * np.pi * np.arange(NF) / NF
    positions = np.stack([t, np.cos(1e-4 * w), -np.sin(1e-4 * w)])
    rates = np.abs(np.linspace(np.log(0.01) / 1.5, np.log(0.01) / 0.3, D))
    decay = np.exp(-t[:, None] * rates[None]) + 0.05
    c["decay"] = decay.reshape(TAU, P, D).transpose(1, 0, 2)
    tau, f = np.arange(NF)[:, None], np.arange(NF // 2)[None]
    cos, sin = np.cos(2 * np.pi * tau * f / NF), -np.sin(2 * np.pi * tau * f / NF)
    sin[:, 0] = (-1.0) ** np.arange(NF)
    dft = np.stack([cos, sin], 1)
    c["dft"] = dft.reshape(TAU, P, 2, NF // 2).transpose(1, 0, 2, 3)
    weight = np.where(np.arange(NF // 2) == 0, 1.0, 2.0) / NF
    inv = (dft[:L] * weight).transpose(1, 2, 0)
    c["inverse_dft"] = inv.reshape(2, FB, P, L).transpose(2, 0, 1, 3)
    c["identity"] = np.eye(P)
    row = np.arange(P)[:, None]
    c["head_of_group"] = (row // HD % GROUPS == np.arange(GROUPS)[None]) * 1.0
    c["own_head"] = np.repeat(row // HD == np.arange(HEADS)[None], HV, 1) * 1.0
    c["causal"] = (np.arange(P)[None] >= row) * 1.0
    c["tie_rank"] = np.tile(E - np.arange(E), (P, 1)) * 1.0
    c["tile_starts"] = np.tile(P * np.arange(TILES), (P, 1)) * 1.0
    c["tile_numbers"] = np.tile(np.arange(RT), (P, 1)) * 1.0
    tables = np.concatenate([c[name].reshape(P, -1) for name in TABLES], 1)
    return np.ascontiguousarray(tables, np.float32), np.ascontiguousarray(positions, np.float32)


def wait(eng, sem, value):
    if not isinstance(value, int) or value > 0:
        eng.wait_ge(sem, value)


def hybrid_block(nc, x, weights, filter_weights, f_w1, filt_bias, b_out, rt_gate, rt_up, rt_down,
                 tables, positions, out, phases=4):
    with ExitStack() as ctx:
        def sb(name, shape, dt=F32):
            return ctx.enter_context(nc.sbuf_tensor(name, shape, dt))

        def sem(name):
            return ctx.enter_context(nc.semaphore(name))

        bank = [ctx.enter_context(nc.psum_tensor(f"bank{i}", [P, 512], F32)) for i in range(8)]
        sorted_rows = nc.dram_tensor("sorted_rows", [RT * P, D], F32, kind="Internal").ap()
        sorted_out = nc.dram_tensor("sorted_out", [RT * P, D], F32, kind="Internal").ap()

        residual = sb("residual", [P, TILES, D])
        tables_sb = sb("tables_sb", [P, TABLES_N])
        weights_sb = sb("weights_sb", [P, WEIGHTS_N])
        filter_sb = sb("filter_sb", [ORDER, FILTER_N])

        def table(name, pattern=None, **sizes):
            v = tables_sb[:, TABLES[name][0]:TABLES[name][1]]
            return v.rearrange(pattern, **sizes) if pattern else v

        def weight(name, pattern=None, **sizes):
            v = weights_sb[:, WEIGHTS[name][0]:WEIGHTS[name][1]]
            return v.rearrange(pattern, **sizes) if pattern else v

        ident = table("identity")
        decay = table("decay", "p (t d) -> p t d", t=TAU)
        dft = table("dft", "p (t c f) -> p t c f", t=TAU, c=2)
        inverse_dft = table("inverse_dft", "p (c f t) -> p c f t", c=2, f=FB)
        head_of_group, own_head, causal = table("head_of_group"), table("own_head"), table("causal")
        tie_rank, tile_starts, tile_numbers = table("tie_rank"), table("tile_starts"), table("tile_numbers")
        w_in_sb, w_out_sb, gate_sb = weight("w_in"), weight("w_out"), weight("gate_w")
        w_attn_sb, w_proj_sb = weight("w_attn"), weight("w_proj")
        taps = weight("taps", "p (g k) -> p g k", g=3)
        b_in_sb, sf_b_sb = weight("b_in"), weight("sf_b")
        shared_gate, shared_up = weight("sh_gate"), weight("sh_up")
        shared_down = weight("sh_down", "p (i d) -> p i d", i=IB)
        f_w2_sb, f_w3_sb, f_wout_sb, f_vec = (filter_sb[:, a:b] for a, b in FILTER.values())
        positions_sb = sb("positions_sb", [3, NF])
        f_w1_sb = sb("f_w1_sb", [3, ORDER])
        filt_bias_row = sb("filt_bias_row", [1, D])
        b_out_all = sb("b_out_all", [P, D])
        experts = sb("experts", [P, E * WE])
        experts_v = experts[:].rearrange("p (e c) -> p e c", e=E)

        stats = sb("stats", [P, PAIR, 6])
        step_stats = sb("step_stats", [P, PAIR, 2])
        step_rstd = sb("step_rstd", [P, PAIR])
        mean_var = sb("mean_var", [P, TILES, 2])
        rstd = sb("rstd", [P, TILES])
        held = sb("held", [P, 8])
        step_kept = sb("step_kept", [P, PAIR, 2])
        eps_tile = sb("eps_tile", [P, TILES])
        neg_half = sb("neg_half", [P, TILES])
        normed = sb("normed", [P, PAIR, D])
        normed_t = sb("normed_t", [P, PT])

        rows = sb("rows", [P, TILES, D])
        wide = sb("wide", [P, TILES * D])

        x_loaded = [sem(f"x_loaded{n}") for n in range(3)]
        filter_loaded = sem("filter_loaded")
        tables_loaded = [sem(f"tables_loaded{n}") for n in range(3)]
        weights_loaded = sem("weights_loaded")
        loaded_experts = sem("loaded_experts")
        const_made = sem("const_made")
        zero_rows_stored = sem("zero_rows_stored")
        stored = sem("stored")

        class Norm:

            def __init__(self, name, n):
                self.n = n
                self.bn = sem(f"{name}_bn")
                self.aggr = sem(f"{name}_aggr")
                self.kept = sem(f"{name}_kept")
                self.eps = sem(f"{name}_eps")
                self.rstd = sem(f"{name}_rstd")
                self.normed = sem(f"{name}_normed")
                self.turned = sem(f"{name}_turned")
                self.copied = sem(f"{name}_copied")

        def hold_vector(dve):
            dve.memset(held[:, 0:1], 0.0)

        def hold_gpsimd(pool, n):
            pool.tensor_tensor(held[:, 1 + n:2 + n], neg_half[:, 0:1], neg_half[:, 0:1], ALU.add)

        def norm_stats(dve, ln, k, added=None):
            n = ln.n
            if added is not None:
                dve.wait_ge(added, k + 1)
            wait(dve, ln.aggr, k)
            hold_vector(dve)
            for j in range(n):
                dve.bn_stats(stats[:, j, :], residual[:, bass.ds(k * n + j, 1), :]).then_inc(ln.bn, 1)
            dve.wait_ge(ln.bn, n * (k + 1))
            wait(dve, ln.normed, n * k)
            hold_vector(dve)
            for j in range(n):
                last = dve.bn_aggr(step_stats[:, j, :], stats[:, j, :])
            last.then_inc(ln.aggr, 1)

        def norm_rstd(pool, ln, k):
            n = ln.n
            pool.wait_ge(ln.aggr, k + 1)
            pool.tensor_tensor(step_rstd[:, 0:n], step_stats[:, 0:n, 1], eps_tile[:, 0:n], ALU.add).then_inc(ln.eps, 1)
            pool.wait_ge(ln.eps, k + 1)
            pool.tensor_tensor(step_rstd[:, 0:n], step_rstd[:, 0:n], neg_half[:, 0:n], ALU.pow).then_inc(ln.rstd, 1)

        def norm_apply(dve, ln, k, kept=False):
            n = ln.n
            if not kept:
                dve.wait_ge(ln.rstd, k + 1)
            wait(dve, ln.turned, k)
            for j in range(n):
                t = bass.ds(k * n + j, 1)
                mean, scale = (mean_var[:, t, 0], rstd[:, t]) if kept else (step_stats[:, j, 0:1], step_rstd[:, j:j + 1])
                dve.tensor_scalar(normed[:, j, :], residual[:, t, :], mean, scale,
                                  ALU.subtract, ALU.mult).then_inc(ln.normed, 1)

        def keep_stats(dve, ln, tiles, k, added):
            at = k * tiles
            dve.wait_ge(added, k + 1)
            wait(dve, ln.aggr, k)
            hold_vector(dve)
            for j in range(tiles):
                dve.bn_stats(stats[:, j, :], residual[:, bass.ds(at + j, 1), :]).then_inc(ln.bn, 1)
            dve.wait_ge(ln.bn, tiles * (k + 1))
            wait(dve, ln.kept, k)
            hold_vector(dve)
            for j in range(tiles):
                last = dve.bn_aggr(step_kept[:, j, :], stats[:, j, :])
            last.then_inc(ln.aggr, 1)
            dve.wait_ge(ln.aggr, k + 1)
            dve.tensor_scalar(mean_var[:, bass.ds(at, tiles), :], step_kept[:, 0:tiles, :], 1.0, None, ALU.mult
                              ).then_inc(ln.kept, 1)

        def norm_turn(pe, ln, k, into):
            n = ln.n
            pe.wait_ge(ln.normed, n * (k + 1))
            wait(pe, ln.copied, k)
            for j in range(n):
                turned = pe.transpose(into[:, j * P:(j + 1) * P], normed[:, j, :], ident)
            turned.then_inc(ln.turned, 1)

        ln_c = Norm("conv_ln", PAIR)
        spectrum = sb("spectrum", [P, 3, FB, D])
        filter_h = sb("filter_h", [ORDER, NF])
        filter_a = sb("filter_a", [ORDER, NF])
        filter_r = sb("filter_r", [ORDER, NF])
        filter_k = sb("filter_k", [P, TAU, D])
        conv_bias = sb("conv_bias", [P, 3])
        conv_edge = sb("conv_edge", [P, 3, 2])
        edge_tmp = sb("edge_tmp", [P, 3, 2])
        conv_xv = sb("conv_xv", [P, 2, PT])
        value_c = sb("value_c", [P, PT])
        value_t = sb("value_t", [P, PAIR, D])
        prod = sb("prod", [P, 4, PT])
        spect_y = sb("spect_y", [P, 2, PT])
        gated = sb("gated", [P, PT])

        flt = sem("flt")
        flt_pe = sem("flt_pe")
        flt_act = sem("flt_act")
        edges_made = sem("edges_made")
        c_proj = sem("c_proj")
        c_tap2 = sem("c_tap2")
        c_edge = sem("c_edge")
        c_tap1 = sem("c_tap1")
        c_conv = sem("c_conv")
        c_value = sem("c_value")
        c_value_turned = sem("c_value_turned")
        c_value_copied = sem("c_value_copied")
        c_forward = sem("c_forward")
        c_prod = sem("c_prod")
        c_spect = sem("c_spect")
        c_inverse = sem("c_inverse")
        c_gated = sem("c_gated")
        c_out = sem("c_out")
        c_bias = sem("c_bias")
        c_added = sem("c_added")

        gates = wide[:]

        logits = sb("logits", [P, TILES, E])
        r_a = sb("r_a", [P, TILES, E])
        r_b = sb("r_b", [P, TILES, E])
        chosen = sb("chosen", [P, TILES, E])
        chosen_b = sb("chosen_b", [P, TILES, E], BF16)
        before_b = sb("before_b", [P, P], BF16)
        ones_b = sb("ones_b", [P, P], BF16)
        top = sb("top", [P, TILES])
        best = sb("best", [P, TILES])
        score = sb("score", [P, TILES])
        counts = sb("counts", [P, E, TILES])
        running = sb("running", [P, E, TILES])
        cmp_tiles = sb("cmp_tiles", [P, E, TILES])
        zeros = sb("zeros", [P, E * TILES])
        ends = sb("ends", [P, E + 1])
        n_tok = sb("n_tok", [P, E])
        n_tiles = sb("n_tiles", [P, E])
        tile_ends = sb("tile_ends", [P, E])
        start_at = sb("start_at", [P, E])
        place_f = sb("place_f", [P, TILES])
        place = sb("place", [P, TILES], I32)
        cmp_e = sb("cmp_e", [P, RT, E - 1])
        tile_expert_f = sb("tile_expert_f", [P, RT])
        tile_expert = sb("tile_expert", [P, RT], I32)
        silu_sh = sb("silu_sh", [P, IB, PT])
        act_sh = sb("act_sh", [P, IB, PT])
        row_in = sb("row_in", [P, RING, D])
        row_in_t = sb("row_in_t", [P, RING, P])
        row_silu = sb("row_silu", [P, RING, I])
        row_act = sb("row_act", [P, RING, I])
        row_act_t = sb("row_act_t", [P, RING, IB, P])
        row_out = sb("row_out", [P, RING, D])
        normed_all = wide[:]

        class Experts:

            def __init__(self, name, stat_steps):
                self.stat_steps = stat_steps
                s = lambda what: sem(f"{name}_{what}")
                self.ln = Norm(f"{name}_ln", PAIR)
                self.kept = s("kept")
                self.logits = s("logits")
                self.route = s("route")
                self.score = s("score")
                self.counted = s("counted")
                self.rows = s("rows")
                self.sent = s("sent")
                self.up = s("up")
                self.silu = s("silu")
                self.act = s("act")
                self.down = s("down")
                self.added = s("added")
                self.row_in = [s(f"row_in{r}") for r in range(RING)]
                self.row_turned = s("row_turned")
                self.row_copied = s("row_copied")
                self.row_up = s("row_up")
                self.row_silu = s("row_silu")
                self.row_act = s("row_act")
                self.act_turned = s("act_turned")
                self.act_copied = s("act_copied")
                self.row_down = s("row_down")
                self.row_out = s("row_out")
                self.row_stored = [s(f"row_stored{r}") for r in range(RING)]
                self.back = s("back")
                self.summed = s("summed")

        moe = [Experts("moe0", PAIRS), Experts("moe1", B)]

        def routed_steps(eng, *parts):
            most = max(lead for lead, _ in parts)
            for n in range(-most, 0):
                for lead, part in parts:
                    if n + lead >= 0:
                        part(0, n + lead)
            steps = RT // RING

            def body(i, limit=None):
                for r in range(RING):
                    for lead, part in parts:
                        if limit is None or RING * i + r + lead < limit:
                            part(i + (r + lead) // RING, (r + lead) % RING)

            body(0)
            with eng.Fori(1, steps - 1) as i:
                body(i)
            body(steps - 1, RT)

        AT = 2
        ln_a = Norm("att_ln", AT)
        att_exp = sb("att_exp", [P, 2 * L])
        att_relu = sb("att_relu", [P, 2 * L])
        qk = sb("qk", [P, 2 * L])
        q_by_head = sb("q_by_head", [P, GROUPS, L])
        k_tok = sb("k_tok", [P, P])
        v_aug = sb("v_aug", [P, AT, HEADS, HV])
        scores = sb("scores", [P, AT, HEADS, P])
        state = sb("state", [P, HEADS * HV])
        den = sb("den", [P, AT * HEADS])
        att_y = sb("att_y", [P, AT, D])
        att_yt = sb("att_yt", [P, AT * P])
        a_proj = sem("a_proj")
        a_vproj = sem("a_vproj")
        a_exp = sem("a_exp")
        a_relu = sem("a_relu")
        a_qk = sem("a_qk")
        a_by_head = sem("a_by_head")
        a_v = sem("a_v")
        a_k_turned = sem("a_k_turned")
        a_k_tok = sem("a_k_tok")
        a_state_mm = sem("a_state_mm")
        a_state = sem("a_state")
        a_score = sem("a_score")
        a_masked = sem("a_masked")
        a_copied = sem("a_copied")
        a_cleared = sem("a_cleared")
        a_y_mm = sem("a_y_mm")
        a_den = sem("a_den")
        a_y = sem("a_y")
        a_y_turned = sem("a_y_turned")
        a_yt = sem("a_yt")
        a_out = sem("a_out")
        a_added = sem("a_added")

        block = ctx.enter_context(nc.Block())

        x_v = x.rearrange("b (s p) d -> p (b s) d", p=P)
        out_v = out.rearrange("b (s p) d -> p (b s) d", p=P)
        x_parts = (0, PAIR, 2 * PAIR, TILES)
        filter_loads = [(filter_sb[:], filter_weights), (positions_sb[:], positions), (f_w1_sb[:], f_w1),
                        (filt_bias_row[:], filt_bias.rearrange("(a d) -> a d", a=1))]
        table_parts = (0, TABLES["decay"][1], TABLES["inverse_dft"][1], TABLES_N)
        expert_loads = [(experts_v[:, :, 0:I], rt_gate.rearrange("e p i -> p e i")),
                        (experts_v[:, :, I:2 * I], rt_up.rearrange("e p i -> p e i"))] + [
            (experts_v[:, :, 2 * I + i * D:2 * I + (i + 1) * D],
             rt_down[:, i * P:(i + 1) * P, :].rearrange("e p d -> p e d")) for i in range(IB)]

        def routed_io(sp, m):
            def load(i):
                for r in range(RING):
                    wait(sp, m.row_turned, RING * i + r - RING + 1)
                    sp.dma_start(row_in[:, r, :], sorted_rows[bass.ds((RING * i + r) * P, P), :]
                                 ).then_inc(m.row_in[r], 16)

            def store(i):
                for r in range(RING):
                    sp.wait_ge(m.row_out, RING * i + r + 1)
                    sp.dma_start(sorted_out[bass.ds((RING * i + r) * P, P), :], row_out[:, r, :]
                                 ).then_inc(m.row_stored[r], 16)

            sp.wait_ge(m.sent, 16 * TILES)
            load(0)
            with sp.Fori(1, RT // RING) as i:
                load(i)
                store(i - 1)
            store(RT // RING - 1)

        @block.sync
        def _(sp):
            for n in range(3):
                a, b = x_parts[n:n + 2]
                sp.dma_start(residual[:, a:b, :], x_v[:, a:b, :]).then_inc(x_loaded[n], 16)
            a, b = table_parts[1:3]
            sp.dma_start(tables_sb[:, a:b], tables[:, a:b]).then_inc(tables_loaded[1], 16)
            for dst, src in expert_loads:
                sp.dma_start(dst, src).then_inc(loaded_experts, 16)
            sp.wait_ge(const_made, 5)
            sp.dma_start(sorted_rows.rearrange("(t p) d -> p t d", p=P),
                         zeros[:, 0:D].unsqueeze(1).to_broadcast([P, RT, D])).then_inc(zero_rows_stored, 16)
            if phases >= 2:
                routed_io(sp, moe[0])
            if phases >= 4:
                routed_io(sp, moe[1])
            if phases in (1, 3):
                sp.wait_ge(c_added if phases == 1 else a_added, PAIRS if phases == 1 else B)
            for k in range(PAIRS):
                if phases in (2, 4):
                    sp.wait_ge(moe[phases // 2 - 1].summed, k + 1)
                sp.dma_start(out_v[:, k * PAIR:(k + 1) * PAIR, :], residual[:, k * PAIR:(k + 1) * PAIR, :]
                             ).then_inc(stored, 16)
            sp.wait_ge(stored, 16 * PAIRS)
            sp.wait_ge(zero_rows_stored, 16)
            sp.wait_ge(loaded_experts, 16 * len(expert_loads))
            sp.wait_ge(tables_loaded[2], 16)

        def send_rows(pool, m):
            for t in range(TILES):
                pool.wait_ge(m.rows, t + 1)
                pool.indirect_dma_start(
                    sorted_rows, bass.IndirectOffsetOnAxis(ap=place[:, t:t + 1].bitcast(U32), axis=0),
                    rows[:, t, :], None).then_inc(m.sent, 16)

        def fetch_rows(pool, m):
            for r in range(RING):
                pool.wait_ge(m.row_stored[r], 16 * (RT // RING))
            for t in range(TILES):
                pool.indirect_dma_start(
                    rows[:, t, :], None, sorted_out,
                    bass.IndirectOffsetOnAxis(ap=place[:, t:t + 1].bitcast(U32), axis=0)).then_inc(m.back, 16)

        def experts_pool(pool, m):
            pool.wait_ge(m.ln.kept, m.stat_steps)
            pool.tensor_tensor(rstd[:], mean_var[:, :, 1], eps_tile[:], ALU.add).then_inc(m.ln.eps, 1)
            pool.wait_ge(m.ln.eps, 1)
            pool.tensor_tensor(rstd[:], rstd[:], neg_half[:], ALU.pow).then_inc(m.ln.rstd, 1)
            send_rows(pool, m)
            fetch_rows(pool, m)

        @block.gpsimd
        def _(pool):
            pool.memset(neg_half[:], -0.5).then_inc(const_made, 1)
            pool.memset(zeros[:], 0.0).then_inc(const_made, 1)
            pool.memset(ones_b[:], 1.0).then_inc(const_made, 1)
            pool.memset(v_aug[:], 1.0).then_inc(const_made, 1)
            pool.memset(eps_tile[:], LN_EPS).then_inc(const_made, 1)
            pool.wait_ge(const_made, 5)
            pool.affine_select(out=before_b[:], in_=ones_b[:], compare_op=ALU.is_gt, fill=0.0, base=0,
                               pattern=[[1, P]], channel_multiplier=-1).then_inc(const_made, 1)

            def spectrum_sums(k):
                wait(pool, c_inverse, k)
                pool.wait_ge(c_prod, 4 * k + 2)
                pool.tensor_tensor(spect_y[:, 0, :], prod[:, 0, :], prod[:, 1, :], ALU.subtract).then_inc(c_spect, 1)
                pool.wait_ge(c_prod, 4 * k + 4)
                pool.tensor_tensor(spect_y[:, 1, :], prod[:, 2, :], prod[:, 3, :], ALU.add).then_inc(c_spect, 1)

            def out_bias(k):
                pool.wait_ge(ln_c.normed, PAIR * (k + 1))
                here = residual[:, bass.ds(k * PAIR, PAIR), :]
                pool.tensor_tensor(here, here, b_out_all[:].rearrange("p (a d) -> p a d", a=1).to_broadcast(
                    [P, PAIR, D]), ALU.add).then_inc(c_bias, 1)

            pool.wait_ge(weights_loaded, 32)
            norm_rstd(pool, ln_c, 0)
            norm_rstd(pool, ln_c, 1)
            out_bias(0)
            with pool.Fori(0, PAIRS - 2) as k:
                spectrum_sums(k)
                norm_rstd(pool, ln_c, k + 2)
                out_bias(k + 1)
            spectrum_sums(PAIRS - 2)
            out_bias(PAIRS - 1)
            spectrum_sums(PAIRS - 1)
            if phases < 2:
                return
            experts_pool(pool, moe[0])
            if phases < 3:
                return

            def clear_future(b):
                for n in range(2 * AT):
                    t, g = n // 2, 2 + n % 2
                    pool.wait_ge(a_copied, 2 * AT * b + n + 1)
                    wait(pool, a_cleared, 2 * AT * b)
                    hold_gpsimd(pool, n)
                    s = scores[:, t, g * GROUPS:(g + 1) * GROUPS, :]
                    pool.affine_select(out=s, in_=s, compare_op=ALU.is_ge, fill=0.0, base=0,
                                       pattern=[[0, GROUPS], [1, P]], channel_multiplier=-1).then_inc(a_cleared, 1)

            norm_rstd(pool, ln_a, 0)
            with pool.Fori(0, B - 1) as b:
                norm_rstd(pool, ln_a, b + 1)
                clear_future(b)
            clear_future(B - 1)
            if phases < 4:
                return
            experts_pool(pool, moe[1])

        def mm(pe, out_, lhsT, rhs, start=True, stop=True, **kw):
            return pe.matmul(out_, lhsT, rhs, start=start, stop=stop, **kw)

        def experts_pe(pe, m):
            def turn(k):
                norm_turn(pe, m.ln, k, bank[0])

            def gate(k):
                pe.wait_ge(m.ln.copied, k + 1)
                for j in range(PAIR):
                    last = mm(pe, bank[1][:, bass.ds((k * PAIR + j) * E, E)], normed_t[:, j * P:(j + 1) * P],
                              gate_sb)
                last.then_inc(m.logits, 1)

            with pe.Fori(0, PAIRS) as k:
                turn(k)
                gate(k)

            pe.wait_ge(m.route, 7)
            all_chosen = chosen_b[:].rearrange("p t e -> p (t e)")
            mm(pe, bank[2][:, 0:TILES * E], before_b[:], all_chosen)
            mm(pe, bank[3][:, 0:TILES * E], ones_b[:], all_chosen).then_inc(m.counted, 1)

            def up(k):
                pe.wait_ge(m.kept, k + 1)
                wait(pe, m.silu, IB * k)
                wait(pe, m.act, IB * k)
                for i in range(IB):
                    mm(pe, bank[4 + i][:], shared_gate[:, i * P:(i + 1) * P], normed_all[:, bass.ds(k * PT, PT)])
                    mm(pe, bank[6 + i][:], shared_up[:, i * P:(i + 1) * P], normed_all[:, bass.ds(k * PT, PT)]
                       ).then_inc(m.up, 1)

            def down(k):
                pe.wait_ge(m.act, IB * (k + 1))
                wait(pe, m.added, k)
                for j in range(PAIR):
                    for i in range(IB):
                        last = mm(pe, bank[1][:, j * P:(j + 1) * P], act_sh[:, i, j * P:(j + 1) * P],
                                  shared_down[:, i, :], start=(i == 0), stop=(i == IB - 1))
                last.then_inc(m.down, 1)

            pe.wait_ge(m.route, 1)
            up(0)
            with pe.Fori(0, PAIRS - 1) as k:
                up(k + 1)
                down(k)
            down(PAIRS - 1)

            def row_turn(i, r):
                pe.wait_ge(m.row_in[r], 16 * (i + 1))
                wait(pe, m.row_copied, RING * i + r)
                pe.transpose(bank[0][:, 0:P], row_in[:, r, :], ident).then_inc(m.row_turned, 1)

            def expert_of(i, r):
                return pe.value_load(tile_expert[0:1, bass.ds(RING * i + r, 1)], min_val=0, max_val=E - 1)

            def expert_columns(e, at, n):
                return experts[:, bass.ds(e * WE + at, n)]

            def row_up(i, r):
                e = expert_of(i, r)
                pe.wait_ge(m.row_copied, RING * i + r + 1)
                wait(pe, m.row_silu, RING * i + r - 1)
                wait(pe, m.row_act, RING * i + r - 1)
                mm(pe, bank[2 + r % 2 * 2][:, 0:I], row_in_t[:, r, :], expert_columns(e, 0, I))
                mm(pe, bank[3 + r % 2 * 2][:, 0:I], row_in_t[:, r, :], expert_columns(e, I, I)
                   ).then_inc(m.row_up, 1)

            def act_turn(i, r):
                pe.wait_ge(m.row_act, RING * i + r + 1)
                wait(pe, m.act_copied, RING * i + r)
                for b in range(IB):
                    last = pe.transpose(bank[6][:, b * P:(b + 1) * P], row_act[:, r, b * P:(b + 1) * P], ident)
                last.then_inc(m.act_turned, 1)

            def row_down(i, r):
                e = expert_of(i, r)
                pe.wait_ge(m.act_copied, RING * i + r + 1)
                wait(pe, m.row_out, RING * i + r)
                for b in range(IB):
                    last = mm(pe, bank[7][:, 0:D], row_act_t[:, r, b, :], expert_columns(e, 2 * I + b * D, D),
                              start=(b == 0), stop=(b == IB - 1))
                last.then_inc(m.row_down, 1)

            pe.wait_ge(m.route, 8)
            pe.wait_ge(m.added, PAIRS)
            routed_steps(pe, (3, row_turn), (2, row_up), (1, act_turn), (0, row_down))

        @block.tensor
        def _(pe):
            pe.wait_ge(filter_loaded, 16 * len(filter_loads))
            mm(pe, bank[0][0:ORDER, :], f_w1_sb[:], positions_sb[:]).then_inc(flt_pe, 1)
            for n, w in enumerate((f_w2_sb, f_w3_sb)):
                pe.wait_ge(flt_act, n + 1)
                mm(pe, bank[0][0:ORDER, :], w, filter_h[:]).then_inc(flt_pe, 1)
            pe.wait_ge(flt_act, 3)
            for t in range(TAU):
                last = mm(pe, bank[1][:, t * D:(t + 1) * D], filter_h[:, t * P:(t + 1) * P], f_wout_sb)
            last.then_inc(flt_pe, 1)
            pe.wait_ge(flt, FLT_K)
            pe.wait_ge(tables_loaded[0], 16)
            pe.wait_ge(tables_loaded[1], 16)
            pe.wait_ge(weights_loaded, 32)
            for c in range(2):
                for f in range(FB):
                    at = (c * FB + f) * D
                    for t in range(TAU):
                        last = mm(pe, bank[2][:, at:at + D], dft[:, t, c, f * P:(f + 1) * P], filter_k[:, t, :],
                                  start=(t == 0), stop=(t == TAU - 1))
            last.then_inc(flt_pe, 1)

            def project(k):
                pe.wait_ge(ln_c.copied, k + 1)
                wait(pe, c_conv, 3 * k)
                for g in range(3):
                    last = mm(pe, bank[1 + g][:], w_in_sb[:, g * D:(g + 1) * D], normed_t[:])
                last.then_inc(c_proj, 1)

            def turn_value(k):
                pe.wait_ge(c_value, k + 1)
                pe.wait_ge(ln_c.copied, k + 1)
                for j in range(PAIR):
                    last = pe.transpose(bank[0][:, j * P:(j + 1) * P], value_c[:, j * P:(j + 1) * P], ident)
                last.then_inc(c_value_turned, 1)

            def forward(k):
                pe.wait_ge(c_value_copied, k + 1)
                wait(pe, c_prod, 4 * k)
                v = value_t[:].rearrange("p (b s) d -> p s b d", s=SB)
                for c in range(2):
                    for f in range(FB):
                        o = bank[4 + c][:, f * 2 * D:(f + 1) * 2 * D].rearrange("p (b d) -> p b d", b=2)
                        for s in range(SB):
                            last = mm(pe, o, dft[:, s, c, f * P:(f + 1) * P], v[:, s, :, :],
                                      start=(s == 0), stop=(s == SB - 1))
                    last.then_inc(c_forward, 1)

            def inverse(k):
                pe.wait_ge(c_spect, 2 * k + 2)
                wait(pe, c_gated, k)
                y = spect_y[:].rearrange("p c (f b d) -> p c f b d", f=FB, b=2)
                for b in range(2):
                    for c in range(2):
                        for f in range(FB):
                            last = mm(pe, bank[6][:, b * L:(b + 1) * L], y[:, c, f, b, :], inverse_dft[:, c, f, :],
                                      start=(c == 0 and f == 0), stop=(c == 1 and f == FB - 1))
                last.then_inc(c_inverse, 1)

            def project_out(k):
                pe.wait_ge(c_gated, k + 1)
                wait(pe, c_added, k)
                for j in range(PAIR):
                    last = mm(pe, bank[7][:, j * P:(j + 1) * P], gated[:, j * P:(j + 1) * P], w_out_sb)
                last.then_inc(c_out, 1)

            def conv_turn(k):
                wait(pe, c_value_copied, k)
                norm_turn(pe, ln_c, k, bank[0])

            pe.wait_ge(flt, FLT_SPECTRUM)
            conv_turn(0)
            project(0)
            turn_value(0)
            conv_turn(1)
            forward(0)
            project(1)
            inverse(0)
            with pe.Fori(1, PAIRS - 1) as k:
                turn_value(k)
                conv_turn(k + 1)
                forward(k)
                project_out(k - 1)
                project(k + 1)
                inverse(k)
            turn_value(PAIRS - 1)
            forward(PAIRS - 1)
            project_out(PAIRS - 2)
            inverse(PAIRS - 1)
            project_out(PAIRS - 1)
            if phases < 2:
                return
            pe.wait_ge(loaded_experts, 16 * len(expert_loads))
            pe.wait_ge(const_made, 5)
            pe.wait_ge(tables_loaded[2], 16)
            experts_pe(pe, moe[0])
            if phases < 3:
                return

            def att_project(b):
                pe.wait_ge(ln_a.copied, b + 1)
                wait(pe, a_relu, b)
                mm(pe, bank[1][:, 0:L], w_attn_sb[:, 0:D], normed_t[:, 0:L])
                mm(pe, bank[1][:, L:2 * L], w_attn_sb[:, D:2 * D], normed_t[:, 0:L]).then_inc(a_proj, 1)
                wait(pe, a_added, b)
                for t in range(AT):
                    last = mm(pe, bank[3][:, t * D:(t + 1) * D], normed_t[:, t * P:(t + 1) * P],
                              w_attn_sb[:, 2 * D:3 * D])
                last.then_inc(a_vproj, 1)

            def att_scores(b):
                for n in range(AT * GROUPS):
                    t, g = n // GROUPS, n % GROUPS
                    if n >= 3:
                        q = n - 3
                        at = b * AT * 2 + q // GROUPS * 2 + q % 2 + 1
                        pe.wait_ge(a_masked if q % GROUPS < 2 else a_copied, at)
                    else:
                        wait(pe, a_masked, b * AT * 2)
                        wait(pe, a_copied, b * AT * 2)
                    rows_g = slice(32 * g, 32 * g + 32)
                    mm(pe, bank[4 + n % 3][:].rearrange("p (h q) -> p h q", h=GROUPS),
                       qk[rows_g, L + t * P:L + (t + 1) * P], q_by_head[rows_g, :, t * P:(t + 1) * P]
                       ).then_inc(a_score, 1)

            def att_core(b):
                pe.wait_ge(a_qk, b + 1)
                pe.wait_ge(ln_a.copied, b + 1)
                pe.transpose(bank[0][:, 0:P], qk[:, L:L + P], ident).then_inc(a_k_turned, 1)
                pe.wait_ge(a_by_head, b + 1)
                att_scores(b)
                pe.wait_ge(a_k_tok, b + 1)
                pe.wait_ge(a_v, b + 1)
                mm(pe, bank[3][:, 2 * P:2 * P + HEADS * HV], k_tok[:],
                   v_aug[:, 0, :, :].rearrange("p h e -> p (h e)")).then_inc(a_state_mm, 1)

            def att_values(b):
                pe.wait_ge(a_masked, 2 * AT * (b + 1))
                pe.wait_ge(a_cleared, 2 * AT * (b + 1))
                pe.wait_ge(a_state, b + 1)
                wait(pe, a_y, b)
                W = HEADS * HV
                mm(pe, bank[7][:, W:2 * W], qk[:, P:2 * P], state[:], start=True, stop=False,
                   skip_group_check=True)
                for t in (1, 0):
                    for h in range(HEADS):
                        last = mm(pe, bank[7][:, t * W + h * HV:t * W + (h + 1) * HV], scores[:, t, h, :],
                                  v_aug[:, t, h, :], start=(t == 0), stop=True, skip_group_check=True)
                last.then_inc(a_y_mm, 1)

            def att_out(b):
                pe.wait_ge(a_y, b + 1)
                wait(pe, a_yt, b)
                for t in range(AT):
                    last = pe.transpose(bank[2][:, t * P:(t + 1) * P], att_y[:, t, :], ident)
                last.then_inc(a_y_turned, 1)
                pe.wait_ge(a_yt, b + 1)
                for t in range(AT):
                    last = mm(pe, bank[3][:, t * D:(t + 1) * D], att_yt[:, t * P:(t + 1) * P], w_proj_sb)
                last.then_inc(a_out, 1)

            def att_turn(b):
                wait(pe, a_k_tok, b)
                norm_turn(pe, ln_a, b, bank[0])

            att_turn(0)
            att_project(0)
            with pe.Fori(0, B - 1) as b:
                att_core(b)
                att_turn(b + 1)
                att_values(b)
                att_out(b)
                att_project(b + 1)
            att_core(B - 1)
            att_values(B - 1)
            att_out(B - 1)
            if phases < 4:
                return
            pe.wait_ge(a_added, B)
            experts_pe(pe, moe[1])

        def copy(act, out_, in_):
            return act.activation(out_, in_, ACT.Copy)

        def experts_act(act, m):
            with act.Fori(0, PAIRS) as k:
                act.wait_ge(m.ln.turned, k + 1)
                copy(act, normed_all[:, bass.ds(k * PT, PT)], bank[0][:]).then_inc(m.kept, 1)
                wait(act, m.logits, k)
                copy(act, normed_t[:], bank[0][:]).then_inc(m.ln.copied, 1)
            act.wait_ge(m.route, 2)
            act.activation(score[:], top[:], ACT.Sigmoid).then_inc(m.score, 1)

            with act.Fori(0, PAIRS) as k:
                for i in range(IB):
                    act.wait_ge(m.up, IB * k + i + 1)
                    wait(act, m.act, IB * k)
                    act.activation(silu_sh[:, i, :], bank[4 + i][:], ACT.Silu).then_inc(m.silu, 1)

            def row_copy(i, r):
                act.wait_ge(m.row_turned, RING * i + r + 1)
                wait(act, m.row_up, RING * i + r - RING + 1)
                copy(act, row_in_t[:, r, :], bank[0][:, 0:P]).then_inc(m.row_copied, 1)

            def row_silu_(i, r):
                act.wait_ge(m.row_up, RING * i + r + 1)
                wait(act, m.row_act, RING * i + r - RING + 1)
                act.activation(row_silu[:, r, :], bank[2 + r % 2 * 2][:, 0:I], ACT.Silu).then_inc(m.row_silu, 1)

            def act_copy(i, r):
                act.wait_ge(m.act_turned, RING * i + r + 1)
                wait(act, m.row_down, RING * i + r - RING + 1)
                copy(act, row_act_t[:, r, :, :].rearrange("p b t -> p (b t)"), bank[6][:, 0:I]
                     ).then_inc(m.act_copied, 1)

            routed_steps(act, (3, row_copy), (2, row_silu_), (1, act_copy))

        @block.scalar
        def _(act):
            for dst, src in filter_loads:
                act.dma_start(dst, src).then_inc(filter_loaded, 16)
            act.dma_start(tables_sb[:, 0:table_parts[1]], tables[:, 0:table_parts[1]]).then_inc(tables_loaded[0], 16)
            act.dma_start(weights_sb[:], weights).then_inc(weights_loaded, 16)
            act.dma_start(b_out_all[:], b_out.rearrange("(a d) -> a d", a=1).to_broadcast([P, D])
                          ).then_inc(weights_loaded, 16)
            a, b = table_parts[2:4]
            act.dma_start(tables_sb[:, a:b], tables[:, a:b]).then_inc(tables_loaded[2], 16)
            for n in range(3):
                act.wait_ge(flt, FLT_LAYER * (n + 1))
                act.activation(filter_h[:], filter_r[:], ACT.Sin).then_inc(flt_act, 1)

            def copy_normed(k):
                act.wait_ge(ln_c.turned, k + 1)
                wait(act, c_proj, k)
                copy(act, normed_t[:], bank[0][:]).then_inc(ln_c.copied, 1)

            def copy_value(k):
                act.wait_ge(c_value_turned, k + 1)
                wait(act, c_forward, 2 * k)
                copy(act, value_t[:].rearrange("p j d -> p (j d)"), bank[0][:]).then_inc(c_value_copied, 1)

            def tap2(k):
                act.wait_ge(c_proj, k + 1)
                for g in range(3):
                    if g:
                        wait(act, c_value, k)
                        dst = conv_xv[:, g - 1, :]
                    else:
                        dst = gates[:, bass.ds(k * PT, PT)]
                    act.activation(dst, bank[1 + g][:], ACT.Identity, bias=conv_bias[:, g:g + 1],
                                   scale=taps[:, g, 2:3]).then_inc(c_tap2, 1)

            act.wait_ge(edges_made, 4)
            copy_normed(0)
            tap2(0)
            with act.Fori(0, PAIRS - 1) as k:
                copy_value(k)
                copy_normed(k + 1)
                tap2(k + 1)
            copy_value(PAIRS - 1)
            if phases < 2:
                return
            experts_act(act, moe[0])
            if phases < 3:
                return

            def att_normed(b):
                act.wait_ge(ln_a.turned, b + 1)
                wait(act, a_vproj, b)
                copy(act, normed_t[:, 0:L], bank[0][:, 0:L]).then_inc(ln_a.copied, 1)

            def att_features(b):
                act.wait_ge(a_proj, b + 1)
                wait(act, a_qk, b)
                act.activation(att_exp[:], bank[1][:], ACT.Exp).then_inc(a_exp, 1)
                act.activation(att_relu[:], bank[1][:], ACT.Relu).then_inc(a_relu, 1)

            def att_v(b):
                act.wait_ge(a_vproj, b + 1)
                wait(act, a_y_mm, b)
                for t in range(AT):
                    last = copy(act, v_aug[:, t, :, 0:HD], bank[3][:, t * D:(t + 1) * D].rearrange(
                        "p (h e) -> p h e", h=HEADS))
                last.then_inc(a_v, 1)

            def att_by_head(b):
                act.wait_ge(a_qk, b + 1)
                wait(act, a_score, AT * GROUPS * b)
                for g in range(GROUPS):
                    last = act.activation(q_by_head[:, g, :], qk[:, 0:L], ACT.Copy, scale=head_of_group[:, g:g + 1])
                last.then_inc(a_by_head, 1)

            def att_k(b):
                act.wait_ge(a_k_turned, b + 1)
                wait(act, a_state_mm, b)
                copy(act, k_tok[:], bank[0][:, 0:P]).then_inc(a_k_tok, 1)

            def att_scores_copy(b):
                for n in range(2 * AT):
                    t, g = n // 2, 2 + n % 2
                    act.wait_ge(a_score, AT * GROUPS * b + t * GROUPS + g + 1)
                    wait(act, a_y_mm, b)
                    copy(act, scores[:, t, g * GROUPS:(g + 1) * GROUPS, :].rearrange("p h q -> p (h q)"),
                         bank[4 + (t * GROUPS + g) % 3][:]).then_inc(a_copied, 1)

            def att_y_copy(b):
                act.wait_ge(a_y_turned, b + 1)
                wait(act, a_out, b)
                copy(act, att_yt[:], bank[2][:, 0:L]).then_inc(a_yt, 1)

            att_normed(0)
            att_features(0)
            att_v(0)
            with act.Fori(0, B - 1) as b:
                att_k(b)
                att_by_head(b)
                att_scores_copy(b)
                att_normed(b + 1)
                att_y_copy(b)
                att_features(b + 1)
                att_v(b + 1)
            att_k(B - 1)
            att_by_head(B - 1)
            att_scores_copy(B - 1)
            att_y_copy(B - 1)
            if phases < 4:
                return
            experts_act(act, moe[1])

        def experts_dve(dve, m):
            dve.wait_ge(m.ln.rstd, 1)
            with dve.Fori(0, PAIRS) as k:
                norm_apply(dve, m.ln, k, kept=True)

            def bc(ap, axis, n):
                v = ap.unsqueeze(axis)
                shape = list(v.shape)
                shape[axis] = n
                return v.to_broadcast(shape)

            step = [0]

            def then(ins):
                step[0] += 1
                ins.then_inc(m.route, 1)
                dve.wait_ge(m.route, step[0])

            dve.wait_ge(m.logits, PAIRS)
            then(dve.tensor_copy(logits[:].rearrange("p t e -> p (t e)"), bank[1][:, 0:TILES * E]))
            then(dve.tensor_reduce(top[:], logits[:], AX.X, ALU.max))
            then(dve.tensor_tensor(r_a[:], logits[:], bc(top[:], 2, E), ALU.is_equal))
            then(dve.tensor_tensor(r_b[:], r_a[:], bc(tie_rank, 1, TILES), ALU.mult))
            then(dve.tensor_reduce(best[:], r_b[:], AX.X, ALU.max))
            then(dve.tensor_tensor(chosen[:], r_b[:], bc(best[:], 2, E), ALU.is_equal))
            then(dve.tensor_copy(chosen_b[:], chosen[:]))
            return step, then, bc

        def route_rest(dve, m, step, then, bc):
            dve.wait_ge(m.counted, 1)
            tmp = sem_steps
            def t2(ins):
                tmp[1] += 1
                ins.then_inc(tmp[0], 1)
                dve.wait_ge(tmp[0], tmp[1])
            t2(dve.tensor_copy(counts[:], bank[3][:, 0:TILES * E].rearrange("p (t e) -> p e t", e=E)))
            t2(dve.tensor_tensor_scan(running[:].rearrange("p e t -> p (e t)"), counts[:].rearrange("p e t -> p (e t)"),
                                      zeros[:], 0.0, ALU.add, ALU.add))
            t2(dve.memset(ends[:], 0.0))
            t2(dve.tensor_copy(ends[:, 1:E + 1], running[:, :, TILES - 1]))
            t2(dve.tensor_tensor(n_tok[:], ends[:, 1:E + 1], ends[:, 0:E], ALU.subtract))
            t2(dve.tensor_tensor(cmp_tiles[:], bc(n_tok[:], 2, TILES), bc(tile_starts, 1, E), ALU.is_gt))
            t2(dve.tensor_reduce(n_tiles[:], cmp_tiles[:], AX.X, ALU.add))
            t2(dve.tensor_tensor_scan(tile_ends[:], n_tiles[:], zeros[:, 0:E], 0.0, ALU.add, ALU.add))
            t2(dve.tensor_tensor(start_at[:], tile_ends[:], n_tiles[:], ALU.subtract))
            t2(dve.scalar_tensor_tensor(start_at[:], start_at[:], float(P), ends[:, 0:E], ALU.mult, ALU.subtract))
            t2(dve.tensor_tensor(running[:], running[:], counts[:], ALU.subtract))
            t2(dve.tensor_tensor(running[:], running[:], bc(start_at[:], 2, TILES), ALU.add))
            t2(dve.tensor_tensor(r_b[:], bank[2][:, 0:TILES * E].rearrange("p (t e) -> p t e", e=E),
                                 running[:].rearrange("p e t -> p t e"), ALU.add))
            t2(dve.tensor_tensor(r_b[:], r_b[:], chosen[:], ALU.mult))
            t2(dve.tensor_reduce(place_f[:], r_b[:], AX.X, ALU.add))
            t2(dve.tensor_copy(place[:], place_f[:]))
            t2(dve.tensor_tensor(cmp_e[:], bc(tile_ends[:, 0:E - 1], 1, RT), bc(tile_numbers, 2, E - 1), ALU.is_le))
            t2(dve.tensor_reduce(tile_expert_f[:], cmp_e[:], AX.X, ALU.add))
            then(dve.tensor_copy(tile_expert[:], tile_expert_f[:]))
            dve.wait_ge(m.score, 1)
            t2(dve.tensor_tensor(best[:], rstd[:], score[:], ALU.mult))
            if m is moe[0]:
                dve.wait_ge(zero_rows_stored, 16)
            with dve.Fori(0, PAIRS) as k:
                for j in range(PAIR):
                    t = bass.ds(k * PAIR + j, 1)
                    dve.tensor_scalar(rows[:, t, :], residual[:, t, :], mean_var[:, t, 0], best[:, t],
                                      ALU.subtract, ALU.mult).then_inc(m.rows, 1)
            dve.wait_ge(m.rows, TILES)

        def experts_main(dve, m):
            def gate_up(k):
                for i in range(IB):
                    dve.wait_ge(m.silu, IB * k + i + 1)
                    wait(dve, m.down, k)
                    dve.tensor_tensor(act_sh[:, i, :], silu_sh[:, i, :], bank[6 + i][:], ALU.mult).then_inc(m.act, 1)

            def add_shared(k):
                dve.wait_ge(m.down, k + 1)
                here = residual[:, bass.ds(k * PAIR, PAIR), :]
                dve.tensor_tensor(here, here, bank[1][:].rearrange("p (j d) -> p j d", j=PAIR), ALU.add
                                  ).then_inc(m.added, 1)

            gate_up(0)
            with dve.Fori(0, PAIRS - 1) as k:
                add_shared(k)
                gate_up(k + 1)
            add_shared(PAIRS - 1)

            def row_gate_up(i, r):
                dve.wait_ge(m.row_silu, RING * i + r + 1)
                wait(dve, m.act_turned, RING * i + r - RING + 1)
                dve.tensor_tensor(row_act[:, r, :], row_silu[:, r, :], bank[3 + r % 2 * 2][:, 0:I], ALU.mult).then_inc(m.row_act, 1)

            def row_result(i, r):
                dve.wait_ge(m.row_down, RING * i + r + 1)
                wait(dve, m.row_stored[r], 16 * i)
                dve.tensor_copy(row_out[:, r, :], bank[7][:, 0:D]).then_inc(m.row_out, 1)

            routed_steps(dve, (2, row_gate_up), (0, row_result))

        def add_routed(dve, m, k, n):
            dve.wait_ge(m.back, 16 * TILES)
            here, got = (a[:, bass.ds(k * n, n), :] for a in (residual, rows))
            dve.tensor_tensor(here, here, got, ALU.add).then_inc(m.summed, 1)

        sem_steps = [sem("router_steps"), 0]

        @block.vector
        def _(dve):
            dve.wait_ge(x_loaded[0], 16)
            norm_stats(dve, ln_c, 0)
            norm_apply(dve, ln_c, 0)
            dve.wait_ge(x_loaded[1], 16)
            norm_stats(dve, ln_c, 1)
            dve.wait_ge(weights_loaded, 32)
            es = [0]

            def edge_step(ins):
                es[0] += 1
                ins.then_inc(edges_made, 1)
                dve.wait_ge(edges_made, es[0])

            edge_step(dve.tensor_tensor(conv_edge[:, :, 0], taps[:, :, 0], taps[:, :, 1], ALU.add))
            edge_step(dve.tensor_tensor(conv_bias[:], conv_edge[:, :, 0], taps[:, :, 2], ALU.add))
            edge_step(dve.tensor_tensor(conv_bias[:], conv_bias[:], b_in_sb, ALU.mult))
            edge_step(dve.tensor_tensor(conv_bias[:], conv_bias[:], sf_b_sb, ALU.add))
            edge_step(dve.tensor_copy(conv_edge[:, :, 1], taps[:, :, 0]))
            edge_step(dve.tensor_tensor(edge_tmp[:], conv_edge[:], b_in_sb.unsqueeze(2).to_broadcast([P, 3, 2]),
                                        ALU.mult))
            edge_step(dve.tensor_scalar(conv_edge[:], edge_tmp[:], -1.0, None, ALU.mult))

            fs = [0]

            def flt_step(ins):
                fs[0] += 1
                ins.then_inc(flt, 1)
                dve.wait_ge(flt, fs[0])

            for n in range(3):
                dve.wait_ge(flt_pe, n + 1)
                flt_step(dve.tensor_scalar(filter_a[:], bank[0][0:ORDER, :], f_vec[:, 2 * n:2 * n + 1],
                                           f_vec[:, 2 * n + 1:2 * n + 2], ALU.add, ALU.mult))
                flt_step(dve.tensor_scalar(filter_r[:], filter_a[:], float(1 / (2 * np.pi)), ROUND, ALU.mult, ALU.add))
                flt_step(dve.tensor_scalar(filter_r[:], filter_r[:], ROUND, None, ALU.subtract))
                flt_step(dve.scalar_tensor_tensor(filter_a[:], filter_r[:], -TWO_PI_HI, filter_a[:], ALU.mult, ALU.add))
                flt_step(dve.scalar_tensor_tensor(filter_a[:], filter_r[:], -float(TWO_PI_LO), filter_a[:],
                                                  ALU.mult, ALU.add))
                flt_step(dve.tensor_scalar(filter_r[:], filter_a[:], PI_BELOW, -PI_BELOW, ALU.min, ALU.max))
                assert fs[0] == FLT_LAYER * (n + 1)
            dve.wait_ge(flt_pe, 4)
            dve.wait_ge(tables_loaded[0], 16)
            flt_step(dve.tensor_tensor(filter_k[:], bank[1][:].rearrange("p (t d) -> p t d", t=TAU), decay, ALU.mult))
            flt_step(dve.tensor_tensor(filter_k[0:1, 0, :], filter_k[0:1, 0, :], filt_bias_row[:], ALU.add))
            assert fs[0] == FLT_K
            dve.wait_ge(flt_pe, 5)
            half = FB * D
            for part, src in ((0, 0), (1, 1), (2, 0)):
                flt_step(dve.tensor_copy(spectrum[:, part, :, :].rearrange("p f d -> p (f d)"),
                                         bank[2][:, src * half:(src + 1) * half]))
            flt_step(dve.tensor_copy(spectrum[0:1, 2, 0, :], bank[2][0:1, half:half + D]))
            flt_step(dve.memset(spectrum[0:1, 1, 0, :], 0.0))
            assert fs[0] == FLT_SPECTRUM

            def short_conv(k):
                def seqs(ap):
                    return ap.rearrange("p (b t) -> p b t", b=2)

                for g in range(3):
                    dve.wait_ge(c_tap2, 3 * k + g + 1)
                    dst = seqs(conv_xv[:, g - 1, :] if g else gates[:, bass.ds(k * PT, PT)])
                    src = seqs(bank[1 + g][:])
                    dve.tensor_tensor(dst[:, :, 0:2], dst[:, :, 0:2],
                                      conv_edge[:, g, :].unsqueeze(1).to_broadcast([P, 2, 2]), ALU.add
                                      ).then_inc(c_edge, 1)
                    dve.wait_ge(c_edge, 3 * k + g + 1)
                    dve.scalar_tensor_tensor(dst[:, :, 1:L], src[:, :, 0:L - 1], taps[:, g, 1:2], dst[:, :, 1:L],
                                             ALU.mult, ALU.add).then_inc(c_tap1, 1)
                    dve.wait_ge(c_tap1, 3 * k + g + 1)
                    dve.scalar_tensor_tensor(dst[:, :, 2:L], src[:, :, 0:L - 2], taps[:, g, 0:1], dst[:, :, 2:L],
                                             ALU.mult, ALU.add).then_inc(c_conv, 1)
                dve.wait_ge(c_conv, 3 * k + 3)
                wait(dve, c_value_turned, k)
                dve.tensor_tensor(value_c[:], conv_xv[:, 0, :], conv_xv[:, 1, :], ALU.mult).then_inc(c_value, 1)

            def products(k):
                wait(dve, c_spect, 2 * k)
                for n, (c, part) in enumerate(((0, 0), (1, 1), (1, 2), (0, 1))):
                    dve.wait_ge(c_forward, 2 * k + c + 1)
                    dve.tensor_tensor(
                        prod[:, n, :].rearrange("p (f b d) -> p f b d", f=FB, b=2),
                        bank[4 + c][:].rearrange("p (f b d) -> p f b d", f=FB, b=2),
                        spectrum[:, part, :, :].unsqueeze(2).to_broadcast([P, FB, 2, D]), ALU.mult).then_inc(c_prod, 1)

            def gate(k):
                dve.wait_ge(c_inverse, k + 1)
                wait(dve, c_out, k)
                dve.tensor_tensor(gated[:], bank[6][:], gates[:, bass.ds(k * PT, PT)], ALU.mult).then_inc(c_gated, 1)

            def add_conv(k):
                dve.wait_ge(c_out, k + 1)
                dve.wait_ge(c_bias, k + 1)
                here = residual[:, bass.ds(k * PAIR, PAIR), :]
                dve.tensor_tensor(here, here, bank[7][:].rearrange("p (j d) -> p j d", j=PAIR), ALU.add
                                  ).then_inc(c_added, 1)

            def conv_stats(k):
                keep_stats(dve, moe[0].ln, PAIR, k, c_added)

            short_conv(0)
            norm_apply(dve, ln_c, 1)
            products(0)
            short_conv(1)
            gate(0)
            dve.wait_ge(x_loaded[2], 16)
            norm_stats(dve, ln_c, 2)
            with dve.Fori(1, PAIRS - 2) as k:
                norm_apply(dve, ln_c, k + 1)
                products(k)
                add_conv(k - 1)
                conv_stats(k - 1)
                short_conv(k + 1)
                gate(k)
                norm_stats(dve, ln_c, k + 2)
            norm_apply(dve, ln_c, PAIRS - 1)
            products(PAIRS - 2)
            add_conv(PAIRS - 3)
            conv_stats(PAIRS - 3)
            short_conv(PAIRS - 1)
            gate(PAIRS - 2)
            products(PAIRS - 1)
            add_conv(PAIRS - 2)
            gate(PAIRS - 1)
            conv_stats(PAIRS - 2)
            add_conv(PAIRS - 1)
            conv_stats(PAIRS - 1)
            if phases < 2:
                return
            dve.wait_ge(c_added, PAIRS)
            dve.wait_ge(tables_loaded[2], 16)
            dve.wait_ge(const_made, 6)

            def experts_vector(m):
                route_rest(dve, m, *experts_dve(dve, m))
                experts_main(dve, m)
                dve.wait_ge(m.added, PAIRS)

            experts_vector(moe[0])
            if phases < 3:
                with dve.Fori(0, PAIRS) as k:
                    add_routed(dve, moe[0], k, PAIR)
                return

            def att_in(b):
                add_routed(dve, moe[0], b, AT)
                norm_stats(dve, ln_a, b, moe[0].summed)

            def att_feature_sum(b):
                dve.wait_ge(a_relu, b + 1)
                wait(dve, a_y_mm, b)
                dve.scalar_tensor_tensor(qk[:], att_exp[:], 1.0, att_relu[:], ALU.min, ALU.add).then_inc(a_qk, 1)

            def att_mask(b):
                for n in range(2 * AT):
                    t, g = n // 2, n % 2
                    dve.wait_ge(a_score, AT * GROUPS * b + t * GROUPS + g + 1)
                    wait(dve, a_y_mm, b)
                    dve.tensor_tensor(scores[:, t, g * GROUPS:(g + 1) * GROUPS, :],
                                      bank[4 + (t * GROUPS + g) % 3][:].rearrange("p (h q) -> p h q", h=GROUPS),
                                      causal.unsqueeze(1).to_broadcast([P, GROUPS, P]), ALU.mult
                                      ).then_inc(a_masked, 1)

            def att_state(b):
                dve.wait_ge(a_state_mm, b + 1)
                dve.tensor_tensor(state[:], bank[3][:, 2 * P:2 * P + HEADS * HV], own_head, ALU.mult
                                  ).then_inc(a_state, 1)

            def att_divide(b):
                dve.wait_ge(a_y_mm, b + 1)
                y = bank[7][:, 0:AT * HEADS * HV].rearrange("p (h e) -> p h e", e=HV)
                wait(dve, a_y, b)
                dve.tensor_scalar(den[:], y[:, :, HD], ATT_EPS, None, ALU.add).then_inc(a_den, 1)
                dve.wait_ge(a_den, 2 * b + 1)
                dve.reciprocal(den[:], den[:]).then_inc(a_den, 1)
                dve.wait_ge(a_den, 2 * b + 2)
                wait(dve, a_y_turned, b)
                dve.tensor_tensor(att_y[:].rearrange("p t (h e) -> p (t h) e", e=HD), y[:, :, 0:HD],
                                  den[:].unsqueeze(2).to_broadcast([P, AT * HEADS, HD]), ALU.mult).then_inc(a_y, 1)

            def att_add(b):
                dve.wait_ge(a_out, b + 1)
                here = residual[:, bass.ds(b * AT, AT), :]
                dve.tensor_tensor(here, here, bank[3][:, 0:AT * D].rearrange("p (t d) -> p t d", t=AT), ALU.add
                                  ).then_inc(a_added, 1)

            def att_stats(b):
                keep_stats(dve, moe[1].ln, AT, b, a_added)

            att_in(0)
            norm_apply(dve, ln_a, 0)
            att_in(1)
            with dve.Fori(0, B - 2) as b:
                att_feature_sum(b)
                norm_apply(dve, ln_a, b + 1)
                att_mask(b)
                att_state(b)
                att_divide(b)
                att_in(b + 2)
                att_add(b)
                att_stats(b)
            att_feature_sum(B - 2)
            norm_apply(dve, ln_a, B - 1)
            for b in (B - 2, B - 1):
                if b == B - 1:
                    att_feature_sum(b)
                att_mask(b)
                att_state(b)
                att_divide(b)
                att_add(b)
                att_stats(b)
            if phases < 4:
                return
            dve.wait_ge(a_added, B)
            experts_vector(moe[1])
            with dve.Fori(0, PAIRS) as k:
                add_routed(dve, moe[1], k, PAIR)


FLT_LAYER = 6
FLT_K = 3 * FLT_LAYER + 2
FLT_SPECTRUM = FLT_K + 5


def kernel(L0_attn_a_u, L0_attn_a_w_in, L0_attn_a_b_in, L0_attn_a_sf_w, L0_attn_a_sf_b, L0_attn_a_f_w1,
           L0_attn_a_f_b1, L0_attn_a_freq1, L0_attn_a_f_w2, L0_attn_a_f_b2, L0_attn_a_freq2, L0_attn_a_f_w3,
           L0_attn_a_f_b3, L0_attn_a_freq3, L0_attn_a_f_wout, L0_attn_a_filt_bias, L0_attn_a_w_out,
           L0_attn_a_b_out, L0_attn_b_w_attn, L0_attn_b_w_proj, L0_ffn_gate_w, L0_ffn_sh_gate, L0_ffn_sh_up,
           L0_ffn_sh_down, L0_ffn_rt_gate, L0_ffn_rt_up, L0_ffn_rt_down):
    import concourse.bacc as bacc
    from concourse.bass_utils import run_bass_kernel_spmd

    def thirds(a):
        return np.asarray(a).reshape(3, P, -1).transpose(1, 0, 2).reshape(P, -1)

    by_name = {
        "w_in": L0_attn_a_w_in, "taps": thirds(L0_attn_a_sf_w), "b_in": thirds(L0_attn_a_b_in),
        "sf_b": thirds(L0_attn_a_sf_b), "w_out": L0_attn_a_w_out, "gate_w": L0_ffn_gate_w,
        "sh_gate": L0_ffn_sh_gate, "sh_up": L0_ffn_sh_up,
        "sh_down": np.asarray(L0_ffn_sh_down).reshape(IB, P, D).transpose(1, 0, 2).reshape(P, IB * D),
        "w_attn": L0_attn_b_w_attn, "w_proj": L0_attn_b_w_proj}
    vectors = np.stack([np.asarray(v) for v in (L0_attn_a_f_b1, L0_attn_a_freq1, L0_attn_a_f_b2,
                                                L0_attn_a_freq2, L0_attn_a_f_b3, L0_attn_a_freq3)], 1)
    tables, positions = shape_constants()
    arrays = {
        "x": L0_attn_a_u,
        "weights": np.concatenate([np.asarray(by_name[name]) for name in WEIGHTS], 1),
        "filter_weights": np.concatenate([np.asarray(L0_attn_a_f_w2), np.asarray(L0_attn_a_f_w3),
                                          np.asarray(L0_attn_a_f_wout), vectors], 1),
        "f_w1": L0_attn_a_f_w1, "filt_bias": L0_attn_a_filt_bias, "b_out": L0_attn_a_b_out,
        "rt_gate": L0_ffn_rt_gate, "rt_up": L0_ffn_rt_up, "rt_down": L0_ffn_rt_down,
        "tables": tables, "positions": positions}
    arrays = {name: np.ascontiguousarray(a) for name, a in arrays.items()}

    nc = bacc.Bacc("TRN2", target_bir_lowering=False, num_devices=1)
    args = [nc.dram_tensor(name, a.shape, mybir.dt.from_np(a.dtype), kind="ExternalInput").ap()
            for name, a in arrays.items()]
    out = nc.dram_tensor("out", (B, L, D), F32, kind="ExternalOutput").ap()
    hybrid_block(nc, *args, out)
    return run_bass_kernel_spmd(nc, [arrays], core_ids=[0]).results[0]["out"]
```

```python
from contextlib import ExitStack

import numpy as np

import concourse.bass as bass
from concourse import mybir

F32 = mybir.dt.float32
BF16 = mybir.dt.bfloat16
I32 = mybir.dt.int32
U32 = mybir.dt.uint32
ALU = mybir.AluOpType
ACT = mybir.ActivationFunctionType
AX = mybir.AxisListType

P = 128
B, L, D = 16, 256, 128
TILES = B * L // P
PAIR = 4
PAIRS = TILES // PAIR
PT = PAIR * P
NF = 512
TAU = NF // P
SB = L // P
FB = NF // 2 // P
ORDER = 64
E = 8
I = 256
IB = I // P
WE = 2 * I + IB * D
RING = 4
RT = -(-(TILES + E - 1) // RING) * RING
HEADS, HD = 16, 8
HV = HD + 1
HC = 32
GROUPS = 4
LN_EPS = 1e-5
ATT_EPS = 1e-6
ROUND = 1.5 * 2.0 ** 23
TWO_PI_HI = 6.28125
TWO_PI_LO = 2 * np.pi - TWO_PI_HI
PI_BELOW = 3.1415925


def packed(columns):
    at, where = 0, {}
    for name, n in columns:
        where[name] = (at, at + n)
        at += n
    return where, at


TABLES, TABLES_N = packed([
    ("identity", P), ("decay", TAU * D), ("dft", TAU * NF), ("inverse_dft", 2 * FB * L),
    ("causal", P), ("own_head", HEADS * HV), ("head_of_half", HEADS // 2), ("tie_rank", E),
    ("tile_starts", TILES), ("tile_numbers", RT)])
WEIGHTS, WEIGHTS_N = packed([
    ("w_in", 3 * D), ("taps", 9), ("b_in", 3), ("sf_b", 3), ("w_out", D), ("gate_w", E),
    ("sh_gate", I), ("sh_up", I), ("sh_down", IB * D), ("w_attn", 3 * D), ("w_proj", D)])
FILTER, FILTER_N = packed([("f_w2", ORDER), ("f_w3", ORDER), ("f_wout", D), ("f_vectors", 6)])


def shape_constants():
    c = {}
    t = np.linspace(0.0, 1.0, NF)
    w = 2 * np.pi * np.arange(NF) / NF
    positions = np.stack([t, np.cos(1e-4 * w), -np.sin(1e-4 * w)])
    rates = np.abs(np.linspace(np.log(0.01) / 1.5, np.log(0.01) / 0.3, D))
    decay = np.exp(-t[:, None] * rates[None]) + 0.05
    c["decay"] = decay.reshape(TAU, P, D).transpose(1, 0, 2)
    tau, f = np.arange(NF)[:, None], np.arange(NF // 2)[None]
    cos, sin = np.cos(2 * np.pi * tau * f / NF), -np.sin(2 * np.pi * tau * f / NF)
    sin[:, 0] = (-1.0) ** np.arange(NF)
    dft = np.stack([cos, sin], 1)
    c["dft"] = dft.reshape(TAU, P, 2, NF // 2).transpose(1, 0, 2, 3)
    weight = np.where(np.arange(NF // 2) == 0, 1.0, 2.0) / NF
    inv = (dft[:L] * weight).transpose(1, 2, 0)
    c["inverse_dft"] = inv.reshape(2, FB, P, L).transpose(2, 0, 1, 3)
    c["identity"] = np.eye(P)
    row = np.arange(P)[:, None]
    c["head_of_half"] = (row // HD % (HEADS // 2) == np.arange(HEADS // 2)[None]) * 1.0
    c["own_head"] = np.repeat(row // HD == np.arange(HEADS)[None], HV, 1) * 1.0
    c["causal"] = (np.arange(P)[None] >= row) * 1.0
    c["tie_rank"] = np.tile(E - np.arange(E), (P, 1)) * 1.0
    c["tile_starts"] = np.tile(P * np.arange(TILES), (P, 1)) * 1.0
    c["tile_numbers"] = np.tile(np.arange(RT), (P, 1)) * 1.0
    tables = np.concatenate([c[name].reshape(P, -1) for name in TABLES], 1)
    return np.ascontiguousarray(tables, np.float32), np.ascontiguousarray(positions, np.float32)


def wait(eng, sem, value):
    if not isinstance(value, int) or value > 0:
        eng.wait_ge(sem, value)


def hybrid_block(nc, x, weights, filter_weights, f_w1, filt_bias, b_out, rt_gate, rt_up, rt_down,
                 tables, positions, out, phases=4):
    with ExitStack() as ctx:
        def sb(name, shape, dt=F32):
            return ctx.enter_context(nc.sbuf_tensor(name, shape, dt))

        def sem(name):
            return ctx.enter_context(nc.semaphore(name))

        bank = [ctx.enter_context(nc.psum_tensor(f"bank{i}", [P, 512], F32)) for i in range(8)]
        sorted_rows = nc.dram_tensor("sorted_rows", [RT * P, D], F32, kind="Internal").ap()
        sorted_out = nc.dram_tensor("sorted_out", [RT * P, D], F32, kind="Internal").ap()

        residual = sb("residual", [P, TILES, D])
        tables_sb = sb("tables_sb", [P, TABLES_N])
        weights_sb = sb("weights_sb", [P, WEIGHTS_N])
        filter_sb = sb("filter_sb", [ORDER, FILTER_N])

        def table(name, pattern=None, **sizes):
            v = tables_sb[:, TABLES[name][0]:TABLES[name][1]]
            return v.rearrange(pattern, **sizes) if pattern else v

        def weight(name, pattern=None, **sizes):
            v = weights_sb[:, WEIGHTS[name][0]:WEIGHTS[name][1]]
            return v.rearrange(pattern, **sizes) if pattern else v

        ident = table("identity")
        decay = table("decay", "p (t d) -> p t d", t=TAU)
        dft = table("dft", "p (t c f) -> p t c f", t=TAU, c=2)
        inverse_dft = table("inverse_dft", "p (c f t) -> p c f t", c=2, f=FB)
        head_of_half, own_head, causal = table("head_of_half"), table("own_head"), table("causal")
        tie_rank, tile_starts, tile_numbers = table("tie_rank"), table("tile_starts"), table("tile_numbers")
        w_in_sb, w_out_sb, gate_sb = weight("w_in"), weight("w_out"), weight("gate_w")
        w_attn_sb, w_proj_sb = weight("w_attn"), weight("w_proj")
        taps = weight("taps", "p (g k) -> p g k", g=3)
        b_in_sb, sf_b_sb = weight("b_in"), weight("sf_b")
        shared_gate, shared_up = weight("sh_gate"), weight("sh_up")
        shared_down = weight("sh_down", "p (i d) -> p i d", i=IB)
        f_w2_sb, f_w3_sb, f_wout_sb, f_vec = (filter_sb[:, a:b] for a, b in FILTER.values())
        positions_sb = sb("positions_sb", [3, NF])
        f_w1_sb = sb("f_w1_sb", [3, ORDER])
        filt_bias_row = sb("filt_bias_row", [1, D])
        b_out_all = sb("b_out_all", [P, D])
        experts = sb("experts", [P, E * WE])
        experts_v = experts[:].rearrange("p (e c) -> p e c", e=E)

        stats = sb("stats", [P, PAIR, 6])
        step_stats = sb("step_stats", [P, PAIR, 2])
        step_rstd = sb("step_rstd", [P, PAIR])
        mean_var = sb("mean_var", [P, TILES, 2])
        rstd = sb("rstd", [P, TILES])
        held = sb("held", [P, 8])
        step_kept = sb("step_kept", [P, PAIR, 2])
        eps_tile = sb("eps_tile", [P, TILES])
        neg_half = sb("neg_half", [P, TILES])
        normed = sb("normed", [P, PAIR, D])
        normed_t = sb("normed_t", [P, PT])

        rows = sb("rows", [P, TILES, D])
        wide = sb("wide", [P, TILES * D])

        x_loaded = [sem(f"x_loaded{n}") for n in range(3)]
        filter_loaded = sem("filter_loaded")
        tables_loaded = [sem(f"tables_loaded{n}") for n in range(3)]
        weights_loaded = sem("weights_loaded")
        loaded_experts = sem("loaded_experts")
        const_made = sem("const_made")
        zero_rows_stored = sem("zero_rows_stored")
        stored = sem("stored")

        class Norm:

            def __init__(self, name, n):
                self.n = n
                self.bn = sem(f"{name}_bn")
                self.aggr = sem(f"{name}_aggr")
                self.kept = sem(f"{name}_kept")
                self.eps = sem(f"{name}_eps")
                self.rstd = sem(f"{name}_rstd")
                self.normed = sem(f"{name}_normed")
                self.turned = sem(f"{name}_turned")
                self.copied = sem(f"{name}_copied")

        def hold_vector(dve):
            dve.memset(held[:, 0:1], 0.0)

        def hold_gpsimd(pool, n):
            pool.tensor_tensor(held[:, 1 + n:2 + n], neg_half[:, 0:1], neg_half[:, 0:1], ALU.add)

        def norm_stats(dve, ln, k, added=None):
            n = ln.n
            if added is not None:
                dve.wait_ge(added, k + 1)
            wait(dve, ln.aggr, k)
            hold_vector(dve)
            for j in range(n):
                dve.bn_stats(stats[:, j, :], residual[:, bass.ds(k * n + j, 1), :]).then_inc(ln.bn, 1)
            dve.wait_ge(ln.bn, n * (k + 1))
            wait(dve, ln.normed, n * k)
            hold_vector(dve)
            for j in range(n):
                last = dve.bn_aggr(step_stats[:, j, :], stats[:, j, :])
            last.then_inc(ln.aggr, 1)

        def norm_rstd(pool, ln, k):
            n = ln.n
            pool.wait_ge(ln.aggr, k + 1)
            pool.tensor_tensor(step_rstd[:, 0:n], step_stats[:, 0:n, 1], eps_tile[:, 0:n], ALU.add).then_inc(ln.eps, 1)
            pool.wait_ge(ln.eps, k + 1)
            pool.tensor_tensor(step_rstd[:, 0:n], step_rstd[:, 0:n], neg_half[:, 0:n], ALU.pow).then_inc(ln.rstd, 1)

        def norm_apply(dve, ln, k):
            n = ln.n
            dve.wait_ge(ln.rstd, k + 1)
            wait(dve, ln.turned, k)
            for j in range(n):
                t = bass.ds(k * n + j, 1)
                dve.tensor_scalar(normed[:, j, :], residual[:, t, :], step_stats[:, j, 0:1], step_rstd[:, j:j + 1],
                                  ALU.subtract, ALU.mult).then_inc(ln.normed, 1)

        def keep_stats(dve, ln, tiles, k, added):
            at = k * tiles
            dve.wait_ge(added, k + 1)
            wait(dve, ln.aggr, k)
            hold_vector(dve)
            for j in range(tiles):
                dve.bn_stats(stats[:, j, :], residual[:, bass.ds(at + j, 1), :]).then_inc(ln.bn, 1)
            dve.wait_ge(ln.bn, tiles * (k + 1))
            wait(dve, ln.kept, k)
            hold_vector(dve)
            for j in range(tiles):
                last = dve.bn_aggr(step_kept[:, j, :], stats[:, j, :])
            last.then_inc(ln.aggr, 1)
            dve.wait_ge(ln.aggr, k + 1)
            dve.tensor_scalar(mean_var[:, bass.ds(at, tiles), :], step_kept[:, 0:tiles, :], 1.0, None, ALU.mult
                              ).then_inc(ln.kept, 1)

        def norm_turn(pe, ln, k, into):
            n = ln.n
            pe.wait_ge(ln.normed, n * (k + 1))
            wait(pe, ln.copied, k)
            for j in range(n):
                turned = pe.transpose(into[:, j * P:(j + 1) * P], normed[:, j, :], ident)
            turned.then_inc(ln.turned, 1)

        ln_c = Norm("conv_ln", PAIR)
        spectrum = sb("spectrum", [P, 3, FB, D])
        filter_h = sb("filter_h", [ORDER, NF])
        filter_a = sb("filter_a", [ORDER, NF])
        filter_r = sb("filter_r", [ORDER, NF])
        filter_k = sb("filter_k", [P, TAU, D])
        conv_bias = sb("conv_bias", [P, 3])
        conv_edge = sb("conv_edge", [P, 3, 2])
        edge_tmp = sb("edge_tmp", [P, 3, 2])
        conv_xv = sb("conv_xv", [P, 2, PT])
        value_c = sb("value_c", [P, PT])
        value_t = sb("value_t", [P, PAIR, D])
        prod = sb("prod", [P, 4, PT])
        spect_y = sb("spect_y", [P, 2, PT])
        gated = sb("gated", [P, PT])

        flt = sem("flt")
        flt_pe = sem("flt_pe")
        flt_act = sem("flt_act")
        edges_made = sem("edges_made")
        c_proj = sem("c_proj")
        c_tap2 = sem("c_tap2")
        c_edge = sem("c_edge")
        c_tap1 = sem("c_tap1")
        c_conv = sem("c_conv")
        c_value = sem("c_value")
        c_value_turned = sem("c_value_turned")
        c_value_copied = sem("c_value_copied")
        c_forward = sem("c_forward")
        c_prod = sem("c_prod")
        c_spect = sem("c_spect")
        c_inverse = sem("c_inverse")
        c_gated = sem("c_gated")
        c_out = sem("c_out")
        c_bias = sem("c_bias")
        c_added = sem("c_added")

        gates = wide[:]

        logits = sb("logits", [P, TILES, E])
        r_a = sb("r_a", [P, TILES, E])
        r_b = sb("r_b", [P, TILES, E])
        chosen = sb("chosen", [P, TILES, E])
        chosen_b = sb("chosen_b", [P, TILES, E], BF16)
        before_b = sb("before_b", [P, P], BF16)
        ones_b = sb("ones_b", [P, P], BF16)
        top = sb("top", [P, TILES])
        best = sb("best", [P, TILES])
        score = sb("score", [P, TILES])
        counts = sb("counts", [P, E, TILES])
        running = sb("running", [P, E, TILES])
        cmp_tiles = sb("cmp_tiles", [P, E, TILES])
        zeros = sb("zeros", [P, E * TILES])
        ends = sb("ends", [P, E + 1])
        n_tok = sb("n_tok", [P, E])
        n_tiles = sb("n_tiles", [P, E])
        tile_ends = sb("tile_ends", [P, E])
        start_at = sb("start_at", [P, E])
        place_f = sb("place_f", [P, TILES])
        place = sb("place", [P, TILES], I32)
        cmp_e = sb("cmp_e", [P, RT, E - 1])
        tile_expert_f = sb("tile_expert_f", [P, RT])
        tile_expert = sb("tile_expert", [P, RT], I32)
        silu_sh = sb("silu_sh", [P, IB, PT])
        act_sh = prod[:].rearrange("p (r i) t -> p r i t", r=2)
        normed_t_of = (normed_t, value_c)
        normed_of = (normed, spect_y[:, 0, :].rearrange("p (j d) -> p j d", j=PAIR))
        row_in = sb("row_in", [P, RING, D])
        row_in_t = sb("row_in_t", [P, RING, P])
        row_silu = sb("row_silu", [P, RING, I])
        row_act = sb("row_act", [P, RING, I])
        row_weights = sb("row_weights", [P, 2, 2 * I])
        row_out = sb("row_out", [P, RING, D])
        normed_all = wide[:]

        class Experts:

            def __init__(self, name, stat_steps, parts):
                self.stat_steps = stat_steps
                s = lambda what: sem(f"{name}_{what}")
                self.ln = Norm(f"{name}_ln", PAIR)
                self.kept = s("kept")
                self.logits = s("logits")
                self.route = s("route")
                self.score = s("score")
                self.counted = s("counted")
                self.rows = s("rows")
                self.sent = s("sent")
                self.up = s("up")
                self.silu = s("silu")
                self.act = s("act")
                self.down = s("down")
                self.added = s("added")
                self.row_in = [s(f"row_in{r}") for r in range(RING)]
                self.row_turned = s("row_turned")
                self.row_copied = s("row_copied")
                self.row_up = s("row_up")
                self.row_silu = s("row_silu")
                self.row_act = s("row_act")
                self.row_weights = s("row_weights")
                self.row_down = s("row_down")
                self.row_out = s("row_out")
                self.row_stored = [s(f"row_stored{r}") for r in range(RING)]
                self.parts = parts
                self.back = [s(f"back{n}") for n in range(len(parts))]
                self.summed = s("summed")

        moe = [Experts("moe0", PAIRS, (1, 1, 1, PAIRS - 3)), Experts("moe1", B, (PAIRS - 2, 1, 1))]

        def pipelined(eng, parts, n_items=RT, ring=RING, before=None):
            most = max(lead for lead, _ in parts)
            for n in range(-most, 0):
                if before and n in before:
                    before[n]()
                for lead, part in parts:
                    if n + lead >= 0:
                        part((n + lead) // ring, (n + lead) % ring)
            steps = n_items // ring
            last_whole = steps - 1 - -(-most // ring)

            def body(i, limit=None):
                for r in range(ring):
                    if before and isinstance(i, int) and ring * i + r in before:
                        before[ring * i + r]()
                    for lead, part in parts:
                        if limit is None or ring * i + r + lead < limit:
                            part(i + (r + lead) // ring, (r + lead) % ring)

            body(0)
            with eng.Fori(1, last_whole + 1) as i:
                body(i)
            for i in range(last_whole + 1, steps):
                body(i, n_items)

        def each(part):
            return lambda i, r: part(i)

        AT = 2
        ln_a = Norm("att_ln", AT)
        att_exp, att_relu = conv_xv[:, 0, :], conv_xv[:, 1, :]
        qk = silu_sh
        q_by_head_odd = sb("q_by_head_odd", [P, HEADS // 2 * L])
        q_by_head = [q.rearrange("p (h t) -> p h t", h=HEADS // 2)
                     for q in (prod[:].rearrange("p a t -> p (a t)"), q_by_head_odd[:])]
        v_aug = sb("v_aug", [P, 2, AT, HEADS, HC])
        scores_odd = sb("scores_odd", [P, AT * HEADS * P])
        scores = [s.rearrange("p (t h q) -> p t h q", t=AT, h=HEADS)
                  for s in (wide[:], scores_odd[:])]
        state = sb("state", [P, 2, HEADS, HC])
        k_tok = sb("k_tok", [P, P])
        y_rows = spect_y[:].rearrange("p t (g q) -> p t g q", g=GROUPS)
        den = sb("den", [P, AT * HEADS])
        att_y = gated[:, 0:AT * D].rearrange("p (t d) -> p t d", t=AT)
        att_yt = gated[:, AT * D:2 * AT * D]
        a_proj = sem("a_proj")
        a_vproj = sem("a_vproj")
        a_relu = sem("a_relu")
        a_qk = sem("a_qk")
        a_by_head = sem("a_by_head")
        a_by_head_v = sem("a_by_head_v")
        a_v = sem("a_v")
        a_k_turned = sem("a_k_turned")
        a_k_tok = sem("a_k_tok")
        a_state_mm = sem("a_state_mm")
        a_state = sem("a_state")
        a_score = sem("a_score")
        a_masked = sem("a_masked")
        a_copied = sem("a_copied")
        a_cleared = sem("a_cleared")
        a_carried = sem("a_carried")
        a_y_mm = sem("a_y_mm")
        a_y_rows = sem("a_y_rows")
        a_y_back = sem("a_y_back")
        a_den = sem("a_den")
        a_y = sem("a_y")
        a_y_turned = sem("a_y_turned")
        a_yt = sem("a_yt")
        a_out = sem("a_out")
        a_added = sem("a_added")

        block = ctx.enter_context(nc.Block())

        x_v = x.rearrange("b (s p) d -> p (b s) d", p=P)
        out_v = out.rearrange("b (s p) d -> p (b s) d", p=P)
        x_parts = (0, PAIR, 2 * PAIR, TILES)
        filter_loads = [(filter_sb[:], filter_weights), (positions_sb[:], positions), (f_w1_sb[:], f_w1),
                        (filt_bias_row[:], filt_bias.rearrange("(a d) -> a d", a=1))]
        table_parts = (0, TABLES["decay"][1], TABLES["inverse_dft"][1], TABLES_N)
        expert_loads = [(experts_v[:, :, 0:I], rt_gate.rearrange("e p i -> p e i")),
                        (experts_v[:, :, I:2 * I], rt_up.rearrange("e p i -> p e i"))] + [
            (experts_v[:, :, 2 * I + i * D:2 * I + (i + 1) * D],
             rt_down[:, i * P:(i + 1) * P, :].rearrange("e p d -> p e d")) for i in range(IB)]

        def routed_io(sp, m):
            def load(i, r):
                wait(sp, m.row_turned, RING * i + r - RING + 1)
                sp.dma_start(row_in[:, r, :], sorted_rows[bass.ds((RING * i + r) * P, P), :]
                             ).then_inc(m.row_in[r], 16)

            sp.wait_ge(m.sent, 16 * TILES)
            pipelined(sp, [(0, load)])

        @block.sync
        def _(sp):
            sp.dma_start(*filter_loads[0]).then_inc(filter_loaded, 16)
            for n in range(3):
                a, b = x_parts[n:n + 2]
                sp.dma_start(residual[:, a:b, :], x_v[:, a:b, :]).then_inc(x_loaded[n], 16)
            a, b = table_parts[1:3]
            sp.dma_start(tables_sb[:, a:b], tables[:, a:b]).then_inc(tables_loaded[1], 16)
            for dst, src in expert_loads:
                sp.dma_start(dst, src).then_inc(loaded_experts, 16)
            sp.wait_ge(const_made, 7)
            sp.dma_start(sorted_rows.rearrange("(t p) d -> p t d", p=P),
                         zeros[:, 0:D].unsqueeze(1).to_broadcast([P, RT, D])).then_inc(zero_rows_stored, 16)
            if phases >= 2:
                routed_io(sp, moe[0])
            if phases >= 4:
                routed_io(sp, moe[1])
            if phases in (1, 3):
                sp.wait_ge(c_added if phases == 1 else a_added, PAIRS if phases == 1 else B)
            for k in range(PAIRS):
                if phases in (2, 4):
                    sp.wait_ge(moe[phases // 2 - 1].summed, k + 1)
                sp.dma_start(out_v[:, k * PAIR:(k + 1) * PAIR, :], residual[:, k * PAIR:(k + 1) * PAIR, :]
                             ).then_inc(stored, 16)
            sp.wait_ge(stored, 16 * PAIRS)
            sp.wait_ge(zero_rows_stored, 16)
            sp.wait_ge(loaded_experts, 16 * len(expert_loads))
            sp.wait_ge(tables_loaded[2], 16)

        def send_rows(pool, m):
            for t in range(TILES):
                pool.wait_ge(m.rows, t + 1)
                pool.indirect_dma_start(
                    sorted_rows, bass.IndirectOffsetOnAxis(ap=place[:, t:t + 1].bitcast(U32), axis=0),
                    rows[:, t, :], None).then_inc(m.sent, 16)

        def part_of(m, pair):
            return sum(pair >= sum(m.parts[:n + 1]) for n in range(len(m.parts)))

        def fetch_rows(pool, m, pairs):
            if 0 in pairs:
                for r in range(RING):
                    pool.wait_ge(m.row_stored[r], 16 * (RT // RING))
            for t in range(PAIR * pairs.start, PAIR * pairs.stop):
                pool.indirect_dma_start(
                    rows[:, t, :], None, sorted_out,
                    bass.IndirectOffsetOnAxis(ap=place[:, t:t + 1].bitcast(U32), axis=0)).then_inc(m.back[part_of(m, t // PAIR)], 16)

        def experts_pool(pool, m):
            pool.wait_ge(m.ln.kept, m.stat_steps)
            pool.tensor_tensor(rstd[:], mean_var[:, :, 1], eps_tile[:], ALU.add).then_inc(m.ln.eps, 1)
            pool.wait_ge(m.ln.eps, 1)
            pool.tensor_tensor(rstd[:], rstd[:], neg_half[:], ALU.pow).then_inc(m.ln.rstd, 1)
            send_rows(pool, m)

        @block.gpsimd
        def _(pool):
            pool.memset(held[:, 6:7], 0.0).then_inc(const_made, 1)
            pool.memset(neg_half[:], -0.5).then_inc(const_made, 1)
            pool.memset(zeros[:], 0.0).then_inc(const_made, 1)
            pool.memset(ones_b[:], 1.0).then_inc(const_made, 1)
            pool.memset(v_aug[:], 0.0).then_inc(const_made, 1)
            pool.memset(state[:], 0.0).then_inc(const_made, 1)
            pool.memset(eps_tile[:], LN_EPS).then_inc(const_made, 1)
            pool.wait_ge(const_made, 7)
            pool.memset(v_aug[:].rearrange("p r t h e -> p (r t h) e")[:, :, HD:HV], 1.0).then_inc(const_made, 1)
            pool.affine_select(out=before_b[:], in_=ones_b[:], compare_op=ALU.is_gt, fill=0.0, base=0,
                               pattern=[[1, P]], channel_multiplier=-1).then_inc(const_made, 1)

            def norm_rstd_c(k):
                norm_rstd(pool, ln_c, k)

            def spectrum_sums(k):
                wait(pool, c_inverse, k)
                pool.wait_ge(c_prod, 4 * k + 2)
                pool.tensor_tensor(spect_y[:, 0, :], prod[:, 0, :], prod[:, 1, :], ALU.subtract).then_inc(c_spect, 1)
                pool.wait_ge(c_prod, 4 * k + 4)
                pool.tensor_tensor(spect_y[:, 1, :], prod[:, 2, :], prod[:, 3, :], ALU.add).then_inc(c_spect, 1)

            def out_bias(k):
                if isinstance(k, int) and k == 0:
                    pool.wait_ge(weights_loaded, 32)
                pool.wait_ge(ln_c.normed, PAIR * (k + 1))
                here = residual[:, bass.ds(k * PAIR, PAIR), :]
                pool.tensor_tensor(here, here, b_out_all[:].rearrange("p (a d) -> p a d", a=1).to_broadcast(
                    [P, PAIR, D]), ALU.add).then_inc(c_bias, 1)

            pipelined(pool, [(3, each(norm_rstd_c)), (2, each(out_bias)), (1, each(spectrum_sums))], PAIRS, 1)
            if phases < 2:
                return
            experts_pool(pool, moe[0])
            if phases < 3:
                return

            def clear_future(t):
                def part(i, r):
                    b = 2 * i + r
                    for n in range(2):
                        pool.wait_ge(a_copied, 4 * b + 2 * t + n + 1)
                        wait(pool, a_cleared, 4 * b + 2 * t + n - 3)
                        hold_gpsimd(pool, 2 * t + n)
                        s = scores[r][:, t, (2 * n + 1) * GROUPS:(2 * n + 2) * GROUPS, :]
                        pool.affine_select(out=s, in_=s, compare_op=ALU.is_ge, fill=0.0, base=0,
                                           pattern=[[0, GROUPS], [1, P]], channel_multiplier=-1).then_inc(a_cleared, 1)
                return part

            pipelined(pool, [(4, lambda i, r: norm_rstd(pool, ln_a, 2 * i + r)), (2, clear_future(0)),
                             (2, clear_future(1))], B, 2,
                      {n: lambda a=a, b=b: fetch_rows(pool, moe[0], range(a, b))
                       for n, (a, b) in {-4: (0, 1), -3: (1, 2), -2: (2, 3), -1: (3, 5), 0: (5, 7), 1: (7, 8)}.items()})
            if phases < 4:
                return
            experts_pool(pool, moe[1])
            fetch_rows(pool, moe[1], range(PAIRS))

        def mm(pe, out_, lhsT, rhs, start=True, stop=True, **kw):
            return pe.matmul(out_, lhsT, rhs, start=start, stop=stop, **kw)

        def experts_pe(pe, m):
            def turn(i, r):
                k = 2 * i + r
                pe.wait_ge(m.ln.normed, PAIR * (k + 1))
                wait(pe, m.ln.copied, k - 1)
                for j in range(PAIR):
                    last = pe.transpose(bank[2 * r][:, j * P:(j + 1) * P], normed_of[r][:, j, :], ident)
                last.then_inc(m.ln.turned, 1)

            def gate(i, r):
                k = 2 * i + r
                pe.wait_ge(m.kept, k + 1)
                for j in range(PAIR):
                    last = mm(pe, bank[1][:, bass.ds((k * PAIR + j) * E, E)], normed_t_of[r][:, j * P:(j + 1) * P],
                              gate_sb)
                last.then_inc(m.logits, 1)

            pipelined(pe, [(1, turn), (0, gate)], PAIRS, 2)

            pe.wait_ge(m.route, 7)
            pe.wait_ge(m.ln.copied, PAIRS)
            all_chosen = chosen_b[:].rearrange("p t e -> p (t e)")
            mm(pe, bank[2][:, 0:TILES * E], before_b[:], all_chosen)
            mm(pe, bank[3][:, 0:TILES * E], ones_b[:], all_chosen).then_inc(m.counted, 1)

            def up(i, r):
                k = 2 * i + r
                pe.wait_ge(m.ln.copied, k + 1)
                for b in range(IB):
                    wait(pe, m.act, IB * (k - 1) + b + 1)
                    mm(pe, bank[4 + b][:], shared_gate[:, b * P:(b + 1) * P], normed_all[:, bass.ds(k * PT, PT)])
                    mm(pe, bank[6 + b][:], shared_up[:, b * P:(b + 1) * P], normed_all[:, bass.ds(k * PT, PT)]
                       ).then_inc(m.up, 1)

            def down(i, r):
                k = 2 * i + r
                pe.wait_ge(m.act, IB * (k + 1))
                wait(pe, m.added, k)
                for j in range(PAIR):
                    for b in range(IB):
                        last = mm(pe, bank[1][:, j * P:(j + 1) * P], act_sh[:, r, b, j * P:(j + 1) * P],
                                  shared_down[:, b, :], start=(b == 0), stop=(b == IB - 1))
                last.then_inc(m.down, 1)

            pe.wait_ge(m.route, 1)
            pipelined(pe, [(1, up), (0, down)], PAIRS, 2)

            def row_turn(i, r):
                pe.wait_ge(m.row_in[r], 16 * (i + 1))
                pe.transpose(bank[r % 2][:, 0:P], row_in[:, r, :], ident).then_inc(m.row_turned, 1)

            def row_up(i, r):
                pe.wait_ge(m.row_copied, RING * i + r + 1)
                pe.wait_ge(m.row_weights, RING * i + r + 1)
                for b in range(2 * IB):
                    last = mm(pe, bank[2 + r][:, b * P:(b + 1) * P], row_weights[:, r % 2, b * P:(b + 1) * P],
                              row_in_t[:, r, :])
                last.then_inc(m.row_up, 1)

            down_expert = [None]

            def load_expert(i, r):
                down_expert[0] = pe.value_load(tile_expert[0:1, bass.ds(RING * i + r, 1)], min_val=0, max_val=E - 1)

            def row_down(i, r):
                pe.wait_ge(m.row_act, RING * i + r + 1)
                wait(pe, m.row_out, RING * i + r - 1)
                for b in range(IB):
                    last = mm(pe, bank[6 + r % 2][:, 0:D], row_act[:, r, b * P:(b + 1) * P],
                              experts[:, bass.ds(down_expert[0] * WE + 2 * I + b * D, D)],
                              start=(b == 0), stop=(b == IB - 1))
                last.then_inc(m.row_down, 1)

            pe.wait_ge(m.route, 8)
            pe.wait_ge(m.added, PAIRS)
            pipelined(pe, [(3, row_turn), (2, row_up), (0, load_expert), (0, row_down)])

        @block.tensor
        def _(pe):
            def filter_start():
                pe.wait_ge(filter_loaded, 16 * len(filter_loads))
                mm(pe, bank[4][0:ORDER, :], f_w1_sb[:], positions_sb[:]).then_inc(flt_pe, 1)
                pe.wait_ge(tables_loaded[0], 16)

            def filter_network():
                for n, w in enumerate((f_w2_sb, f_w3_sb)):
                    pe.wait_ge(flt_act, n + 1)
                    mm(pe, bank[4][0:ORDER, :], w, filter_h[:]).then_inc(flt_pe, 1)
                pe.wait_ge(flt_act, 3)
                for t in range(TAU):
                    last = mm(pe, bank[5][:, t * D:(t + 1) * D], filter_h[:, t * P:(t + 1) * P], f_wout_sb)
                last.then_inc(flt_pe, 1)

            def filter_spectrum():
                pe.wait_ge(flt, FLT_K)
                pe.wait_ge(tables_loaded[1], 16)
                for c in range(2):
                    for f in range(FB):
                        at = (c * FB + f) * D
                        for t in range(TAU):
                            last = mm(pe, bank[6][:, at:at + D], dft[:, t, c, f * P:(f + 1) * P], filter_k[:, t, :],
                                      start=(t == 0), stop=(t == TAU - 1))
                last.then_inc(flt_pe, 1)

            def project(k):
                pe.wait_ge(ln_c.copied, k + 1)
                if isinstance(k, int) and k == 0:
                    pe.wait_ge(weights_loaded, 32)
                wait(pe, c_conv, 3 * k)
                for g in range(3):
                    last = mm(pe, bank[1 + g][:], w_in_sb[:, g * D:(g + 1) * D], normed_t[:])
                last.then_inc(c_proj, 1)

            def turn_value(k):
                pe.wait_ge(c_value, k + 1)
                pe.wait_ge(ln_c.copied, min(k + 2, PAIRS) if isinstance(k, int) else k + 2)
                for j in range(PAIR):
                    last = pe.transpose(bank[0][:, j * P:(j + 1) * P], value_c[:, j * P:(j + 1) * P], ident)
                last.then_inc(c_value_turned, 1)

            def forward(k):
                pe.wait_ge(c_value_copied, k + 1)
                wait(pe, c_prod, 4 * k)
                v = value_t[:].rearrange("p (b s) d -> p s b d", s=SB)
                for c in range(2):
                    for f in range(FB):
                        o = bank[4 + c][:, f * 2 * D:(f + 1) * 2 * D].rearrange("p (b d) -> p b d", b=2)
                        for s in range(SB):
                            last = mm(pe, o, dft[:, s, c, f * P:(f + 1) * P], v[:, s, :, :],
                                      start=(s == 0), stop=(s == SB - 1))
                    last.then_inc(c_forward, 1)

            def inverse(k):
                pe.wait_ge(c_spect, 2 * k + 2)
                wait(pe, c_gated, k)
                y = spect_y[:].rearrange("p c (f b d) -> p c f b d", f=FB, b=2)
                for b in range(2):
                    for c in range(2):
                        for f in range(FB):
                            last = mm(pe, bank[6][:, b * L:(b + 1) * L], y[:, c, f, b, :], inverse_dft[:, c, f, :],
                                      start=(c == 0 and f == 0), stop=(c == 1 and f == FB - 1))
                last.then_inc(c_inverse, 1)

            def project_out(k):
                pe.wait_ge(c_gated, k + 1)
                wait(pe, c_added, k)
                for j in range(PAIR):
                    last = mm(pe, bank[7][:, j * P:(j + 1) * P], gated[:, j * P:(j + 1) * P], w_out_sb)
                last.then_inc(c_out, 1)

            def conv_turn(k):
                wait(pe, c_value_copied, k - 1)
                norm_turn(pe, ln_c, k, bank[0])

            def spectrum_first():
                filter_spectrum()
                pe.wait_ge(flt, FLT_SPECTRUM)

            pipelined(pe, [(1, each(turn_value)), (2, each(project)), (0, each(inverse)), (1, each(forward)),
                           (0, each(project_out)), (3, each(conv_turn))], PAIRS, 1,
                      {-3: filter_start, -2: filter_network, -1: spectrum_first})
            if phases < 2:
                return
            pe.wait_ge(loaded_experts, 16 * len(expert_loads))
            pe.wait_ge(const_made, 9)
            pe.wait_ge(tables_loaded[2], 16)
            experts_pe(pe, moe[0])
            if phases < 3:
                return

            def att_turn(i, r):
                wait(pe, a_v, 2 * i + r)
                norm_turn(pe, ln_a, 2 * i + r, bank[0])

            def att_project(i, r):
                b = 2 * i + r
                pe.wait_ge(ln_a.copied, b + 1)
                wait(pe, a_relu, b)
                mm(pe, bank[1][:, 0:L], w_attn_sb[:, 0:D], normed_t[:, 0:L])
                mm(pe, bank[1][:, L:2 * L], w_attn_sb[:, D:2 * D], normed_t[:, 0:L]).then_inc(a_proj, 1)
                for t in range(AT):
                    last = mm(pe, bank[0][:, t * D:(t + 1) * D], normed_t[:, t * P:(t + 1) * P],
                              w_attn_sb[:, 2 * D:3 * D])
                last.then_inc(a_vproj, 1)

            def att_turn_keys(i, r):
                b = 2 * i + r
                wait(pe, a_added, b - 2)
                pe.transpose(bank[3][:, 0:P], qk[:, r, L:L + P], ident).then_inc(a_k_turned, 1)

            def att_scores(t):
                def part(i, r):
                    b = 2 * i + r
                    pe.wait_ge(a_by_head, b + 1)
                    pe.wait_ge(a_by_head_v, b + 1)
                    for g in range(GROUPS):
                        wait(pe, a_copied if g % 2 else a_masked, 4 * b + 2 * t + g // 2)
                        rows_g = slice(P // 2 * (g // 2), P // 2 * (g // 2 + 1))
                        heads_g = slice(GROUPS * (g % 2), GROUPS * (g % 2 + 1))
                        mm(pe, bank[4 + g % 2][:].rearrange("p (h q) -> p h q", h=GROUPS),
                           qk[rows_g, r, L + t * P:L + (t + 1) * P], q_by_head[r][rows_g, heads_g, t * P:(t + 1) * P]
                           ).then_inc(a_score, 1)
                return part

            def att_state(i, r):
                b = 2 * i + r
                pe.wait_ge(a_k_tok, b + 1)
                pe.wait_ge(a_v, b + 1)
                mm(pe, bank[3][:, 2 * P:2 * P + HEADS * HV].rearrange("p (h e) -> p h e", e=HV), k_tok[:],
                   v_aug[:, r, 0, :, 0:HV]).then_inc(a_state_mm, 1)

            def att_values(i, r):
                b = 2 * i + r
                pe.wait_ge(a_masked, 4 * (b + 1))
                pe.wait_ge(a_cleared, 4 * (b + 1))
                pe.wait_ge(a_state, b + 1)
                wait(pe, a_y_rows, b)
                for g in range(GROUPS):
                    last = mm(pe, bank[7][:, g * P:(g + 1) * P],
                              state[:, r, g * GROUPS:(g + 1) * GROUPS, :].rearrange("p h e -> p (h e)"),
                              qk[:, r, P:2 * P], start=(g == 0), stop=False, skip_group_check=True)
                last.then_inc(a_carried, 1)
                for t in (1, 0):
                    for h in range(HEADS):
                        g, j = h // GROUPS, h % GROUPS
                        last = mm(pe, bank[6 + t][HC * j:HC * (j + 1), g * P:(g + 1) * P], v_aug[:, r, t, h, :],
                                  scores[r][:, t, h, :], start=(t == 0), stop=True, skip_group_check=True)
                last.then_inc(a_y_mm, 1)

            def att_y_back(t):
                def part(i, r):
                    b = 2 * i + r
                    pe.wait_ge(a_y_rows, b + 1)
                    wait(pe, a_y, 2 * b + t)
                    for g in range(GROUPS):
                        last = pe.transpose(bank[2][:, g * P:(g + 1) * P], y_rows[:, t, g, :], ident)
                    last.then_inc(a_y_back, 1)
                return part

            def att_turn_y(i, r):
                b = 2 * i + r
                pe.wait_ge(a_y, 2 * (b + 1))
                ahead = min(b + 3, B) if isinstance(b, int) else b + 3
                pe.wait_ge(a_state, ahead)
                for t in range(AT):
                    last = pe.transpose(bank[3][:, t * P:(t + 1) * P], att_y[:, t, :], ident)
                last.then_inc(a_y_turned, 1)

            def att_out(i, r):
                b = 2 * i + r
                pe.wait_ge(a_yt, b + 1)
                for t in range(AT):
                    last = mm(pe, bank[3][:, t * D:(t + 1) * D], att_yt[:, t * P:(t + 1) * P], w_proj_sb)
                last.then_inc(a_out, 1)

            pipelined(pe, [(2, att_scores(0)), (2, att_turn_keys), (3, att_turn), (0, att_y_back(0)), (2, att_state),
                           (3, att_project), (0, att_y_back(1)), (1, att_values), (0, att_turn_y),
                           (2, att_scores(1)), (0, att_out)], B, 2)
            if phases < 4:
                return
            pe.wait_ge(a_added, B)
            experts_pe(pe, moe[1])

        def copy(act, out_, in_):
            return act.activation(out_, in_, ACT.Copy)

        def experts_act(act, m):
            def keep(i, r):
                k = 2 * i + r
                act.wait_ge(m.ln.turned, k + 1)
                wait(act, m.logits, k - 1)
                copy(act, normed_t_of[r][:], bank[2 * r][:]).then_inc(m.kept, 1)
                copy(act, normed_all[:, bass.ds(k * PT, PT)], bank[2 * r][:]).then_inc(m.ln.copied, 1)

            pipelined(act, [(0, keep)], PAIRS, 2)
            act.wait_ge(const_made, 9)
            act.wait_ge(m.route, 2)
            act.activation(score[:], top[:], ACT.Sigmoid).then_inc(m.score, 1)
            act.activation(held[:, 6:7], held[:, 6:7], ACT.Silu)

            with act.Fori(0, PAIRS) as k:
                for i in range(IB):
                    act.wait_ge(m.up, IB * k + i + 1)
                    wait(act, m.act, IB * k)
                    act.activation(silu_sh[:, i, :], bank[4 + i][:], ACT.Silu).then_inc(m.silu, 1)

            def row_copy(i, r):
                act.wait_ge(m.row_turned, RING * i + r + 1)
                wait(act, m.row_up, RING * i + r - RING + 1)
                copy(act, row_in_t[:, r, :], bank[r % 2][:, 0:P]).then_inc(m.row_copied, 1)

            def row_silu_(i, r):
                act.wait_ge(m.row_up, RING * i + r + 1)
                wait(act, m.row_act, RING * i + r - RING + 1)
                act.activation(row_silu[:, r, :], bank[2 + r][:, 0:I], ACT.Silu).then_inc(m.row_silu, 1)

            def row_result(i, r):
                act.wait_ge(m.row_down, RING * i + r + 1)
                wait(act, m.row_stored[r], 16 * i)
                copy(act, row_out[:, r, :], bank[6 + r % 2][:, 0:D]).then_inc(m.row_out, 1)

            def row_store(i, r):
                act.wait_ge(m.row_out, RING * i + r + 1)
                act.dma_start(sorted_out[bass.ds((RING * i + r) * P, P), :], row_out[:, r, :]
                              ).then_inc(m.row_stored[r], 16)

            pipelined(act, [(4, row_copy), (3, row_silu_), (1, row_result), (0, row_store)])

        @block.scalar
        def _(act):
            for dst, src in filter_loads[1:]:
                act.dma_start(dst, src).then_inc(filter_loaded, 16)
            act.dma_start(tables_sb[:, 0:table_parts[1]], tables[:, 0:table_parts[1]]).then_inc(tables_loaded[0], 16)
            act.dma_start(weights_sb[:], weights).then_inc(weights_loaded, 16)
            act.dma_start(b_out_all[:], b_out.rearrange("(a d) -> a d", a=1).to_broadcast([P, D])
                          ).then_inc(weights_loaded, 16)
            a, b = table_parts[2:4]
            act.dma_start(tables_sb[:, a:b], tables[:, a:b]).then_inc(tables_loaded[2], 16)
            def filter_sines():
                for n in range(3):
                    act.wait_ge(flt, FLT_LAYER * (n + 1))
                    act.activation(filter_h[:], filter_r[:], ACT.Sin).then_inc(flt_act, 1)
                act.wait_ge(edges_made, 4)

            def copy_normed(k):
                act.wait_ge(ln_c.turned, k + 1)
                wait(act, c_proj, k)
                copy(act, normed_t[:], bank[0][:]).then_inc(ln_c.copied, 1)

            def copy_value(k):
                act.wait_ge(c_value_turned, k + 1)
                wait(act, c_forward, 2 * k)
                copy(act, value_t[:].rearrange("p j d -> p (j d)"), bank[0][:]).then_inc(c_value_copied, 1)

            def tap2(k):
                act.wait_ge(c_proj, k + 1)
                for g in range(3):
                    if g:
                        wait(act, c_value, k)
                        dst = conv_xv[:, g - 1, :]
                    else:
                        dst = gates[:, bass.ds(k * PT, PT)]
                    act.activation(dst, bank[1 + g][:], ACT.Identity, bias=conv_bias[:, g:g + 1],
                                   scale=taps[:, g, 2:3]).then_inc(c_tap2, 1)

            pipelined(act, [(1, each(copy_value)), (2, each(tap2)), (3, each(copy_normed))], PAIRS, 1,
                      {-2: filter_sines})
            if phases < 2:
                return
            experts_act(act, moe[0])
            if phases < 3:
                return

            def att_normed(i, r):
                b = 2 * i + r
                act.wait_ge(ln_a.turned, b + 1)
                wait(act, a_vproj, b)
                copy(act, normed_t[:, 0:L], bank[0][:, 0:L]).then_inc(ln_a.copied, 1)

            def att_features(i, r):
                b = 2 * i + r
                act.wait_ge(a_proj, b + 1)
                wait(act, a_qk, b)
                act.activation(att_exp, bank[1][:], ACT.Exp)
                act.activation(att_relu, bank[1][:], ACT.Relu).then_inc(a_relu, 1)

            def att_v(i, r):
                b = 2 * i + r
                act.wait_ge(a_vproj, b + 1)
                wait(act, a_y_mm, b - 1)
                for t in range(AT):
                    last = copy(act, v_aug[:, r, t, :, 0:HD], bank[0][:, t * D:(t + 1) * D].rearrange(
                        "p (h e) -> p h e", h=HEADS))
                last.then_inc(a_v, 1)

            def att_by_head(i, r):
                b = 2 * i + r
                act.wait_ge(a_qk, b + 1)
                wait(act, a_score, AT * GROUPS * (b - 1))
                for h in range(HEADS // 4):
                    last = act.activation(q_by_head[r][:, h, :], qk[:, r, 0:L], ACT.Copy,
                                          scale=head_of_half[:, h:h + 1])
                last.then_inc(a_by_head, 1)

            def att_k(i, r):
                b = 2 * i + r
                act.wait_ge(a_k_turned, b + 1)
                wait(act, a_state_mm, b)
                copy(act, k_tok[:], bank[3][:, 0:P]).then_inc(a_k_tok, 1)

            def att_scores_copy(t):
                def part(i, r):
                    b = 2 * i + r
                    for n in range(2):
                        g = 2 * n + 1
                        act.wait_ge(a_score, AT * GROUPS * b + t * GROUPS + g + 1)
                        wait(act, a_y_mm, b - 1)
                        copy(act, scores[r][:, t, g * GROUPS:(g + 1) * GROUPS, :].rearrange("p h q -> p (h q)"),
                             bank[5][:]).then_inc(a_copied, 1)
                return part

            def att_y_copy(i, r):
                b = 2 * i + r
                act.wait_ge(a_y_mm, b + 1)
                wait(act, a_y_back, AT * b)
                for t in range(AT):
                    last = copy(act, y_rows[:, t, :, :].rearrange("p g q -> p (g q)"), bank[6 + t][:])
                last.then_inc(a_y_rows, 1)

            def att_yt_copy(i, r):
                b = 2 * i + r
                act.wait_ge(a_y_turned, b + 1)
                wait(act, a_out, b)
                copy(act, att_yt, bank[3][:, 0:L]).then_inc(a_yt, 1)

            pipelined(act, [(2, att_scores_copy(0)), (2, att_k), (3, att_normed), (3, att_features), (3, att_by_head),
                            (1, att_y_copy), (0, att_yt_copy), (2, att_scores_copy(1)), (3, att_v)], B, 2)
            if phases < 4:
                return
            experts_act(act, moe[1])

        def experts_dve(dve, m):
            dve.wait_ge(m.ln.rstd, 1)

            def apply_kept(i, r):
                k = 2 * i + r
                wait(dve, m.ln.turned, k - 1)
                for j in range(PAIR):
                    t = bass.ds(k * PAIR + j, 1)
                    dve.tensor_scalar(normed_of[r][:, j, :], residual[:, t, :], mean_var[:, t, 0], rstd[:, t],
                                      ALU.subtract, ALU.mult).then_inc(m.ln.normed, 1)

            pipelined(dve, [(0, apply_kept)], PAIRS, 2)

            def bc(ap, axis, n):
                v = ap.unsqueeze(axis)
                shape = list(v.shape)
                shape[axis] = n
                return v.to_broadcast(shape)

            step = [0]

            def then(ins):
                step[0] += 1
                ins.then_inc(m.route, 1)
                dve.wait_ge(m.route, step[0])

            dve.wait_ge(m.logits, PAIRS)
            then(dve.tensor_copy(logits[:].rearrange("p t e -> p (t e)"), bank[1][:, 0:TILES * E]))
            then(dve.tensor_reduce(top[:], logits[:], AX.X, ALU.max))
            then(dve.tensor_tensor(r_a[:], logits[:], bc(top[:], 2, E), ALU.is_equal))
            then(dve.tensor_tensor(r_b[:], r_a[:], bc(tie_rank, 1, TILES), ALU.mult))
            then(dve.tensor_reduce(best[:], r_b[:], AX.X, ALU.max))
            then(dve.tensor_tensor(chosen[:], r_b[:], bc(best[:], 2, E), ALU.is_equal))
            then(dve.tensor_copy(chosen_b[:], chosen[:]))
            return step, then, bc

        def route_rest(dve, m, step, then, bc):
            dve.wait_ge(m.counted, 1)
            tmp = sem_steps
            def t2(ins):
                tmp[1] += 1
                ins.then_inc(tmp[0], 1)
                dve.wait_ge(tmp[0], tmp[1])
            t2(dve.tensor_copy(counts[:], bank[3][:, 0:TILES * E].rearrange("p (t e) -> p e t", e=E)))
            t2(dve.tensor_tensor_scan(running[:].rearrange("p e t -> p (e t)"), counts[:].rearrange("p e t -> p (e t)"),
                                      zeros[:], 0.0, ALU.add, ALU.add))
            t2(dve.memset(ends[:], 0.0))
            t2(dve.tensor_copy(ends[:, 1:E + 1], running[:, :, TILES - 1]))
            t2(dve.tensor_tensor(n_tok[:], ends[:, 1:E + 1], ends[:, 0:E], ALU.subtract))
            t2(dve.tensor_tensor(cmp_tiles[:], bc(n_tok[:], 2, TILES), bc(tile_starts, 1, E), ALU.is_gt))
            t2(dve.tensor_reduce(n_tiles[:], cmp_tiles[:], AX.X, ALU.add))
            t2(dve.tensor_tensor_scan(tile_ends[:], n_tiles[:], zeros[:, 0:E], 0.0, ALU.add, ALU.add))
            t2(dve.tensor_tensor(start_at[:], tile_ends[:], n_tiles[:], ALU.subtract))
            t2(dve.scalar_tensor_tensor(start_at[:], start_at[:], float(P), ends[:, 0:E], ALU.mult, ALU.subtract))
            t2(dve.tensor_tensor(running[:], running[:], counts[:], ALU.subtract))
            t2(dve.tensor_tensor(running[:], running[:], bc(start_at[:], 2, TILES), ALU.add))
            t2(dve.tensor_tensor(r_b[:], bank[2][:, 0:TILES * E].rearrange("p (t e) -> p t e", e=E),
                                 running[:].rearrange("p e t -> p t e"), ALU.add))
            t2(dve.tensor_tensor(r_b[:], r_b[:], chosen[:], ALU.mult))
            t2(dve.tensor_reduce(place_f[:], r_b[:], AX.X, ALU.add))
            t2(dve.tensor_copy(place[:], place_f[:]))
            t2(dve.tensor_tensor(cmp_e[:], bc(tile_ends[:, 0:E - 1], 1, RT), bc(tile_numbers, 2, E - 1), ALU.is_le))
            t2(dve.tensor_reduce(tile_expert_f[:], cmp_e[:], AX.X, ALU.add))
            then(dve.tensor_copy(tile_expert[:], tile_expert_f[:]))
            dve.wait_ge(m.score, 1)
            t2(dve.tensor_tensor(best[:], rstd[:], score[:], ALU.mult))
            if m is moe[0]:
                dve.wait_ge(zero_rows_stored, 16)

        def experts_main(dve, m):
            def gate_up(i, r):
                k = 2 * i + r
                for b in range(IB):
                    dve.wait_ge(m.silu, IB * k + b + 1)
                    wait(dve, m.down, k - 1)
                    dve.tensor_tensor(act_sh[:, r, b, :], silu_sh[:, b, :], bank[6 + b][:], ALU.mult
                                      ).then_inc(m.act, 1)

            def add_shared(i, r):
                k = 2 * i + r
                dve.wait_ge(m.down, k + 1)
                here = residual[:, bass.ds(k * PAIR, PAIR), :]
                dve.tensor_tensor(here, here, bank[1][:].rearrange("p (j d) -> p j d", j=PAIR), ALU.add
                                  ).then_inc(m.added, 1)

            def scale_rows(i, r):
                k = 2 * i + r
                for j in range(PAIR):
                    t = bass.ds(k * PAIR + j, 1)
                    dve.tensor_scalar(rows[:, t, :], residual[:, t, :], mean_var[:, t, 0], best[:, t],
                                      ALU.subtract, ALU.mult).then_inc(m.rows, 1)

            def add_shared_after(i, r):
                dve.wait_ge(m.rows, PAIR * (2 * i + r + 1))
                add_shared(i, r)

            pipelined(dve, [(1, gate_up), (3, scale_rows), (0, add_shared_after)], PAIRS, 2)

            def row_gate_up(i, r):
                dve.wait_ge(m.row_silu, RING * i + r + 1)
                wait(dve, m.row_down, RING * i + r - RING + 1)
                dve.tensor_tensor(row_act[:, r, :], row_silu[:, r, :], bank[2 + r][:, I:2 * I], ALU.mult).then_inc(m.row_act, 1)

            def row_expert(i, r):
                e = dve.value_load(tile_expert[0:1, bass.ds(RING * i + r, 1)], min_val=0, max_val=E - 1)
                wait(dve, m.row_up, RING * i + r - 1)
                dve.tensor_scalar(row_weights[:, r % 2, :], experts[:, bass.ds(e * WE, 2 * I)], 1.0, None, ALU.mult
                                  ).then_inc(m.row_weights, 1)

            pipelined(dve, [(3, row_expert), (2, row_gate_up)])

        def add_routed(dve, m, k, n):
            part = part_of(m, k * n // PAIR) if isinstance(k, int) else len(m.parts) - 1
            dve.wait_ge(m.back[part], 16 * PAIR * m.parts[part])
            here, got = (a[:, bass.ds(k * n, n), :] for a in (residual, rows))
            dve.tensor_tensor(here, here, got, ALU.add).then_inc(m.summed, 1)

        sem_steps = [sem("router_steps"), 0]

        @block.vector
        def _(dve):
            fs = [0]

            def flt_step(ins):
                fs[0] += 1
                ins.then_inc(flt, 1)
                dve.wait_ge(flt, fs[0])

            def filter_layers():
                for n in range(3):
                    dve.wait_ge(flt_pe, n + 1)
                    flt_step(dve.tensor_scalar(filter_a[:], bank[4][0:ORDER, :], f_vec[:, 2 * n:2 * n + 1],
                                               f_vec[:, 2 * n + 1:2 * n + 2], ALU.add, ALU.mult))
                    flt_step(dve.tensor_scalar(filter_r[:], filter_a[:], float(1 / (2 * np.pi)), ROUND, ALU.mult, ALU.add))
                    flt_step(dve.tensor_scalar(filter_r[:], filter_r[:], ROUND, None, ALU.subtract))
                    flt_step(dve.scalar_tensor_tensor(filter_a[:], filter_r[:], -TWO_PI_HI, filter_a[:], ALU.mult, ALU.add))
                    flt_step(dve.scalar_tensor_tensor(filter_a[:], filter_r[:], -float(TWO_PI_LO), filter_a[:],
                                                      ALU.mult, ALU.add))
                    flt_step(dve.tensor_scalar(filter_r[:], filter_a[:], PI_BELOW, -PI_BELOW, ALU.min, ALU.max))
                    assert fs[0] == FLT_LAYER * (n + 1)
                dve.wait_ge(weights_loaded, 32)
                es = [0]

                def edge_step(ins):
                    es[0] += 1
                    ins.then_inc(edges_made, 1)
                    dve.wait_ge(edges_made, es[0])

                edge_step(dve.tensor_tensor(conv_edge[:, :, 0], taps[:, :, 0], taps[:, :, 1], ALU.add))
                edge_step(dve.tensor_tensor(conv_bias[:], conv_edge[:, :, 0], taps[:, :, 2], ALU.add))
                edge_step(dve.tensor_tensor(conv_bias[:], conv_bias[:], b_in_sb, ALU.mult))
                edge_step(dve.tensor_tensor(conv_bias[:], conv_bias[:], sf_b_sb, ALU.add))
                edge_step(dve.tensor_copy(conv_edge[:, :, 1], taps[:, :, 0]))
                edge_step(dve.tensor_tensor(edge_tmp[:], conv_edge[:], b_in_sb.unsqueeze(2).to_broadcast([P, 3, 2]),
                                            ALU.mult))
                edge_step(dve.tensor_scalar(conv_edge[:], edge_tmp[:], -1.0, None, ALU.mult))

            def filter_to_spectrum():
                dve.wait_ge(flt_pe, 4)
                dve.wait_ge(tables_loaded[0], 16)
                flt_step(dve.tensor_tensor(filter_k[:], bank[5][:].rearrange("p (t d) -> p t d", t=TAU), decay, ALU.mult))
                flt_step(dve.tensor_tensor(filter_k[0:1, 0, :], filter_k[0:1, 0, :], filt_bias_row[:], ALU.add))
                assert fs[0] == FLT_K
                dve.wait_ge(flt_pe, 5)
                half = FB * D
                for part, src in ((0, 0), (1, 1), (2, 0)):
                    flt_step(dve.tensor_copy(spectrum[:, part, :, :].rearrange("p f d -> p (f d)"),
                                             bank[6][:, src * half:(src + 1) * half]))
                flt_step(dve.tensor_copy(spectrum[0:1, 2, 0, :], bank[6][0:1, half:half + D]))
                flt_step(dve.memset(spectrum[0:1, 1, 0, :], 0.0))
                assert fs[0] == FLT_SPECTRUM

            def short_conv(k):
                def seqs(ap):
                    return ap.rearrange("p (b t) -> p b t", b=2)

                for g in range(3):
                    dve.wait_ge(c_tap2, 3 * k + g + 1)
                    dst = seqs(conv_xv[:, g - 1, :] if g else gates[:, bass.ds(k * PT, PT)])
                    src = seqs(bank[1 + g][:])
                    dve.tensor_tensor(dst[:, :, 0:2], dst[:, :, 0:2],
                                      conv_edge[:, g, :].unsqueeze(1).to_broadcast([P, 2, 2]), ALU.add
                                      ).then_inc(c_edge, 1)
                    dve.wait_ge(c_edge, 3 * k + g + 1)
                    dve.scalar_tensor_tensor(dst[:, :, 1:L], src[:, :, 0:L - 1], taps[:, g, 1:2], dst[:, :, 1:L],
                                             ALU.mult, ALU.add).then_inc(c_tap1, 1)
                    dve.wait_ge(c_tap1, 3 * k + g + 1)
                    dve.scalar_tensor_tensor(dst[:, :, 2:L], src[:, :, 0:L - 2], taps[:, g, 0:1], dst[:, :, 2:L],
                                             ALU.mult, ALU.add).then_inc(c_conv, 1)
                dve.wait_ge(c_conv, 3 * k + 3)
                wait(dve, c_value_turned, k)
                dve.tensor_tensor(value_c[:], conv_xv[:, 0, :], conv_xv[:, 1, :], ALU.mult).then_inc(c_value, 1)

            def products(k):
                wait(dve, c_spect, 2 * k)
                for n, (c, part) in enumerate(((0, 0), (1, 1), (1, 2), (0, 1))):
                    dve.wait_ge(c_forward, 2 * k + c + 1)
                    dve.tensor_tensor(
                        prod[:, n, :].rearrange("p (f b d) -> p f b d", f=FB, b=2),
                        bank[4 + c][:].rearrange("p (f b d) -> p f b d", f=FB, b=2),
                        spectrum[:, part, :, :].unsqueeze(2).to_broadcast([P, FB, 2, D]), ALU.mult).then_inc(c_prod, 1)

            def gate(k):
                dve.wait_ge(c_inverse, k + 1)
                wait(dve, c_out, k)
                dve.tensor_tensor(gated[:], bank[6][:], gates[:, bass.ds(k * PT, PT)], ALU.mult).then_inc(c_gated, 1)

            def add_conv(k):
                dve.wait_ge(c_out, k + 1)
                dve.wait_ge(c_bias, k + 1)
                here = residual[:, bass.ds(k * PAIR, PAIR), :]
                dve.tensor_tensor(here, here, bank[7][:].rearrange("p (j d) -> p j d", j=PAIR), ALU.add
                                  ).then_inc(c_added, 1)

            def conv_stats(k):
                keep_stats(dve, moe[0].ln, PAIR, k, c_added)

            def conv_stats_in(k):
                if isinstance(k, int):
                    dve.wait_ge(x_loaded[min(k, 2)], 16)
                norm_stats(dve, ln_c, k)

            def conv_apply(k):
                norm_apply(dve, ln_c, k)

            pipelined(dve, [(3, each(conv_stats_in)), (3, each(conv_apply)), (2, each(short_conv)), (0, each(gate)),
                            (1, each(products)), (0, each(add_conv)), (0, each(conv_stats))], PAIRS, 1,
                      {-2: filter_layers, -1: filter_to_spectrum})
            if phases < 2:
                return
            dve.wait_ge(c_added, PAIRS)
            dve.wait_ge(tables_loaded[2], 16)
            dve.wait_ge(const_made, 9)

            def experts_vector(m):
                route_rest(dve, m, *experts_dve(dve, m))
                experts_main(dve, m)
                dve.wait_ge(m.added, PAIRS)

            experts_vector(moe[0])
            if phases < 3:
                with dve.Fori(0, PAIRS) as k:
                    add_routed(dve, moe[0], k, PAIR)
                return

            def att_in(i, r):
                b = 2 * i + r
                add_routed(dve, moe[0], b, AT)
                norm_stats(dve, ln_a, b, moe[0].summed)

            def att_feature_sum(i, r):
                b = 2 * i + r
                dve.wait_ge(a_relu, b + 1)
                wait(dve, a_carried, b - 1)
                dve.scalar_tensor_tensor(qk[:, r, :], att_exp, 1.0, att_relu, ALU.min, ALU.add).then_inc(a_qk, 1)

            def att_by_head(i, r):
                b = 2 * i + r
                dve.wait_ge(a_qk, b + 1)
                wait(dve, a_score, AT * GROUPS * (b - 1))
                for h in range(HEADS // 4, HEADS // 2):
                    last = dve.tensor_scalar(q_by_head[r][:, h, :], qk[:, r, 0:L], head_of_half[:, h:h + 1], None,
                                             ALU.mult)
                last.then_inc(a_by_head_v, 1)

            def att_mask(t):
                def part(i, r):
                    b = 2 * i + r
                    for n in range(2):
                        g = 2 * n
                        dve.wait_ge(a_score, AT * GROUPS * b + t * GROUPS + g + 1)
                        wait(dve, a_y_mm, b - 1)
                        dve.tensor_tensor(scores[r][:, t, g * GROUPS:(g + 1) * GROUPS, :],
                                          bank[4][:].rearrange("p (h q) -> p h q", h=GROUPS),
                                          causal.unsqueeze(1).to_broadcast([P, GROUPS, P]), ALU.mult
                                          ).then_inc(a_masked, 1)
                return part

            def att_state(i, r):
                b = 2 * i + r
                dve.wait_ge(a_state_mm, b + 1)
                wait(dve, a_carried, b - 1)
                dve.tensor_tensor(state[:, r, :, 0:HV],
                                  bank[3][:, 2 * P:2 * P + HEADS * HV].rearrange("p (h e) -> p h e", e=HV),
                                  own_head.rearrange("p (h e) -> p h e", e=HV), ALU.mult).then_inc(a_state, 1)

            def att_divide(t):
                def part(i, r):
                    b = 2 * i + r
                    dve.wait_ge(a_y_back, 2 * b + t + 1)
                    y = bank[2][:].rearrange("p (h e) -> p h e", e=HC)
                    here = den[:, t * HEADS:(t + 1) * HEADS]
                    wait(dve, a_y, 2 * b + t - 1)
                    dve.tensor_scalar(here, y[:, :, HD], ATT_EPS, None, ALU.add).then_inc(a_den, 1)
                    dve.wait_ge(a_den, 4 * b + 2 * t + 1)
                    dve.reciprocal(here, here).then_inc(a_den, 1)
                    dve.wait_ge(a_den, 4 * b + 2 * t + 2)
                    wait(dve, a_y_turned, b)
                    dve.tensor_tensor(att_y[:, t, :].rearrange("p (h e) -> p h e", e=HD), y[:, :, 0:HD],
                                      here.unsqueeze(2).to_broadcast([P, HEADS, HD]), ALU.mult).then_inc(a_y, 1)
                return part

            def att_add(i, r):
                b = 2 * i + r
                dve.wait_ge(a_out, b + 1)
                here = residual[:, bass.ds(b * AT, AT), :]
                dve.tensor_tensor(here, here, bank[3][:, 0:AT * D].rearrange("p (t d) -> p t d", t=AT), ALU.add
                                  ).then_inc(a_added, 1)

            def att_stats(i, r):
                keep_stats(dve, moe[1].ln, AT, 2 * i + r, a_added)

            pipelined(dve, [(3, att_mask(0)), (1, att_divide(0)), (5, att_in), (3, att_state), (1, att_divide(1)),
                            (5, lambda i, r: norm_apply(dve, ln_a, 2 * i + r)), (4, att_feature_sum),
                            (4, att_by_head), (0, att_stats), (3, att_mask(1)), (1, att_add)], B, 2)
            if phases < 4:
                return
            dve.wait_ge(a_added, B)
            experts_vector(moe[1])
            for k in range(PAIRS):
                add_routed(dve, moe[1], k, PAIR)


FLT_LAYER = 6
FLT_K = 3 * FLT_LAYER + 2
FLT_SPECTRUM = FLT_K + 5


def kernel(L0_attn_a_u, L0_attn_a_w_in, L0_attn_a_b_in, L0_attn_a_sf_w, L0_attn_a_sf_b, L0_attn_a_f_w1,
           L0_attn_a_f_b1, L0_attn_a_freq1, L0_attn_a_f_w2, L0_attn_a_f_b2, L0_attn_a_freq2, L0_attn_a_f_w3,
           L0_attn_a_f_b3, L0_attn_a_freq3, L0_attn_a_f_wout, L0_attn_a_filt_bias, L0_attn_a_w_out,
           L0_attn_a_b_out, L0_attn_b_w_attn, L0_attn_b_w_proj, L0_ffn_gate_w, L0_ffn_sh_gate, L0_ffn_sh_up,
           L0_ffn_sh_down, L0_ffn_rt_gate, L0_ffn_rt_up, L0_ffn_rt_down):
    import concourse.bacc as bacc
    from concourse.bass_utils import run_bass_kernel_spmd

    def thirds(a):
        return np.asarray(a).reshape(3, P, -1).transpose(1, 0, 2).reshape(P, -1)

    by_name = {
        "w_in": L0_attn_a_w_in, "taps": thirds(L0_attn_a_sf_w), "b_in": thirds(L0_attn_a_b_in),
        "sf_b": thirds(L0_attn_a_sf_b), "w_out": L0_attn_a_w_out, "gate_w": L0_ffn_gate_w,
        "sh_gate": L0_ffn_sh_gate, "sh_up": L0_ffn_sh_up,
        "sh_down": np.asarray(L0_ffn_sh_down).reshape(IB, P, D).transpose(1, 0, 2).reshape(P, IB * D),
        "w_attn": L0_attn_b_w_attn, "w_proj": L0_attn_b_w_proj}
    vectors = np.stack([np.asarray(v) for v in (L0_attn_a_f_b1, L0_attn_a_freq1, L0_attn_a_f_b2,
                                                L0_attn_a_freq2, L0_attn_a_f_b3, L0_attn_a_freq3)], 1)
    tables, positions = shape_constants()
    arrays = {
        "x": L0_attn_a_u,
        "weights": np.concatenate([np.asarray(by_name[name]) for name in WEIGHTS], 1),
        "filter_weights": np.concatenate([np.asarray(L0_attn_a_f_w2), np.asarray(L0_attn_a_f_w3),
                                          np.asarray(L0_attn_a_f_wout), vectors], 1),
        "f_w1": L0_attn_a_f_w1, "filt_bias": L0_attn_a_filt_bias, "b_out": L0_attn_a_b_out,
        "rt_gate": L0_ffn_rt_gate, "rt_up": L0_ffn_rt_up, "rt_down": L0_ffn_rt_down,
        "tables": tables, "positions": positions}
    arrays = {name: np.ascontiguousarray(a) for name, a in arrays.items()}

    nc = bacc.Bacc("TRN2", target_bir_lowering=False, num_devices=1)
    args = [nc.dram_tensor(name, a.shape, mybir.dt.from_np(a.dtype), kind="ExternalInput").ap()
            for name, a in arrays.items()]
    out = nc.dram_tensor("out", (B, L, D), F32, kind="ExternalOutput").ap()
    hybrid_block(nc, *args, out)
    return run_bass_kernel_spmd(nc, [arrays], core_ids=[0]).results[0]["out"]
```

```python
from contextlib import ExitStack

import numpy as np

import concourse.bass as bass
from concourse import mybir

F32 = mybir.dt.float32
BF16 = mybir.dt.bfloat16
I32 = mybir.dt.int32
U32 = mybir.dt.uint32
ALU = mybir.AluOpType
ACT = mybir.ActivationFunctionType
AX = mybir.AxisListType

P = 128
B, L, D = 16, 256, 128
TILES = B * L // P
PAIR = 4
PAIRS = TILES // PAIR
PT = PAIR * P
NF = 512
TAU = NF // P
SB = L // P
FB = NF // 2 // P
HALF = NF // 2
ORDER = 64
E = 8
I = 256
IB = I // P
WE = 2 * I + IB * D
RING = 4
RT = -(-(TILES + E - 1) // RING) * RING
HEADS, HD = 16, 8
HV = HD + 1
HC = 32
GROUPS = 4
LN_EPS = 1e-5
ATT_EPS = 1e-6
NO_TOKEN = TILES * P
ROUND = 1.5 * 2.0 ** 23
TWO_PI_HI = 6.28125
TWO_PI_LO = 2 * np.pi - TWO_PI_HI
PI_BELOW = 3.1415925


def packed(columns):
    at, where = 0, {}
    for name, n in columns:
        where[name] = (at, at + n)
        at += n
    return where, at


TABLES, TABLES_N = packed([
    ("identity", P), ("decay", TAU * D), ("dft", TAU * NF), ("inverse_dft", 2 * FB * L),
    ("causal", P), ("own_head", HEADS * HV), ("head_of_half", HEADS // 2), ("tie_rank", E),
    ("tile_starts", TILES), ("tile_numbers", RT),
    ("token_numbers", TILES)])
WEIGHTS, WEIGHTS_N = packed([
    ("w_in", 3 * D), ("taps", 9), ("b_in", 3), ("sf_b", 3), ("w_out", D), ("gate_w", E),
    ("sh_gate", I), ("sh_up", I), ("sh_down", IB * D), ("w_attn", 3 * D), ("w_proj", D)])
FILTER, FILTER_N = packed([("f_w2", ORDER), ("f_w3", ORDER), ("f_wout", D), ("f_vectors", 6)])


def shape_constants():
    c = {}
    t = np.linspace(0.0, 1.0, NF)
    w = 2 * np.pi * np.arange(NF) / NF
    positions = np.stack([t, np.cos(1e-4 * w), -np.sin(1e-4 * w)])
    rates = np.abs(np.linspace(np.log(0.01) / 1.5, np.log(0.01) / 0.3, D))
    decay = np.exp(-t[:, None] * rates[None]) + 0.05
    c["decay"] = decay.reshape(TAU, P, D).transpose(1, 0, 2)
    tau, f = np.arange(NF)[:, None], np.arange(NF // 2)[None]
    cos, sin = np.cos(2 * np.pi * tau * f / NF), -np.sin(2 * np.pi * tau * f / NF)
    sin[:, 0] = (-1.0) ** np.arange(NF)
    dft = np.stack([cos, sin], 1)
    c["dft"] = dft.reshape(TAU, P, 2, NF // 2).transpose(1, 0, 2, 3)
    weight = np.where(np.arange(NF // 2) == 0, 1.0, 2.0) / NF
    inv = (dft[:L] * weight).transpose(1, 2, 0)
    c["inverse_dft"] = inv.reshape(2, FB, P, L).transpose(2, 0, 1, 3)
    c["identity"] = np.eye(P)
    row = np.arange(P)[:, None]
    c["head_of_half"] = (row // HD % (HEADS // 2) == np.arange(HEADS // 2)[None]) * 1.0
    c["own_head"] = np.repeat(row // HD == np.arange(HEADS)[None], HV, 1) * 1.0
    c["causal"] = (np.arange(P)[None] >= row) * 1.0
    c["tie_rank"] = np.tile(E - np.arange(E), (P, 1)) * 1.0
    c["tile_starts"] = np.tile(P * np.arange(TILES), (P, 1)) * 1.0
    c["token_numbers"] = row + P * np.arange(TILES)[None] * 1.0
    c["tile_numbers"] = np.tile(np.arange(RT), (P, 1)) * 1.0
    tables = np.concatenate([c[name].reshape(P, -1) for name in TABLES], 1)
    blank_rows = np.zeros((RING * P, D + 1))
    blank_rows[:, D] = NO_TOKEN + np.arange(RING * P)
    return [np.ascontiguousarray(a, np.float32) for a in (tables, positions, blank_rows)]


def wait(eng, sem, value):
    if not isinstance(value, int) or value > 0:
        eng.wait_ge(sem, value)


def hybrid_block(nc, x, weights, filter_weights, f_w1, filt_bias, b_out, rt_gate, rt_up, rt_down,
                 tables, positions, blank_rows, out):
    with ExitStack() as ctx:
        def sb(name, shape, dt=F32):
            return ctx.enter_context(nc.sbuf_tensor(name, shape, dt))

        def sem(name):
            return ctx.enter_context(nc.semaphore(name))

        bank = [ctx.enter_context(nc.psum_tensor(f"bank{i}", [P, 512], F32)) for i in range(8)]
        sorted_rows = nc.dram_tensor("sorted_rows", [RT * P, D + 1], F32, kind="Internal").ap()
        routed = nc.dram_tensor("routed", [NO_TOKEN + RING * P, D], F32, kind="Internal").ap()

        residual = sb("residual", [P, TILES, D])
        tables_sb = sb("tables_sb", [P, TABLES_N])
        weights_sb = sb("weights_sb", [P, WEIGHTS_N])
        filter_sb = sb("filter_sb", [ORDER, FILTER_N])

        def table(name, pattern=None, **sizes):
            v = tables_sb[:, TABLES[name][0]:TABLES[name][1]]
            return v.rearrange(pattern, **sizes) if pattern else v

        def weight(name, pattern=None, **sizes):
            v = weights_sb[:, WEIGHTS[name][0]:WEIGHTS[name][1]]
            return v.rearrange(pattern, **sizes) if pattern else v

        ident = table("identity")
        decay = table("decay", "p (t d) -> p t d", t=TAU)
        dft = table("dft", "p (t c f) -> p t c f", t=TAU, c=2)
        inverse_dft = table("inverse_dft", "p (c f t) -> p c f t", c=2, f=FB)
        head_of_half, own_head, causal = table("head_of_half"), table("own_head"), table("causal")
        tie_rank, tile_starts, tile_numbers = table("tie_rank"), table("tile_starts"), table("tile_numbers")
        w_in_sb, w_out_sb, gate_sb = weight("w_in"), weight("w_out"), weight("gate_w")
        w_attn_sb, w_proj_sb = weight("w_attn"), weight("w_proj")
        taps = weight("taps", "p (g k) -> p g k", g=3)
        b_in_sb, sf_b_sb = weight("b_in"), weight("sf_b")
        shared_gate, shared_up = weight("sh_gate"), weight("sh_up")
        shared_down = weight("sh_down", "p (i d) -> p i d", i=IB)
        f_w2_sb, f_w3_sb, f_wout_sb, f_vec = (filter_sb[:, a:b] for a, b in FILTER.values())
        positions_sb = sb("positions_sb", [3, NF])
        f_w1_sb = sb("f_w1_sb", [3, ORDER])
        filt_bias_row = sb("filt_bias_row", [1, D])
        b_out_all = sb("b_out_all", [P, D])
        experts = sb("experts", [P, E * WE])
        experts_v = experts[:].rearrange("p (e c) -> p e c", e=E)

        stats = sb("stats", [P, PAIR, 6])
        step_stats = sb("step_stats", [P, PAIR, 2])
        step_rstd = sb("step_rstd", [P, PAIR])
        step_shift = sb("step_shift", [P, PAIR])
        mean_var = sb("mean_var", [P, TILES, 2])
        rstd = sb("rstd", [P, TILES])
        held = sb("held", [P, 8])
        step_kept = sb("step_kept", [P, PAIR, 2])
        eps_tile = sb("eps_tile", [P, TILES])
        neg_half = sb("neg_half", [P, TILES])
        normed = sb("normed", [P, PAIR, D])
        normed_t = sb("normed_t", [P, PT])

        rows = sb("rows", [P, TILES, D + 1])
        wide = sb("wide", [P, TILES * D])

        x_loaded = [sem(f"x_loaded{n}") for n in range(3)]
        filter_loaded = sem("filter_loaded")
        tables_loaded = [sem(f"tables_loaded{n}") for n in range(3)]
        weights_loaded = sem("weights_loaded")
        loaded_experts = sem("loaded_experts")
        const_made = sem("const_made")
        blank_rows_stored = sem("blank_rows_stored")
        stored = sem("stored")

        class Norm:

            def __init__(self, name, n, keeps=False):
                self.n = n
                if keeps:
                    self.kept = sem(f"{name}_kept")
                self.bn = sem(f"{name}_bn")
                self.aggr = sem(f"{name}_aggr")
                self.eps = sem(f"{name}_eps")
                self.rstd = sem(f"{name}_rstd")
                self.normed = sem(f"{name}_normed")
                self.turned = sem(f"{name}_turned")
                self.copied = sem(f"{name}_copied")

        def hold_vector(dve):
            dve.memset(held[:, 0:1], 0.0)

        def hold_gpsimd(pool, n):
            pool.tensor_tensor(held[:, 1 + n:2 + n], neg_half[:, 0:1], neg_half[:, 0:1], ALU.add)

        def norm_stats(dve, ln, k, added=None):
            n = ln.n
            if added is not None:
                dve.wait_ge(added, k + 1)
            wait(dve, ln.aggr, k)
            hold_vector(dve)
            for j in range(n):
                dve.bn_stats(stats[:, j, :], residual[:, bass.ds(k * n + j, 1), :]).then_inc(ln.bn, 1)
            dve.wait_ge(ln.bn, n * (k + 1))
            wait(dve, ln.normed, n * k)
            hold_vector(dve)
            for j in range(n):
                last = dve.bn_aggr(step_stats[:, j, :], stats[:, j, :])
            last.then_inc(ln.aggr, 1)

        def norm_rstd(pool, ln, k):
            n = ln.n
            pool.wait_ge(ln.aggr, k + 1)
            pool.tensor_tensor(step_rstd[:, 0:n], step_stats[:, 0:n, 1], eps_tile[:, 0:n], ALU.add).then_inc(ln.eps, 1)
            pool.wait_ge(ln.eps, k + 1)
            pool.tensor_tensor(step_rstd[:, 0:n], step_rstd[:, 0:n], neg_half[:, 0:n], ALU.pow).then_inc(ln.rstd, 1)

        def norm_apply(dve, ln, k):
            n = ln.n
            dve.wait_ge(ln.rstd, k + 1)
            wait(dve, ln.turned, k)
            for j in range(n):
                t = bass.ds(k * n + j, 1)
                dve.tensor_scalar(normed[:, j, :], residual[:, t, :], step_stats[:, j, 0:1], step_rstd[:, j:j + 1],
                                  ALU.subtract, ALU.mult).then_inc(ln.normed, 1)

        def keep_stats(dve, ln, tiles, k, added):
            at = k * tiles
            dve.wait_ge(added, k + 1)
            wait(dve, ln.aggr, k)
            hold_vector(dve)
            for j in range(tiles):
                dve.bn_stats(stats[:, j, :], residual[:, bass.ds(at + j, 1), :]).then_inc(ln.bn, 1)
            dve.wait_ge(ln.bn, tiles * (k + 1))
            wait(dve, ln.kept, k)
            hold_vector(dve)
            for j in range(tiles):
                last = dve.bn_aggr(step_kept[:, j, :], stats[:, j, :])
            last.then_inc(ln.aggr, 1)
            dve.wait_ge(ln.aggr, k + 1)
            dve.tensor_scalar(mean_var[:, bass.ds(at, tiles), :], step_kept[:, 0:tiles, :], 1.0, None, ALU.mult
                              ).then_inc(ln.kept, 1)

        def norm_turn(pe, ln, k, into):
            n = ln.n
            pe.wait_ge(ln.normed, n * (k + 1))
            wait(pe, ln.copied, k)
            for j in range(n):
                turned = pe.transpose(into[:, j * P:(j + 1) * P], normed[:, j, :], ident)
            turned.then_inc(ln.turned, 1)

        ln_c = Norm("conv_ln", PAIR)
        spectrum = sb("spectrum", [P, 3, FB, D])
        filter_h = sb("filter_h", [ORDER, NF])
        filter_a = sb("filter_a", [ORDER, NF])
        filter_r = sb("filter_r", [ORDER, NF])
        filter_k = sb("filter_k", [P, TAU, D])
        conv_bias = sb("conv_bias", [P, 3])
        conv_edge = sb("conv_edge", [P, 3, 2])
        edge_tmp = sb("edge_tmp", [P, 3, 2])
        conv_xv = sb("conv_xv", [P, 2, PT])
        value_c = sb("value_c", [P, PT])
        value_t = sb("value_t", [P, PAIR, D])
        prod = sb("prod", [P, 4, PT])
        spect_y = sb("spect_y", [P, 2, PT])
        gated = sb("gated", [P, PT])

        flt = sem("flt")
        flt_pe = sem("flt_pe")
        flt_act = sem("flt_act")
        edges_made = sem("edges_made")
        c_shift = sem("c_shift")
        c_proj = sem("c_proj")
        c_tap2 = sem("c_tap2")
        c_edge = sem("c_edge")
        c_tap1 = sem("c_tap1")
        c_conv = sem("c_conv")
        c_value = sem("c_value")
        c_value_turned = sem("c_value_turned")
        c_value_copied = sem("c_value_copied")
        c_forward = sem("c_forward")
        c_prod = sem("c_prod")
        c_spect = sem("c_spect")
        c_inverse = sem("c_inverse")
        c_gated = sem("c_gated")
        c_out = sem("c_out")
        c_bias = sem("c_bias")
        c_added = sem("c_added")

        gates = wide[:]

        logits = sb("logits", [P, TILES, E])
        r_a = sb("r_a", [P, TILES, E])
        r_b = sb("r_b", [P, TILES, E])
        chosen = sb("chosen", [P, TILES, E])
        chosen_b = sb("chosen_b", [P, TILES, E], BF16)
        before_b = sb("before_b", [P, P], BF16)
        ones_b = sb("ones_b", [P, P], BF16)
        top = sb("top", [P, TILES])
        best = sb("best", [P, TILES])
        score = sb("score", [P, TILES])
        counts = sb("counts", [P, E, TILES])
        running = sb("running", [P, E, TILES])
        cmp_tiles = sb("cmp_tiles", [P, E, TILES])
        zeros = sb("zeros", [P, E * TILES])[:]
        ends = sb("ends", [P, E + 1])
        n_tok = sb("n_tok", [P, E])
        n_tiles = sb("n_tiles", [P, E])
        tile_ends = sb("tile_ends", [P, E])
        start_at = sb("start_at", [P, E])
        place_f = sb("place_f", [P, TILES])
        place = sb("place", [P, TILES], I32)
        cmp_e = sb("cmp_e", [P, RT, E - 1])
        tile_expert_f = sb("tile_expert_f", [P, RT])
        tile_expert = sb("tile_expert", [P, RT], I32)
        silu_sh = sb("silu_sh", [P, IB, PT])
        act_sh = prod[:].rearrange("p (r i) t -> p r i t", r=2)
        normed_t_of = (normed_t, value_c)
        normed_of = (normed, spect_y[:, 0, :].rearrange("p (j d) -> p j d", j=PAIR))
        row_in = sb("row_in", [P, RING, D + 1])
        row_token = sb("row_token", [P, RING], I32)
        row_in_t = sb("row_in_t", [P, RING, P])
        row_silu = sb("row_silu", [P, RING, I])
        row_act = sb("row_act", [P, RING, I])
        row_weights = sb("row_weights", [P, 2, 2 * I])
        row_out = sb("row_out", [P, RING, D])
        normed_all = wide[:]

        class Experts:

            def __init__(self, name, stat_steps, parts):
                self.stat_steps = stat_steps
                s = lambda what: sem(f"{name}_{what}")
                self.ln = Norm(f"{name}_ln", PAIR, keeps=True)
                self.kept = s("kept")
                self.logits = s("logits")
                self.route = s("route")
                self.score = s("score")
                self.counted = s("counted")
                self.rows = s("rows")
                self.sent = s("sent")
                self.up = s("up")
                self.silu = s("silu")
                self.act = s("act")
                self.down = s("down")
                self.added = s("added")
                self.row_in = [s(f"row_in{r}") for r in range(RING)]
                self.row_turned = s("row_turned")
                self.row_copied = s("row_copied")
                self.row_up = s("row_up")
                self.row_silu = s("row_silu")
                self.row_act = s("row_act")
                self.row_weights = s("row_weights")
                self.row_token = s("row_token")
                self.held = s("held")
                self.row_down = s("row_down")
                self.row_out = s("row_out")
                self.row_stored = [s(f"row_stored{r}") for r in range(RING)]
                self.parts = parts
                self.back = [s(f"back{n}") for n in range(len(parts))]
                self.summed = s("summed")

        moe = [Experts("moe0", PAIRS, (1, PAIRS - 1)), Experts("moe1", B, (3, 3, 1, 1))]

        def pipelined(eng, parts, n_items=RT, ring=RING, before=None):
            most = max(lead for lead, _ in parts)
            for n in range(-most, 0):
                if before and n in before:
                    before[n]()
                for lead, part in parts:
                    if n + lead >= 0:
                        part((n + lead) // ring, (n + lead) % ring)
            steps = n_items // ring
            last_whole = steps - 1 - -(-most // ring)

            def body(i, limit=None):
                for r in range(ring):
                    if before and isinstance(i, int) and ring * i + r in before:
                        before[ring * i + r]()
                    for lead, part in parts:
                        if limit is None or ring * i + r + lead < limit:
                            part(i + (r + lead) // ring, (r + lead) % ring)

            body(0)
            with eng.Fori(1, last_whole + 1) as i:
                body(i)
            for i in range(last_whole + 1, steps):
                body(i, n_items)

        def each(part):
            return lambda i, r: part(i)

        AT = 2
        ln_a = Norm("att_ln", AT)
        att_exp, att_relu = conv_xv[:, 0, :], conv_xv[:, 1, :]
        qk = silu_sh
        q_by_head_odd = sb("q_by_head_odd", [P, HEADS // 2 * L])
        q_by_head = [q.rearrange("p (h t) -> p h t", h=HEADS // 2)
                     for q in (prod[:].rearrange("p a t -> p (a t)"), q_by_head_odd[:])]
        v_aug = sb("v_aug", [P, 2, AT, HEADS, HC])
        scores_odd = sb("scores_odd", [P, AT * HEADS * P])
        scores = [s.rearrange("p (t h q) -> p t h q", t=AT, h=HEADS)
                  for s in (wide[:], scores_odd[:])]
        state = sb("state", [P, 2, HEADS, HC])
        k_tok = sb("k_tok", [P, P])
        y_rows = spect_y[:].rearrange("p t (g q) -> p t g q", g=GROUPS)
        den = sb("den", [P, AT * HEADS])
        att_y = gated[:, 0:AT * D].rearrange("p (t d) -> p t d", t=AT)
        att_yt = gated[:, AT * D:2 * AT * D]
        a_proj = sem("a_proj")
        a_vproj = sem("a_vproj")
        a_relu = sem("a_relu")
        a_qk = sem("a_qk")
        a_by_head = sem("a_by_head")
        a_by_head_v = sem("a_by_head_v")
        a_v = sem("a_v")
        a_k_turned = sem("a_k_turned")
        a_k_tok = sem("a_k_tok")
        a_state_mm = sem("a_state_mm")
        a_state = sem("a_state")
        a_score = sem("a_score")
        a_masked = sem("a_masked")
        a_copied = sem("a_copied")
        a_cleared = sem("a_cleared")
        a_carried = sem("a_carried")
        a_y_mm = sem("a_y_mm")
        a_y_rows = sem("a_y_rows")
        a_y_back = sem("a_y_back")
        a_den = sem("a_den")
        a_y = sem("a_y")
        a_y_turned = sem("a_y_turned")
        a_yt = sem("a_yt")
        a_out = sem("a_out")
        a_added = sem("a_added")

        block = ctx.enter_context(nc.Block())

        x_v = x.rearrange("b (s p) d -> p (b s) d", p=P)
        out_v = out.rearrange("b (s p) d -> p (b s) d", p=P)
        x_parts = (0, PAIR, 2 * PAIR, TILES)
        filter_loads = [(filter_sb[:], filter_weights), (ident, tables[:, 0:P]), (positions_sb[:], positions),
                        (f_w1_sb[:], f_w1),
                        (filt_bias_row[:], filt_bias.rearrange("(a d) -> a d", a=1))]
        table_parts = (0, TABLES["decay"][1], TABLES["inverse_dft"][1], TABLES_N)
        expert_loads = [(experts_v[:, :, 0:I], rt_gate.rearrange("e p i -> p e i")),
                        (experts_v[:, :, I:2 * I], rt_up.rearrange("e p i -> p e i"))] + [
            (experts_v[:, :, 2 * I + i * D:2 * I + (i + 1) * D],
             rt_down[:, i * P:(i + 1) * P, :].rearrange("e p d -> p e d")) for i in range(IB)]

        def store_blank_rows(sp):
            sp.dma_start(sorted_rows.rearrange("(i n) d -> i n d", n=RING * P),
                         blank_rows.unsqueeze(0).to_broadcast([RT // RING, RING * P, D + 1])
                         ).then_inc(blank_rows_stored, 16)

        def part_of(m, pair):
            return sum(pair >= sum(m.parts[:n + 1]) for n in range(len(m.parts)))

        def routed_io(sp, m):
            def load(i, r):
                wait(sp, m.row_turned, RING * i + r - RING + 1)
                wait(sp, m.row_token, RING * i + r - RING + 1)
                sp.dma_start(row_in[:, r, :], sorted_rows[bass.ds((RING * i + r) * P, P), :]
                             ).then_inc(m.row_in[r], 16)

            sp.wait_ge(m.sent, 16 * TILES)
            pipelined(sp, [(0, load)])
            for r in range(RING):
                sp.wait_ge(m.row_stored[r], 16 * (RT // RING))
            sp.wait_ge(m.sent, 16 * TILES)
            for k in range(PAIRS):
                sp.dma_start(rows[:, k * PAIR:(k + 1) * PAIR, 0:D],
                             routed[k * PT:(k + 1) * PT, :].rearrange("(j p) d -> p j d", p=P)
                             ).then_inc(m.back[part_of(m, k)], 16)

        @block.sync
        def _(sp):
            for dst, src in filter_loads[:2]:
                sp.dma_start(dst, src).then_inc(filter_loaded, 16)
            for n in range(3):
                a, b = x_parts[n:n + 2]
                sp.dma_start(residual[:, a:b, :], x_v[:, a:b, :]).then_inc(x_loaded[n], 16)
            a, b = table_parts[1:3]
            sp.dma_start(tables_sb[:, a:b], tables[:, a:b]).then_inc(tables_loaded[1], 16)
            for dst, src in expert_loads:
                sp.dma_start(dst, src).then_inc(loaded_experts, 16)
            store_blank_rows(sp)
            routed_io(sp, moe[0])
            for r in range(RING):
                sp.wait_ge(moe[0].row_in[r], 16 * (RT // RING))
            store_blank_rows(sp)
            routed_io(sp, moe[1])
            for k in range(PAIRS):
                sp.wait_ge(moe[1].summed, k + 1)
                sp.dma_start(out_v[:, k * PAIR:(k + 1) * PAIR, :], residual[:, k * PAIR:(k + 1) * PAIR, :]
                             ).then_inc(stored, 16)
            sp.wait_ge(stored, 16 * PAIRS)
            sp.wait_ge(blank_rows_stored, 32)
            sp.wait_ge(loaded_experts, 16 * len(expert_loads))
            sp.wait_ge(tables_loaded[2], 16)

        def send_rows(pool, m):
            for t in range(TILES):
                pool.wait_ge(m.rows, t + 1)
                pool.indirect_dma_start(
                    sorted_rows, bass.IndirectOffsetOnAxis(ap=place[:, t:t + 1].bitcast(U32), axis=0),
                    rows[:, t, :], None).then_inc(m.sent, 16)

        def scatter_result(pool, m):
            def part(i, r):
                pool.wait_ge(m.row_out, RING * i + r + 1)
                pool.wait_ge(m.row_token, RING * i + r + 1)
                wait(pool, m.held, RING * i + r - RING + 1)
                pool.tensor_tensor(held[:, 1 + r:2 + r], neg_half[:, 0:1], neg_half[:, 0:1], ALU.add
                                   ).then_inc(m.held, 1)
                pool.indirect_dma_start(
                    routed, bass.IndirectOffsetOnAxis(ap=row_token[:, r:r + 1].bitcast(U32), axis=0),
                    row_out[:, r, :], None).then_inc(m.row_stored[r], 16)
            return part

        def experts_pool(pool, m):
            last = TILES - TILES // m.stat_steps
            for n, (a, b) in enumerate(((0, last), (last, TILES))):
                pool.wait_ge(m.ln.kept, m.stat_steps - 1 + n)
                pool.tensor_tensor(rstd[:, a:b], mean_var[:, a:b, 1], eps_tile[:, a:b], ALU.add).then_inc(m.ln.eps, 1)
                pool.wait_ge(m.ln.eps, n + 1)
                pool.tensor_tensor(rstd[:, a:b], rstd[:, a:b], neg_half[:, a:b], ALU.pow).then_inc(m.ln.rstd, 1)
            send_rows(pool, m)
            pipelined(pool, [(0, scatter_result(pool, m))])

        @block.gpsimd
        def _(pool):
            pool.memset(held[:, 6:7], 0.0).then_inc(const_made, 1)
            pool.memset(neg_half[:], -0.5).then_inc(const_made, 1)
            pool.memset(zeros, 0.0).then_inc(const_made, 1)
            pool.memset(ones_b[:], 1.0).then_inc(const_made, 1)
            pool.memset(v_aug[:], 0.0).then_inc(const_made, 1)
            pool.memset(state[:], 0.0).then_inc(const_made, 1)
            pool.memset(eps_tile[:], LN_EPS).then_inc(const_made, 1)
            pool.wait_ge(const_made, 7)
            pool.memset(v_aug[:].rearrange("p r t h e -> p (r t h) e")[:, :, HD:HV], 1.0).then_inc(const_made, 1)
            pool.affine_select(out=before_b[:], in_=ones_b[:], compare_op=ALU.is_gt, fill=0.0, base=0,
                               pattern=[[1, P]], channel_multiplier=-1).then_inc(const_made, 1)

            def norm_rstd_c(k):
                norm_rstd(pool, ln_c, k)
                pool.wait_ge(ln_c.rstd, k + 1)
                pool.tensor_tensor(step_shift[:], step_stats[:, :, 0], step_rstd[:], ALU.mult).then_inc(c_shift, 1)
                pool.wait_ge(c_shift, 2 * k + 1)
                pool.tensor_tensor(step_shift[:], zeros[:, 0:PAIR], step_shift[:], ALU.subtract).then_inc(c_shift, 1)

            def spectrum_sums(k):
                wait(pool, c_inverse, k)
                pool.wait_ge(c_prod, 4 * k + 2)
                pool.tensor_tensor(spect_y[:, 0, :], prod[:, 0, :], prod[:, 1, :], ALU.subtract).then_inc(c_spect, 1)
                pool.wait_ge(c_prod, 4 * k + 4)
                pool.tensor_tensor(spect_y[:, 1, :], prod[:, 2, :], prod[:, 3, :], ALU.add).then_inc(c_spect, 1)

            def value(k):
                pool.wait_ge(c_conv, 3 * k + 3)
                wait(pool, c_value_turned, k)
                pool.tensor_tensor(value_c[:], conv_xv[:, 0, :], conv_xv[:, 1, :], ALU.mult).then_inc(c_value, 1)

            def out_bias(k):
                if isinstance(k, int) and k == 0:
                    pool.wait_ge(weights_loaded, 32)
                pool.wait_ge(ln_c.normed, PAIR * (k + 1))
                here = residual[:, bass.ds(k * PAIR, PAIR), :]
                pool.tensor_tensor(here, here, b_out_all[:].rearrange("p (a d) -> p a d", a=1).to_broadcast(
                    [P, PAIR, D]), ALU.add).then_inc(c_bias, 1)

            pipelined(pool, [(3, each(norm_rstd_c)), (2, each(out_bias)), (2, each(value)),
                             (1, each(spectrum_sums))], PAIRS, 1)
            experts_pool(pool, moe[0])

            def clear_future(t):
                def part(i, r):
                    b = 2 * i + r
                    for n in range(2):
                        pool.wait_ge(a_copied, 4 * b + 2 * t + n + 1)
                        wait(pool, a_cleared, 4 * b + 2 * t + n - 3)
                        hold_gpsimd(pool, 2 * t + n)
                        s = scores[r][:, t, (2 * n + 1) * GROUPS:(2 * n + 2) * GROUPS, :]
                        pool.affine_select(out=s, in_=s, compare_op=ALU.is_ge, fill=0.0, base=0,
                                           pattern=[[0, GROUPS], [1, P]], channel_multiplier=-1).then_inc(a_cleared, 1)
                return part

            pipelined(pool, [(4, lambda i, r: norm_rstd(pool, ln_a, 2 * i + r)), (2, clear_future(0)),
                             (2, clear_future(1))], B, 2)
            experts_pool(pool, moe[1])

        def mm(pe, out_, lhsT, rhs, start=True, stop=True, **kw):
            return pe.matmul(out_, lhsT, rhs, start=start, stop=stop, **kw)

        def experts_pe(pe, m):
            def turn(i, r):
                k = 2 * i + r
                pe.wait_ge(m.ln.normed, PAIR * (k + 1))
                wait(pe, m.ln.copied, k - 1)
                for j in range(PAIR):
                    last = pe.transpose(bank[2 * r][:, j * P:(j + 1) * P], normed_of[r][:, j, :], ident)
                last.then_inc(m.ln.turned, 1)

            def gate(i, r):
                k = 2 * i + r
                pe.wait_ge(m.kept, k + 1)
                for j in range(PAIR):
                    last = mm(pe, bank[1][:, bass.ds((k * PAIR + j) * E, E)], normed_t_of[r][:, j * P:(j + 1) * P],
                              gate_sb)
                last.then_inc(m.logits, 1)

            pipelined(pe, [(1, turn), (0, gate)], PAIRS, 2)

            pe.wait_ge(m.route, 7)
            pe.wait_ge(m.ln.copied, PAIRS)
            all_chosen = chosen_b[:].rearrange("p t e -> p (t e)")
            mm(pe, bank[2][:, 0:TILES * E], before_b[:], all_chosen)
            mm(pe, bank[3][:, 0:TILES * E], ones_b[:], all_chosen).then_inc(m.counted, 1)

            def up(i, r):
                k = 2 * i + r
                pe.wait_ge(m.ln.copied, k + 1)
                for b in range(IB):
                    wait(pe, m.act, IB * (k - 1) + b + 1)
                    mm(pe, bank[4 + b][:], shared_gate[:, b * P:(b + 1) * P], normed_all[:, bass.ds(k * PT, PT)])
                    mm(pe, bank[6 + b][:], shared_up[:, b * P:(b + 1) * P], normed_all[:, bass.ds(k * PT, PT)]
                       ).then_inc(m.up, 1)

            def down(i, r):
                k = 2 * i + r
                pe.wait_ge(m.act, IB * (k + 1))
                wait(pe, m.added, k)
                for j in range(PAIR):
                    for b in range(IB):
                        last = mm(pe, bank[1][:, j * P:(j + 1) * P], act_sh[:, r, b, j * P:(j + 1) * P],
                                  shared_down[:, b, :], start=(b == 0), stop=(b == IB - 1))
                last.then_inc(m.down, 1)

            pe.wait_ge(m.route, 1)
            pipelined(pe, [(1, up), (0, down)], PAIRS, 2)

            def row_turn(i, r):
                pe.wait_ge(m.row_in[r], 16 * (i + 1))
                pe.transpose(bank[r % 2][:, 0:P], row_in[:, r, 0:D], ident).then_inc(m.row_turned, 1)

            def row_up(i, r):
                pe.wait_ge(m.row_copied, RING * i + r + 1)
                pe.wait_ge(m.row_weights, RING * i + r + 1)
                for b in range(2 * IB):
                    last = mm(pe, bank[2 + r][:, b * P:(b + 1) * P], row_weights[:, r % 2, b * P:(b + 1) * P],
                              row_in_t[:, r, :])
                last.then_inc(m.row_up, 1)

            down_expert = [None]

            def load_expert(i, r):
                down_expert[0] = pe.value_load(tile_expert[0:1, bass.ds(RING * i + r, 1)], min_val=0, max_val=E - 1)

            def row_down(i, r):
                pe.wait_ge(m.row_act, RING * i + r + 1)
                wait(pe, m.row_out, RING * i + r - 1)
                for b in range(IB):
                    last = mm(pe, bank[6 + r % 2][:, 0:D], row_act[:, r, b * P:(b + 1) * P],
                              experts[:, bass.ds(down_expert[0] * WE + 2 * I + b * D, D)],
                              start=(b == 0), stop=(b == IB - 1))
                last.then_inc(m.row_down, 1)

            pe.wait_ge(m.route, 10)
            pe.wait_ge(m.added, PAIRS)
            pipelined(pe, [(0, load_expert), (3, row_turn), (2, row_up), (0, row_down)])

        @block.tensor
        def _(pe):
            def filter_start():
                pe.wait_ge(filter_loaded, 16 * len(filter_loads))
                for h in range(2):
                    mm(pe, bank[4 + h][0:ORDER, 0:HALF], f_w1_sb[:], positions_sb[:, h * HALF:(h + 1) * HALF]
                       ).then_inc(flt_pe, 1)

            def filter_network():
                for n, w in enumerate((f_w2_sb, f_w3_sb)):
                    for h in range(2):
                        pe.wait_ge(flt_act, 2 * n + h + 1)
                        mm(pe, bank[4 + h][0:ORDER, 0:HALF], w, filter_h[:, h * HALF:(h + 1) * HALF]
                           ).then_inc(flt_pe, 1)
                pe.wait_ge(flt_act, 6)
                for t in range(TAU):
                    last = mm(pe, bank[7][:, t * D:(t + 1) * D], filter_h[:, t * P:(t + 1) * P], f_wout_sb)
                last.then_inc(flt_pe, 1)

            def filter_spectrum():
                pe.wait_ge(flt, FLT_K)
                pe.wait_ge(tables_loaded[1], 16)
                for c in range(2):
                    for f in range(FB):
                        at = (c * FB + f) * D
                        for t in range(TAU):
                            last = mm(pe, bank[6][:, at:at + D], dft[:, t, c, f * P:(f + 1) * P], filter_k[:, t, :],
                                      start=(t == 0), stop=(t == TAU - 1))
                last.then_inc(flt_pe, 1)

            def project(k):
                pe.wait_ge(ln_c.copied, k + 1)
                if isinstance(k, int) and k == 0:
                    pe.wait_ge(weights_loaded, 32)
                wait(pe, c_conv, 3 * k)
                for g in range(3):
                    last = mm(pe, bank[1 + g][:], w_in_sb[:, g * D:(g + 1) * D], normed_t[:])
                last.then_inc(c_proj, 1)

            def turn_value(k):
                pe.wait_ge(c_value, k + 1)
                pe.wait_ge(ln_c.copied, min(k + 2, PAIRS) if isinstance(k, int) else k + 2)
                for j in range(PAIR):
                    last = pe.transpose(bank[0][:, j * P:(j + 1) * P], value_c[:, j * P:(j + 1) * P], ident)
                last.then_inc(c_value_turned, 1)

            def forward(k):
                pe.wait_ge(c_value_copied, k + 1)
                wait(pe, c_prod, 4 * k)
                v = value_t[:].rearrange("p (b s) d -> p s b d", s=SB)
                for c in range(2):
                    for f in range(FB):
                        o = bank[4 + c][:, f * 2 * D:(f + 1) * 2 * D].rearrange("p (b d) -> p b d", b=2)
                        for s in range(SB):
                            last = mm(pe, o, dft[:, s, c, f * P:(f + 1) * P], v[:, s, :, :],
                                      start=(s == 0), stop=(s == SB - 1))
                    last.then_inc(c_forward, 1)

            def inverse(k):
                pe.wait_ge(c_spect, 2 * k + 2)
                wait(pe, c_gated, k)
                y = spect_y[:].rearrange("p c (f b d) -> p c f b d", f=FB, b=2)
                for b in range(2):
                    for c in range(2):
                        for f in range(FB):
                            last = mm(pe, bank[6][:, b * L:(b + 1) * L], y[:, c, f, b, :], inverse_dft[:, c, f, :],
                                      start=(c == 0 and f == 0), stop=(c == 1 and f == FB - 1))
                last.then_inc(c_inverse, 1)

            def project_out(k):
                pe.wait_ge(c_gated, k + 1)
                wait(pe, c_added, k)
                for j in range(PAIR):
                    last = mm(pe, bank[7][:, j * P:(j + 1) * P], gated[:, j * P:(j + 1) * P], w_out_sb)
                last.then_inc(c_out, 1)

            def conv_turn(k):
                wait(pe, c_value_copied, k - 1)
                norm_turn(pe, ln_c, k, bank[0])

            def spectrum_first():
                filter_spectrum()
                pe.wait_ge(flt, FLT_SPECTRUM)

            pipelined(pe, [(1, each(turn_value)), (2, each(project)), (0, each(inverse)), (1, each(forward)),
                           (3, each(conv_turn)), (0, each(project_out))], PAIRS, 1,
                      {-3: filter_start, -2: filter_network, -1: spectrum_first})
            pe.wait_ge(loaded_experts, 16 * len(expert_loads))
            pe.wait_ge(const_made, 9)
            pe.wait_ge(tables_loaded[2], 16)
            experts_pe(pe, moe[0])

            def att_turn(i, r):
                wait(pe, a_v, 2 * i + r)
                norm_turn(pe, ln_a, 2 * i + r, bank[0])

            def att_project(i, r):
                b = 2 * i + r
                pe.wait_ge(ln_a.copied, b + 1)
                wait(pe, a_relu, b)
                mm(pe, bank[1][:, 0:L], w_attn_sb[:, 0:D], normed_t[:, 0:L])
                mm(pe, bank[1][:, L:2 * L], w_attn_sb[:, D:2 * D], normed_t[:, 0:L]).then_inc(a_proj, 1)
                for t in range(AT):
                    last = mm(pe, bank[0][:, t * D:(t + 1) * D], normed_t[:, t * P:(t + 1) * P],
                              w_attn_sb[:, 2 * D:3 * D])
                last.then_inc(a_vproj, 1)

            def att_turn_keys(i, r):
                b = 2 * i + r
                wait(pe, a_added, b - 2)
                pe.transpose(bank[3][:, 0:P], qk[:, r, L:L + P], ident).then_inc(a_k_turned, 1)

            def att_scores(t):
                def part(i, r):
                    b = 2 * i + r
                    pe.wait_ge(a_by_head, b + 1)
                    pe.wait_ge(a_by_head_v, b + 1)
                    for g in range(GROUPS):
                        wait(pe, a_copied if g % 2 else a_masked, 4 * b + 2 * t + g // 2)
                        rows_g = slice(P // 2 * (g // 2), P // 2 * (g // 2 + 1))
                        heads_g = slice(GROUPS * (g % 2), GROUPS * (g % 2 + 1))
                        mm(pe, bank[4 + g % 2][:].rearrange("p (h q) -> p h q", h=GROUPS),
                           qk[rows_g, r, L + t * P:L + (t + 1) * P], q_by_head[r][rows_g, heads_g, t * P:(t + 1) * P]
                           ).then_inc(a_score, 1)
                return part

            def att_state(i, r):
                b = 2 * i + r
                pe.wait_ge(a_k_tok, b + 1)
                pe.wait_ge(a_v, b + 1)
                mm(pe, bank[3][:, 2 * P:2 * P + HEADS * HV].rearrange("p (h e) -> p h e", e=HV), k_tok[:],
                   v_aug[:, r, 0, :, 0:HV]).then_inc(a_state_mm, 1)

            def att_values(i, r):
                b = 2 * i + r
                pe.wait_ge(a_masked, 4 * (b + 1))
                pe.wait_ge(a_cleared, 4 * (b + 1))
                pe.wait_ge(a_state, b + 1)
                wait(pe, a_y_rows, b)
                for g in range(GROUPS):
                    last = mm(pe, bank[7][:, g * P:(g + 1) * P],
                              state[:, r, g * GROUPS:(g + 1) * GROUPS, :].rearrange("p h e -> p (h e)"),
                              qk[:, r, P:2 * P], start=(g == 0), stop=False, skip_group_check=True)
                last.then_inc(a_carried, 1)
                for t in (1, 0):
                    for h in range(HEADS):
                        g, j = h // GROUPS, h % GROUPS
                        last = mm(pe, bank[6 + t][HC * j:HC * (j + 1), g * P:(g + 1) * P], v_aug[:, r, t, h, :],
                                  scores[r][:, t, h, :], start=(t == 0), stop=True, skip_group_check=True)
                last.then_inc(a_y_mm, 1)

            def att_y_back(t):
                def part(i, r):
                    b = 2 * i + r
                    pe.wait_ge(a_y_rows, b + 1)
                    wait(pe, a_y, 2 * b + t)
                    for g in range(GROUPS):
                        last = pe.transpose(bank[2][:, g * P:(g + 1) * P], y_rows[:, t, g, :], ident)
                    last.then_inc(a_y_back, 1)
                return part

            def att_turn_y(i, r):
                b = 2 * i + r
                pe.wait_ge(a_y, 2 * (b + 1))
                ahead = min(b + 3, B) if isinstance(b, int) else b + 3
                pe.wait_ge(a_state, ahead)
                for t in range(AT):
                    last = pe.transpose(bank[3][:, t * P:(t + 1) * P], att_y[:, t, :], ident)
                last.then_inc(a_y_turned, 1)

            def att_out(i, r):
                b = 2 * i + r
                pe.wait_ge(a_yt, b + 1)
                for t in range(AT):
                    last = mm(pe, bank[3][:, t * D:(t + 1) * D], att_yt[:, t * P:(t + 1) * P], w_proj_sb)
                last.then_inc(a_out, 1)

            pipelined(pe, [(2, att_scores(0)), (2, att_turn_keys), (3, att_turn), (0, att_y_back(0)), (2, att_state),
                           (3, att_project), (0, att_y_back(1)), (1, att_values), (0, att_turn_y),
                           (2, att_scores(1)), (0, att_out)], B, 2)
            pe.wait_ge(a_added, B)
            experts_pe(pe, moe[1])

        def copy(act, out_, in_):
            return act.activation(out_, in_, ACT.Copy)

        def experts_act(act, m):
            def keep(i, r):
                k = 2 * i + r
                act.wait_ge(m.ln.turned, k + 1)
                wait(act, m.logits, k - 1)
                copy(act, normed_t_of[r][:], bank[2 * r][:]).then_inc(m.kept, 1)
                copy(act, normed_all[:, bass.ds(k * PT, PT)], bank[2 * r][:]).then_inc(m.ln.copied, 1)

            pipelined(act, [(0, keep)], PAIRS, 2)
            act.wait_ge(const_made, 9)
            act.wait_ge(m.route, 2)
            act.activation(score[:], top[:], ACT.Sigmoid).then_inc(m.score, 1)
            act.activation(held[:, 6:7], held[:, 6:7], ACT.Silu)

            def shared_silu(i, r):
                k = 2 * i + r
                for b in range(IB):
                    act.wait_ge(m.up, IB * k + b + 1)
                    wait(act, m.act, IB * (k - 1) + b + 1)
                    act.activation(silu_sh[:, b, :], bank[4 + b][:], ACT.Silu).then_inc(m.silu, 1)

            pipelined(act, [(0, shared_silu)], PAIRS, 2)

            def row_copy(i, r):
                act.wait_ge(m.row_turned, RING * i + r + 1)
                wait(act, m.row_up, RING * i + r - RING + 1)
                copy(act, row_in_t[:, r, :], bank[r % 2][:, 0:P]).then_inc(m.row_copied, 1)

            def row_silu_(i, r):
                act.wait_ge(m.row_up, RING * i + r + 1)
                wait(act, m.row_act, RING * i + r - RING + 1)
                act.activation(row_silu[:, r, :], bank[2 + r][:, 0:I], ACT.Silu).then_inc(m.row_silu, 1)

            def row_result(i, r):
                act.wait_ge(m.row_down, RING * i + r + 1)
                wait(act, m.row_stored[r], 16 * i)
                copy(act, row_out[:, r, :], bank[6 + r % 2][:, 0:D]).then_inc(m.row_out, 1)

            pipelined(act, [(3, row_copy), (2, row_silu_), (0, row_result)])

        @block.scalar
        def _(act):
            for dst, src in filter_loads[2:]:
                act.dma_start(dst, src).then_inc(filter_loaded, 16)
            act.dma_start(tables_sb[:, P:table_parts[1]], tables[:, P:table_parts[1]]).then_inc(tables_loaded[0], 16)
            act.dma_start(weights_sb[:], weights).then_inc(weights_loaded, 16)
            act.dma_start(b_out_all[:], b_out.rearrange("(a d) -> a d", a=1).to_broadcast([P, D])
                          ).then_inc(weights_loaded, 16)
            a, b = table_parts[2:4]
            act.dma_start(tables_sb[:, a:b], tables[:, a:b]).then_inc(tables_loaded[2], 16)
            def filter_sines():
                for n in range(3):
                    for h in range(2):
                        act.wait_ge(flt, FLT_LAYER * (n + 1) - 1 + h)
                        act.activation(filter_h[:, h * HALF:(h + 1) * HALF], filter_r[:, h * HALF:(h + 1) * HALF],
                                       ACT.Sin).then_inc(flt_act, 1)
                act.wait_ge(edges_made, 4)

            def copy_normed(k):
                act.wait_ge(ln_c.turned, k + 1)
                wait(act, c_proj, k)
                copy(act, normed_t[:], bank[0][:]).then_inc(ln_c.copied, 1)

            def conv_apply(k):
                act.wait_ge(c_shift, 2 * k + 2)
                wait(act, ln_c.turned, k)
                for j in range(PAIR):
                    act.activation(normed[:, j, :], residual[:, bass.ds(k * PAIR + j, 1), :].rearrange("p a d -> p (a d)"),
                                   ACT.Identity, bias=step_shift[:, j:j + 1], scale=step_rstd[:, j:j + 1]
                                   ).then_inc(ln_c.normed, 1)

            def copy_value(k):
                act.wait_ge(c_value_turned, k + 1)
                wait(act, c_forward, 2 * k)
                copy(act, value_t[:].rearrange("p j d -> p (j d)"), bank[0][:]).then_inc(c_value_copied, 1)

            def tap2(k):
                act.wait_ge(c_proj, k + 1)
                for g in range(3):
                    if g:
                        wait(act, c_value, k)
                        dst = conv_xv[:, g - 1, :]
                    else:
                        dst = gates[:, bass.ds(k * PT, PT)]
                    act.activation(dst, bank[1 + g][:], ACT.Identity, bias=conv_bias[:, g:g + 1],
                                   scale=taps[:, g, 2:3]).then_inc(c_tap2, 1)

            pipelined(act, [(1, each(copy_value)), (2, each(tap2)), (3, each(conv_apply)), (3, each(copy_normed))], PAIRS, 1,
                      {-2: filter_sines})
            experts_act(act, moe[0])

            def att_normed(i, r):
                b = 2 * i + r
                act.wait_ge(ln_a.turned, b + 1)
                wait(act, a_vproj, b)
                copy(act, normed_t[:, 0:L], bank[0][:, 0:L]).then_inc(ln_a.copied, 1)

            def att_features(i, r):
                b = 2 * i + r
                act.wait_ge(a_proj, b + 1)
                wait(act, a_qk, b)
                act.activation(att_exp, bank[1][:], ACT.Exp)
                act.activation(att_relu, bank[1][:], ACT.Relu).then_inc(a_relu, 1)

            def att_v(i, r):
                b = 2 * i + r
                act.wait_ge(a_vproj, b + 1)
                wait(act, a_y_mm, b - 1)
                for t in range(AT):
                    last = copy(act, v_aug[:, r, t, :, 0:HD], bank[0][:, t * D:(t + 1) * D].rearrange(
                        "p (h e) -> p h e", h=HEADS))
                last.then_inc(a_v, 1)

            def att_by_head(i, r):
                b = 2 * i + r
                act.wait_ge(a_qk, b + 1)
                wait(act, a_score, AT * GROUPS * (b - 1))
                for h in range(HEADS // 4):
                    last = act.activation(q_by_head[r][:, h, :], qk[:, r, 0:L], ACT.Copy,
                                          scale=head_of_half[:, h:h + 1])
                last.then_inc(a_by_head, 1)

            def att_k(i, r):
                b = 2 * i + r
                act.wait_ge(a_k_turned, b + 1)
                wait(act, a_state_mm, b)
                copy(act, k_tok[:], bank[3][:, 0:P]).then_inc(a_k_tok, 1)

            def att_scores_copy(t):
                def part(i, r):
                    b = 2 * i + r
                    for n in range(2):
                        g = 2 * n + 1
                        act.wait_ge(a_score, AT * GROUPS * b + t * GROUPS + g + 1)
                        wait(act, a_y_mm, b - 1)
                        copy(act, scores[r][:, t, g * GROUPS:(g + 1) * GROUPS, :].rearrange("p h q -> p (h q)"),
                             bank[5][:]).then_inc(a_copied, 1)
                return part

            def att_y_copy(i, r):
                b = 2 * i + r
                act.wait_ge(a_y_mm, b + 1)
                wait(act, a_y_back, AT * b)
                for t in range(AT):
                    last = copy(act, y_rows[:, t, :, :].rearrange("p g q -> p (g q)"), bank[6 + t][:])
                last.then_inc(a_y_rows, 1)

            def att_yt_copy(i, r):
                b = 2 * i + r
                act.wait_ge(a_y_turned, b + 1)
                wait(act, a_out, b)
                copy(act, att_yt, bank[3][:, 0:L]).then_inc(a_yt, 1)

            pipelined(act, [(2, att_scores_copy(0)), (2, att_k), (3, att_normed), (3, att_features), (3, att_by_head),
                            (1, att_y_copy), (0, att_yt_copy), (2, att_scores_copy(1)), (3, att_v)], B, 2)
            experts_act(act, moe[1])

        def experts_dve(dve, m):
            dve.wait_ge(m.ln.rstd, 2)

            def apply_kept(i, r):
                k = 2 * i + r
                wait(dve, m.ln.turned, k - 1)
                for j in range(PAIR):
                    t = bass.ds(k * PAIR + j, 1)
                    dve.tensor_scalar(normed_of[r][:, j, :], residual[:, t, :], mean_var[:, t, 0], rstd[:, t],
                                      ALU.subtract, ALU.mult).then_inc(m.ln.normed, 1)

            pipelined(dve, [(0, apply_kept)], PAIRS, 2)

            def bc(ap, axis, n):
                v = ap.unsqueeze(axis)
                shape = list(v.shape)
                shape[axis] = n
                return v.to_broadcast(shape)

            step = [0]

            def then(ins):
                step[0] += 1
                ins.then_inc(m.route, 1)
                dve.wait_ge(m.route, step[0])

            dve.wait_ge(m.logits, PAIRS)
            then(dve.tensor_copy(logits[:].rearrange("p t e -> p (t e)"), bank[1][:, 0:TILES * E]))
            then(dve.tensor_reduce(top[:], logits[:], AX.X, ALU.max))
            then(dve.tensor_tensor(r_a[:], logits[:], bc(top[:], 2, E), ALU.is_equal))
            then(dve.tensor_tensor(r_b[:], r_a[:], bc(tie_rank, 1, TILES), ALU.mult))
            then(dve.tensor_reduce(best[:], r_b[:], AX.X, ALU.max))
            then(dve.tensor_tensor(chosen[:], r_b[:], bc(best[:], 2, E), ALU.is_equal))
            then(dve.tensor_copy(chosen_b[:], chosen[:]))
            return then, bc

        place_steps = sem("place_steps")
        placed_n = [0]

        def route_rest(dve, m, bc):
            def placed(ins):
                placed_n[0] += 1
                ins.then_inc(place_steps, 1)
                dve.wait_ge(place_steps, placed_n[0])

            dve.wait_ge(m.counted, 1)
            placed(dve.tensor_copy(counts[:], bank[3][:, 0:TILES * E].rearrange("p (t e) -> p e t", e=E)))
            placed(dve.tensor_tensor_scan(running[:].rearrange("p e t -> p (e t)"), counts[:].rearrange("p e t -> p (e t)"),
                                      zeros, 0.0, ALU.add, ALU.add))
            placed(dve.memset(ends[:], 0.0))
            placed(dve.tensor_copy(ends[:, 1:E + 1], running[:, :, TILES - 1]))
            placed(dve.tensor_tensor(n_tok[:], ends[:, 1:E + 1], ends[:, 0:E], ALU.subtract))
            placed(dve.tensor_tensor(cmp_tiles[:], bc(n_tok[:], 2, TILES), bc(tile_starts, 1, E), ALU.is_gt))
            placed(dve.tensor_reduce(n_tiles[:], cmp_tiles[:], AX.X, ALU.add))
            placed(dve.tensor_tensor_scan(tile_ends[:], n_tiles[:], zeros[:, 0:E], 0.0, ALU.add, ALU.add))
            placed(dve.tensor_tensor(start_at[:], tile_ends[:], n_tiles[:], ALU.subtract))
            placed(dve.scalar_tensor_tensor(start_at[:], start_at[:], float(P), ends[:, 0:E], ALU.mult, ALU.subtract))
            placed(dve.tensor_tensor(running[:], running[:], counts[:], ALU.subtract))
            placed(dve.tensor_tensor(running[:], running[:], bc(start_at[:], 2, TILES), ALU.add))
            placed(dve.tensor_tensor(r_b[:], bank[2][:, 0:TILES * E].rearrange("p (t e) -> p t e", e=E),
                                 running[:].rearrange("p e t -> p t e"), ALU.add))
            placed(dve.tensor_tensor(r_b[:], r_b[:], chosen[:], ALU.mult))
            placed(dve.tensor_reduce(place_f[:], r_b[:], AX.X, ALU.add))
            placed(dve.tensor_copy(place[:], place_f[:]))
            dve.wait_ge(m.score, 1)
            placed(dve.tensor_tensor(best[:], rstd[:], score[:], ALU.mult))
            dve.wait_ge(blank_rows_stored, 16 * (1 + moe.index(m)))
            if m is moe[0]:
                placed(dve.tensor_copy(rows[:, :, D], table("token_numbers")))

        def experts_main(dve, m, then, bc):
            def tile_experts():
                then(dve.tensor_tensor(cmp_e[:], bc(tile_ends[:, 0:E - 1], 1, RT), bc(tile_numbers, 2, E - 1), ALU.is_le))
                then(dve.tensor_reduce(tile_expert_f[:], cmp_e[:], AX.X, ALU.add))
                then(dve.tensor_copy(tile_expert[:], tile_expert_f[:]))

            def gate_up(i, r):
                k = 2 * i + r
                for b in range(IB):
                    dve.wait_ge(m.silu, IB * k + b + 1)
                    wait(dve, m.down, k - 1)
                    dve.tensor_tensor(act_sh[:, r, b, :], silu_sh[:, b, :], bank[6 + b][:], ALU.mult
                                      ).then_inc(m.act, 1)

            def add_shared(i, r):
                k = 2 * i + r
                dve.wait_ge(m.down, k + 1)
                here = residual[:, bass.ds(k * PAIR, PAIR), :]
                dve.tensor_tensor(here, here, bank[1][:].rearrange("p (j d) -> p j d", j=PAIR), ALU.add
                                  ).then_inc(m.added, 1)

            def scale_rows(i, r):
                k = 2 * i + r
                for j in range(PAIR):
                    t = bass.ds(k * PAIR + j, 1)
                    dve.tensor_scalar(rows[:, t, 0:D], residual[:, t, :], mean_var[:, t, 0], best[:, t],
                                      ALU.subtract, ALU.mult).then_inc(m.rows, 1)

            def add_shared_after(i, r):
                dve.wait_ge(m.rows, PAIR * (2 * i + r + 1))
                add_shared(i, r)

            pipelined(dve, [(1, gate_up), (2, scale_rows), (0, add_shared_after)], PAIRS, 2, {0: tile_experts})

            def row_gate_up(i, r):
                dve.wait_ge(m.row_silu, RING * i + r + 1)
                wait(dve, m.row_down, RING * i + r - RING + 1)
                dve.tensor_tensor(row_act[:, r, :], row_silu[:, r, :], bank[2 + r][:, I:2 * I], ALU.mult
                                  ).then_inc(m.row_act, 1)

            def row_expert(i, r):
                e = dve.value_load(tile_expert[0:1, bass.ds(RING * i + r, 1)], min_val=0, max_val=E - 1)
                wait(dve, m.row_up, RING * i + r - 1)
                dve.tensor_scalar(row_weights[:, r % 2, :], experts[:, bass.ds(e * WE, 2 * I)], 1.0, None, ALU.mult
                                  ).then_inc(m.row_weights, 1)

            def row_number(i, r):
                dve.wait_ge(m.row_in[r], 16 * (i + 1))
                wait(dve, m.row_stored[r], 16 * i)
                dve.tensor_copy(row_token[:, r:r + 1], row_in[:, r, D:D + 1]).then_inc(m.row_token, 1)

            pipelined(dve, [(3, row_expert), (2, row_gate_up), (2, row_number)])

        def add_routed(dve, m, k, n):
            part = part_of(m, k * n // PAIR) if isinstance(k, int) else len(m.parts) - 1
            dve.wait_ge(m.back[part], 16 * m.parts[part])
            here, got = (a[:, bass.ds(k * n, n), 0:D] for a in (residual, rows))
            dve.tensor_tensor(here, here, got, ALU.add).then_inc(m.summed, 1)


        @block.vector
        def _(dve):
            fs = [0]

            def flt_step(ins):
                fs[0] += 1
                ins.then_inc(flt, 1)
                dve.wait_ge(flt, fs[0])

            def filter_layers():
                halves = [(filter_a[:, h * HALF:(h + 1) * HALF], filter_r[:, h * HALF:(h + 1) * HALF],
                           bank[4 + h][0:ORDER, 0:HALF]) for h in range(2)]
                for n in range(3):
                    steps = (
                        lambda a, r, product: dve.tensor_scalar(a, product, f_vec[:, 2 * n:2 * n + 1],
                                                                f_vec[:, 2 * n + 1:2 * n + 2], ALU.add, ALU.mult),
                        lambda a, r, product: dve.tensor_scalar(r, a, float(1 / (2 * np.pi)), ROUND,
                                                                ALU.mult, ALU.add),
                        lambda a, r, product: dve.tensor_scalar(r, r, ROUND, None, ALU.subtract),
                        lambda a, r, product: dve.scalar_tensor_tensor(a, r, -TWO_PI_HI, a, ALU.mult, ALU.add),
                        lambda a, r, product: dve.scalar_tensor_tensor(a, r, -float(TWO_PI_LO), a, ALU.mult, ALU.add),
                        lambda a, r, product: dve.tensor_scalar(r, a, PI_BELOW, -PI_BELOW, ALU.min, ALU.max))
                    for j, step in enumerate(steps):
                        for h, half in enumerate(halves):
                            if j == 0:
                                dve.wait_ge(flt_pe, 2 * n + h + 1)
                            if fs[0] >= 2:
                                dve.wait_ge(flt, fs[0] - 1)
                            step(*half).then_inc(flt, 1)
                            fs[0] += 1
                    assert fs[0] == FLT_LAYER * (n + 1)
                dve.wait_ge(flt, fs[0])
                dve.wait_ge(weights_loaded, 32)
                es = [0]

                def edge_step(ins):
                    es[0] += 1
                    ins.then_inc(edges_made, 1)
                    dve.wait_ge(edges_made, es[0])

                edge_step(dve.tensor_tensor(conv_edge[:, :, 0], taps[:, :, 0], taps[:, :, 1], ALU.add))
                edge_step(dve.tensor_tensor(conv_bias[:], conv_edge[:, :, 0], taps[:, :, 2], ALU.add))
                edge_step(dve.tensor_tensor(conv_bias[:], conv_bias[:], b_in_sb, ALU.mult))
                edge_step(dve.tensor_tensor(conv_bias[:], conv_bias[:], sf_b_sb, ALU.add))
                edge_step(dve.tensor_copy(conv_edge[:, :, 1], taps[:, :, 0]))
                edge_step(dve.tensor_tensor(edge_tmp[:], conv_edge[:], b_in_sb.unsqueeze(2).to_broadcast([P, 3, 2]),
                                            ALU.mult))
                edge_step(dve.tensor_scalar(conv_edge[:], edge_tmp[:], -1.0, None, ALU.mult))

            def filter_to_spectrum():
                dve.wait_ge(flt_pe, 7)
                dve.wait_ge(tables_loaded[0], 16)
                flt_step(dve.tensor_tensor(filter_k[:], bank[7][:].rearrange("p (t d) -> p t d", t=TAU), decay, ALU.mult))
                flt_step(dve.tensor_tensor(filter_k[0:1, 0, :], filter_k[0:1, 0, :], filt_bias_row[:], ALU.add))
                assert fs[0] == FLT_K
                dve.wait_ge(flt_pe, 8)
                half = FB * D
                for part, src in ((0, 0), (1, 1), (2, 0)):
                    flt_step(dve.tensor_copy(spectrum[:, part, :, :].rearrange("p f d -> p (f d)"),
                                             bank[6][:, src * half:(src + 1) * half]))
                flt_step(dve.tensor_copy(spectrum[0:1, 2, 0, :], bank[6][0:1, half:half + D]))
                flt_step(dve.memset(spectrum[0:1, 1, 0, :], 0.0))
                assert fs[0] == FLT_SPECTRUM

            def short_conv(k):
                def seqs(ap):
                    return ap.rearrange("p (b t) -> p b t", b=2)

                for g in range(3):
                    dve.wait_ge(c_tap2, 3 * k + g + 1)
                    dst = seqs(conv_xv[:, g - 1, :] if g else gates[:, bass.ds(k * PT, PT)])
                    src = seqs(bank[1 + g][:])
                    dve.tensor_tensor(dst[:, :, 0:2], dst[:, :, 0:2],
                                      conv_edge[:, g, :].unsqueeze(1).to_broadcast([P, 2, 2]), ALU.add
                                      ).then_inc(c_edge, 1)
                    dve.wait_ge(c_edge, 3 * k + g + 1)
                    dve.scalar_tensor_tensor(dst[:, :, 1:L], src[:, :, 0:L - 1], taps[:, g, 1:2], dst[:, :, 1:L],
                                             ALU.mult, ALU.add).then_inc(c_tap1, 1)
                    dve.wait_ge(c_tap1, 3 * k + g + 1)
                    dve.scalar_tensor_tensor(dst[:, :, 2:L], src[:, :, 0:L - 2], taps[:, g, 0:1], dst[:, :, 2:L],
                                             ALU.mult, ALU.add).then_inc(c_conv, 1)

            def products(k):
                wait(dve, c_spect, 2 * k)
                for n, (c, part) in enumerate(((0, 0), (1, 1), (1, 2), (0, 1))):
                    dve.wait_ge(c_forward, 2 * k + c + 1)
                    dve.tensor_tensor(
                        prod[:, n, :].rearrange("p (f b d) -> p f b d", f=FB, b=2),
                        bank[4 + c][:].rearrange("p (f b d) -> p f b d", f=FB, b=2),
                        spectrum[:, part, :, :].unsqueeze(2).to_broadcast([P, FB, 2, D]), ALU.mult).then_inc(c_prod, 1)

            def gate(k):
                dve.wait_ge(c_inverse, k + 1)
                wait(dve, c_out, k)
                dve.tensor_tensor(gated[:], bank[6][:], gates[:, bass.ds(k * PT, PT)], ALU.mult).then_inc(c_gated, 1)

            def add_conv(k):
                dve.wait_ge(c_out, k + 1)
                dve.wait_ge(c_bias, k + 1)
                here = residual[:, bass.ds(k * PAIR, PAIR), :]
                dve.tensor_tensor(here, here, bank[7][:].rearrange("p (j d) -> p j d", j=PAIR), ALU.add
                                  ).then_inc(c_added, 1)

            def conv_stats(k):
                keep_stats(dve, moe[0].ln, PAIR, k, c_added)

            def conv_stats_in(k):
                if isinstance(k, int):
                    dve.wait_ge(x_loaded[min(k, 2)], 16)
                norm_stats(dve, ln_c, k)

            pipelined(dve, [(3, each(conv_stats_in)), (2, each(short_conv)), (0, each(gate)),
                            (1, each(products)), (0, each(add_conv)), (0, each(conv_stats))], PAIRS, 1,
                      {-2: filter_layers, -1: filter_to_spectrum})
            dve.wait_ge(c_added, PAIRS)
            dve.wait_ge(tables_loaded[2], 16)
            dve.wait_ge(const_made, 9)

            def experts_vector(m):
                then, bc = experts_dve(dve, m)
                route_rest(dve, m, bc)
                experts_main(dve, m, then, bc)
                dve.wait_ge(m.added, PAIRS)

            experts_vector(moe[0])

            def att_in(i, r):
                b = 2 * i + r
                add_routed(dve, moe[0], b, AT)
                norm_stats(dve, ln_a, b, moe[0].summed)

            def att_feature_sum(i, r):
                b = 2 * i + r
                dve.wait_ge(a_relu, b + 1)
                wait(dve, a_carried, b - 1)
                dve.scalar_tensor_tensor(qk[:, r, :], att_exp, 1.0, att_relu, ALU.min, ALU.add).then_inc(a_qk, 1)

            def att_by_head(i, r):
                b = 2 * i + r
                dve.wait_ge(a_qk, b + 1)
                wait(dve, a_score, AT * GROUPS * (b - 1))
                for h in range(HEADS // 4, HEADS // 2):
                    last = dve.tensor_scalar(q_by_head[r][:, h, :], qk[:, r, 0:L], head_of_half[:, h:h + 1], None,
                                             ALU.mult)
                last.then_inc(a_by_head_v, 1)

            def att_mask(t):
                def part(i, r):
                    b = 2 * i + r
                    for n in range(2):
                        g = 2 * n
                        dve.wait_ge(a_score, AT * GROUPS * b + t * GROUPS + g + 1)
                        wait(dve, a_y_mm, b - 1)
                        dve.tensor_tensor(scores[r][:, t, g * GROUPS:(g + 1) * GROUPS, :],
                                          bank[4][:].rearrange("p (h q) -> p h q", h=GROUPS),
                                          causal.unsqueeze(1).to_broadcast([P, GROUPS, P]), ALU.mult
                                          ).then_inc(a_masked, 1)
                return part

            def att_state(i, r):
                b = 2 * i + r
                dve.wait_ge(a_state_mm, b + 1)
                wait(dve, a_carried, b - 1)
                dve.tensor_tensor(state[:, r, :, 0:HV],
                                  bank[3][:, 2 * P:2 * P + HEADS * HV].rearrange("p (h e) -> p h e", e=HV),
                                  own_head.rearrange("p (h e) -> p h e", e=HV), ALU.mult).then_inc(a_state, 1)

            def att_divide(t):
                def part(i, r):
                    b = 2 * i + r
                    dve.wait_ge(a_y_back, 2 * b + t + 1)
                    y = bank[2][:].rearrange("p (h e) -> p h e", e=HC)
                    here = den[:, t * HEADS:(t + 1) * HEADS]
                    wait(dve, a_y, 2 * b + t - 1)
                    dve.tensor_scalar(here, y[:, :, HD], ATT_EPS, None, ALU.add).then_inc(a_den, 1)
                    dve.wait_ge(a_den, 4 * b + 2 * t + 1)
                    dve.reciprocal(here, here).then_inc(a_den, 1)
                    dve.wait_ge(a_den, 4 * b + 2 * t + 2)
                    wait(dve, a_y_turned, b)
                    dve.tensor_tensor(att_y[:, t, :].rearrange("p (h e) -> p h e", e=HD), y[:, :, 0:HD],
                                      here.unsqueeze(2).to_broadcast([P, HEADS, HD]), ALU.mult).then_inc(a_y, 1)
                return part

            def att_add(i, r):
                b = 2 * i + r
                dve.wait_ge(a_out, b + 1)
                here = residual[:, bass.ds(b * AT, AT), :]
                dve.tensor_tensor(here, here, bank[3][:, 0:AT * D].rearrange("p (t d) -> p t d", t=AT), ALU.add
                                  ).then_inc(a_added, 1)

            def att_stats(i, r):
                keep_stats(dve, moe[1].ln, AT, 2 * i + r, a_added)

            pipelined(dve, [(3, att_mask(0)), (1, att_divide(0)), (5, att_in), (3, att_state), (1, att_divide(1)),
                            (5, lambda i, r: norm_apply(dve, ln_a, 2 * i + r)), (4, att_feature_sum),
                            (4, att_by_head), (0, att_stats), (3, att_mask(1)), (1, att_add)], B, 2)
            dve.wait_ge(a_added, B)
            experts_vector(moe[1])
            for k in range(PAIRS):
                add_routed(dve, moe[1], k, PAIR)


FLT_LAYER = 12
FLT_K = 3 * FLT_LAYER + 2
FLT_SPECTRUM = FLT_K + 5


def kernel(L0_attn_a_u, L0_attn_a_w_in, L0_attn_a_b_in, L0_attn_a_sf_w, L0_attn_a_sf_b, L0_attn_a_f_w1,
           L0_attn_a_f_b1, L0_attn_a_freq1, L0_attn_a_f_w2, L0_attn_a_f_b2, L0_attn_a_freq2, L0_attn_a_f_w3,
           L0_attn_a_f_b3, L0_attn_a_freq3, L0_attn_a_f_wout, L0_attn_a_filt_bias, L0_attn_a_w_out,
           L0_attn_a_b_out, L0_attn_b_w_attn, L0_attn_b_w_proj, L0_ffn_gate_w, L0_ffn_sh_gate, L0_ffn_sh_up,
           L0_ffn_sh_down, L0_ffn_rt_gate, L0_ffn_rt_up, L0_ffn_rt_down):
    import concourse.bacc as bacc
    from concourse.bass_utils import run_bass_kernel_spmd

    def thirds(a):
        return np.asarray(a).reshape(3, P, -1).transpose(1, 0, 2).reshape(P, -1)

    by_name = {
        "w_in": L0_attn_a_w_in, "taps": thirds(L0_attn_a_sf_w), "b_in": thirds(L0_attn_a_b_in),
        "sf_b": thirds(L0_attn_a_sf_b), "w_out": L0_attn_a_w_out, "gate_w": L0_ffn_gate_w,
        "sh_gate": L0_ffn_sh_gate, "sh_up": L0_ffn_sh_up,
        "sh_down": np.asarray(L0_ffn_sh_down).reshape(IB, P, D).transpose(1, 0, 2).reshape(P, IB * D),
        "w_attn": L0_attn_b_w_attn, "w_proj": L0_attn_b_w_proj}
    vectors = np.stack([np.asarray(v) for v in (L0_attn_a_f_b1, L0_attn_a_freq1, L0_attn_a_f_b2,
                                                L0_attn_a_freq2, L0_attn_a_f_b3, L0_attn_a_freq3)], 1)
    tables, positions, blank_rows = shape_constants()
    arrays = {
        "x": L0_attn_a_u,
        "weights": np.concatenate([np.asarray(by_name[name]) for name in WEIGHTS], 1),
        "filter_weights": np.concatenate([np.asarray(L0_attn_a_f_w2), np.asarray(L0_attn_a_f_w3),
                                          np.asarray(L0_attn_a_f_wout), vectors], 1),
        "f_w1": L0_attn_a_f_w1, "filt_bias": L0_attn_a_filt_bias, "b_out": L0_attn_a_b_out,
        "rt_gate": L0_ffn_rt_gate, "rt_up": L0_ffn_rt_up, "rt_down": L0_ffn_rt_down,
        "tables": tables, "positions": positions, "blank_rows": blank_rows}
    arrays = {name: np.ascontiguousarray(a) for name, a in arrays.items()}

    nc = bacc.Bacc("TRN2", target_bir_lowering=False, num_devices=1)
    args = [nc.dram_tensor(name, a.shape, mybir.dt.from_np(a.dtype), kind="ExternalInput").ap()
            for name, a in arrays.items()]
    out = nc.dram_tensor("out", (B, L, D), F32, kind="ExternalOutput").ap()
    hybrid_block(nc, *args, out)
    return run_bass_kernel_spmd(nc, [arrays], core_ids=[0]).results[0]["out"]
```
